# Optimizing a Trainium2 kernel written in Bass

```python
import numpy as np
import jax
import jax.numpy as jnp

def _softmax(x, axis=-1):
    return jax.nn.softmax(x, axis=axis)

def _gelu(x):
    return jax.nn.gelu(x, approximate=True)

def _silu(x):
    return jax.nn.silu(x)

def _sigmoid(x):
    return jax.nn.sigmoid(x)

def _layernorm(x, axis=-1, eps=1e-05):
    m = jnp.mean(x, axis=axis, keepdims=True)
    v = jnp.var(x, axis=axis, keepdims=True)
    return (x - m) / jnp.sqrt(v + eps)

def _scatter_add(tgt, idx, src, axis=0):
    return tgt.at[idx].add(src)

def _segment_sum(src, seg, n):
    return jax.ops.segment_sum(src, seg, n)
kernel_name = 'mk_recurrent_d2_jaxref_r8_d5fcc0'

def setup_inputs(seed: int=0):
    np.random.seed(seed)
    _w = jnp.asarray

    def _L0_attn_setup():
        import jax, jax.numpy as jnp
        import numpy as np
        B, L, D, N, K = (2, 256, 128, 16, 4)
        LN_EPS = 1e-05

        def _mamba_block(x, W_in, W_conv, b_conv, W_xproj, W_dt, b_dt, A_log, ln_gamma, ln_beta, W_out, b_out):
            d = x.shape[-1]
            n = A_log.shape[-1]
            k = W_conv.shape[-1]
            x_res = x
            xz = x @ W_in.T
            x_in, z = (xz[..., :d], xz[..., d:])
            xc = jax.lax.conv_general_dilated(x_in.transpose(0, 2, 1), W_conv, window_strides=(1,), padding=[(k - 1, 0)], feature_group_count=d, dimension_numbers=('NCH', 'OIH', 'NCH')) + b_conv[None, :, None]
            x_conv = xc.transpose(0, 2, 1)
            gate = jax.nn.silu(x_conv) * z
            A = -jnp.exp(A_log)
            delta = jax.nn.softplus(gate @ W_dt.T + b_dt)
            BC = gate @ W_xproj.T
            B_p, C_p = (BC[..., :n], BC[..., n:])
            delta_A = jnp.exp(jnp.einsum('bld,dn->bldn', delta, A))
            delta_B_x = jnp.einsum('bld,bln,bld->bldn', delta, B_p, gate)

            def step(h, inp):
                a, bx = inp
                h = a * h + bx
                return (h, h)
            h0 = jnp.zeros((x.shape[0], d, n), x.dtype)
            _, hs = jax.lax.scan(step, h0, (delta_A.transpose(1, 0, 2, 3), delta_B_x.transpose(1, 0, 2, 3)))
            y = jnp.einsum('lbdn,bln->bld', hs, C_p)
            y = y + x_res
            mu = y.mean(-1, keepdims=True)
            var = ((y - mu) ** 2).mean(-1, keepdims=True)
            y = (y - mu) / jnp.sqrt(var + LN_EPS) * ln_gamma + ln_beta
            return y @ W_out.T + b_out
        key = jax.random.key(seed)
        ks = jax.random.split(key, 8)

        def w(k, shape, sc=0.02):
            return jax.random.normal(k, shape, dtype=jnp.float32) * sc
        x = jax.random.normal(ks[0], (B, L, D), dtype=jnp.float32)
        W_in = w(ks[1], (2 * D, D))
        W_conv = w(ks[2], (D, 1, K))
        b_conv = jnp.zeros((D,), jnp.float32)
        W_xproj = w(ks[3], (2 * N, D))
        W_dt = w(ks[4], (D, D))
        b_dt = jnp.zeros((D,), jnp.float32)
        A_log = jnp.log(jnp.tile(jnp.arange(1, N + 1, dtype=jnp.float32), (D, 1)))
        ln_gamma = jnp.ones((D,), jnp.float32)
        ln_beta = jnp.zeros((D,), jnp.float32)
        W_out = w(ks[5], (D, D))
        b_out = jnp.zeros((D,), jnp.float32)
        return dict(x=x, W_in=W_in, W_conv=W_conv, b_conv=b_conv, W_xproj=W_xproj, W_dt=W_dt, b_dt=b_dt, A_log=A_log, ln_gamma=ln_gamma, ln_beta=ln_beta, W_out=W_out, b_out=b_out)
    _L0_attn_in = _L0_attn_setup()

    def _L0_ffn_setup():
        import jax, jax.numpy as jnp
        import numpy as np
        B, S, D, F, E = (4, 256, 128, 512, 8)
        LN_EPS = 1e-05
        key = jax.random.key(seed)
        ks = jax.random.split(key, 6)
        sc = 0.02
        return {'x': jax.random.normal(ks[0], (B, S, D), dtype=jnp.float32), 'Wr': jax.random.normal(ks[1], (D, E), dtype=jnp.float32) * sc, 'br': jnp.zeros((E,), jnp.float32), 'ln_g': jnp.ones((D,), jnp.float32), 'ln_b': jnp.zeros((D,), jnp.float32), 'W1': jax.random.normal(ks[2], (E, D, F), dtype=jnp.float32) * sc, 'b1': jnp.zeros((E, F), jnp.float32), 'W2': jax.random.normal(ks[3], (E, F, D), dtype=jnp.float32) * sc, 'b2': jnp.zeros((E, D), jnp.float32)}
    _L0_ffn_in = _L0_ffn_setup()

    def _L1_attn_setup():
        import jax, jax.numpy as jnp
        import numpy as np
        from jax import lax
        D_MODEL = 128
        N_HEADS = 4
        D_STATE = 64
        D_CONV = 4
        EXPAND = 2
        D_INNER = EXPAND * D_MODEL
        DT_RANK = 64
        H_DIN = D_INNER // N_HEADS
        H_DT = DT_RANK // N_HEADS
        H_DS = D_STATE // N_HEADS
        BATCH, SEQ = (2, 128)
        key = jax.random.key(seed)
        ks = jax.random.split(key, 8)
        hidden_states = jax.random.normal(ks[0], (BATCH, SEQ, D_MODEL), dtype=jnp.float32)
        s_in = 1.0 / np.sqrt(D_MODEL)
        in_proj_w = jax.random.uniform(ks[1], (2 * D_INNER, D_MODEL), minval=-s_in, maxval=s_in)
        s_c = 1.0 / np.sqrt(D_CONV)
        conv_w = jax.random.uniform(ks[2], (D_INNER, 1, D_CONV), minval=-s_c, maxval=s_c)
        conv_b = jax.random.uniform(ks[3], (D_INNER,), minval=-s_c, maxval=s_c)
        s_x = 1.0 / np.sqrt(H_DIN)
        x_proj_w = jax.random.uniform(ks[4], ((2 * H_DS + H_DT) * N_HEADS, H_DIN), minval=-s_x, maxval=s_x)
        s_dt = H_DT ** (-0.5)
        dt_proj_w = jax.random.uniform(ks[5], (D_INNER, H_DT), minval=-s_dt, maxval=s_dt)
        dt = jnp.exp(jax.random.uniform(ks[6], (D_INNER,)) * (np.log(0.1) - np.log(0.001)) + np.log(0.001))
        dt = jnp.clip(dt, 0.0001, None)
        dt_proj_b = dt + jnp.log(-jnp.expm1(-dt))
        A_log = jnp.log(jnp.tile(jnp.arange(1, H_DS + 1, dtype=jnp.float32), (D_INNER, 1)))
        Dskip = jnp.ones((D_INNER,), dtype=jnp.float32)
        out_proj_w = jax.random.uniform(ks[7], (D_MODEL, D_INNER), minval=-s_x, maxval=s_x)
        return {'hidden_states': hidden_states, 'in_proj_w': in_proj_w, 'conv_w': conv_w, 'conv_b': conv_b, 'x_proj_w': x_proj_w, 'dt_proj_w': dt_proj_w, 'dt_proj_b': dt_proj_b, 'A_log': A_log, 'Dskip': Dskip, 'out_proj_w': out_proj_w}
    _L1_attn_in = _L1_attn_setup()

    def _L1_ffn_setup():
        import jax, jax.numpy as jnp
        import numpy as np
        B, S, H = (2, 128, 128)
        E, F = (8, 512)
        GATE_TEMP = 0.1
        key = jax.random.key(seed)
        ks = jax.random.split(key, 6)
        s_h = 1.0 / np.sqrt(H)
        s_f = 1.0 / np.sqrt(F)
        return {'hidden_states': jax.random.normal(ks[0], (B, S, H), dtype=jnp.float32), 'w_router': jax.random.normal(ks[1], (H, E), dtype=jnp.float32) * s_h, 'w_gating': jax.random.normal(ks[2], (H, E), dtype=jnp.float32) * s_h, 'w_gate': jax.random.normal(ks[3], (E, H, F), dtype=jnp.float32) * s_h, 'w_up': jax.random.normal(ks[4], (E, H, F), dtype=jnp.float32) * s_h, 'w_down': jax.random.normal(ks[5], (E, F, H), dtype=jnp.float32) * s_f}
    _L1_ffn_in = _L1_ffn_setup()
    _d = {'L0_attn_x': _L0_attn_in['x'], 'L0_attn_W_in': _L0_attn_in['W_in'], 'L0_attn_W_conv': _L0_attn_in['W_conv'], 'L0_attn_b_conv': _L0_attn_in['b_conv'], 'L0_attn_W_xproj': _L0_attn_in['W_xproj'], 'L0_attn_W_dt': _L0_attn_in['W_dt'], 'L0_attn_b_dt': _L0_attn_in['b_dt'], 'L0_attn_A_log': _L0_attn_in['A_log'], 'L0_attn_ln_gamma': _L0_attn_in['ln_gamma'], 'L0_attn_ln_beta': _L0_attn_in['ln_beta'], 'L0_attn_W_out': _L0_attn_in['W_out'], 'L0_attn_b_out': _L0_attn_in['b_out'], 'L0_ffn_Wr': _L0_ffn_in['Wr'], 'L0_ffn_br': _L0_ffn_in['br'], 'L0_ffn_ln_g': _L0_ffn_in['ln_g'], 'L0_ffn_ln_b': _L0_ffn_in['ln_b'], 'L0_ffn_W1': _L0_ffn_in['W1'], 'L0_ffn_b1': _L0_ffn_in['b1'], 'L0_ffn_W2': _L0_ffn_in['W2'], 'L0_ffn_b2': _L0_ffn_in['b2'], 'L1_attn_in_proj_w': _L1_attn_in['in_proj_w'], 'L1_attn_conv_w': _L1_attn_in['conv_w'], 'L1_attn_conv_b': _L1_attn_in['conv_b'], 'L1_attn_x_proj_w': _L1_attn_in['x_proj_w'], 'L1_attn_dt_proj_w': _L1_attn_in['dt_proj_w'], 'L1_attn_dt_proj_b': _L1_attn_in['dt_proj_b'], 'L1_attn_A_log': _L1_attn_in['A_log'], 'L1_attn_Dskip': _L1_attn_in['Dskip'], 'L1_attn_out_proj_w': _L1_attn_in['out_proj_w'], 'L1_ffn_w_router': _L1_ffn_in['w_router'], 'L1_ffn_w_gating': _L1_ffn_in['w_gating'], 'L1_ffn_w_gate': _L1_ffn_in['w_gate'], 'L1_ffn_w_up': _L1_ffn_in['w_up'], 'L1_ffn_w_down': _L1_ffn_in['w_down']}
    _x0 = _d['L0_attn_x']
    _d['L0_attn_x'] = jax.random.normal(jax.random.fold_in(jax.random.key(seed), 1), (8, 256, 128), dtype=_x0.dtype)
    del _x0
    return _d

def reference(L0_attn_x, L0_attn_W_in, L0_attn_W_conv, L0_attn_b_conv, L0_attn_W_xproj, L0_attn_W_dt, L0_attn_b_dt, L0_attn_A_log, L0_attn_ln_gamma, L0_attn_ln_beta, L0_attn_W_out, L0_attn_b_out, L0_ffn_Wr, L0_ffn_br, L0_ffn_ln_g, L0_ffn_ln_b, L0_ffn_W1, L0_ffn_b1, L0_ffn_W2, L0_ffn_b2, L1_attn_in_proj_w, L1_attn_conv_w, L1_attn_conv_b, L1_attn_x_proj_w, L1_attn_dt_proj_w, L1_attn_dt_proj_b, L1_attn_A_log, L1_attn_Dskip, L1_attn_out_proj_w, L1_ffn_w_router, L1_ffn_w_gating, L1_ffn_w_gate, L1_ffn_w_up, L1_ffn_w_down):

    def _L0_attn_ref(x, W_in, W_conv, b_conv, W_xproj, W_dt, b_dt, A_log, ln_gamma, ln_beta, W_out, b_out):
        import jax, jax.numpy as jnp
        import numpy as np
        B, L, D, N, K = (2, 256, 128, 16, 4)
        LN_EPS = 1e-05

        def _mamba_block(x, W_in, W_conv, b_conv, W_xproj, W_dt, b_dt, A_log, ln_gamma, ln_beta, W_out, b_out):
            d = x.shape[-1]
            n = A_log.shape[-1]
            k = W_conv.shape[-1]
            x_res = x
            xz = x @ W_in.T
            x_in, z = (xz[..., :d], xz[..., d:])
            xc = jax.lax.conv_general_dilated(x_in.transpose(0, 2, 1), W_conv, window_strides=(1,), padding=[(k - 1, 0)], feature_group_count=d, dimension_numbers=('NCH', 'OIH', 'NCH')) + b_conv[None, :, None]
            x_conv = xc.transpose(0, 2, 1)
            gate = jax.nn.silu(x_conv) * z
            A = -jnp.exp(A_log)
            delta = jax.nn.softplus(gate @ W_dt.T + b_dt)
            BC = gate @ W_xproj.T
            B_p, C_p = (BC[..., :n], BC[..., n:])
            delta_A = jnp.exp(jnp.einsum('bld,dn->bldn', delta, A))
            delta_B_x = jnp.einsum('bld,bln,bld->bldn', delta, B_p, gate)

            def step(h, inp):
                a, bx = inp
                h = a * h + bx
                return (h, h)
            h0 = jnp.zeros((x.shape[0], d, n), x.dtype)
            _, hs = jax.lax.scan(step, h0, (delta_A.transpose(1, 0, 2, 3), delta_B_x.transpose(1, 0, 2, 3)))
            y = jnp.einsum('lbdn,bln->bld', hs, C_p)
            y = y + x_res
            mu = y.mean(-1, keepdims=True)
            var = ((y - mu) ** 2).mean(-1, keepdims=True)
            y = (y - mu) / jnp.sqrt(var + LN_EPS) * ln_gamma + ln_beta
            return y @ W_out.T + b_out
        return _mamba_block(x, W_in, W_conv, b_conv, W_xproj, W_dt, b_dt, A_log, ln_gamma, ln_beta, W_out, b_out)

    def _L0_ffn_ref(x, Wr, br, ln_g, ln_b, W1, b1, W2, b2):
        import jax, jax.numpy as jnp
        import numpy as np
        B, S, D, F, E = (4, 256, 128, 512, 8)
        LN_EPS = 1e-05
        tokens_shape = x.shape[:-1]
        xt = x.reshape(-1, x.shape[-1])
        router_logits = xt @ Wr + br
        router_probs = jax.nn.softmax(router_logits, axis=-1)
        gates = jnp.max(router_probs, axis=-1, keepdims=True)
        idx = jnp.argmax(router_probs, axis=-1)
        onehot = jax.nn.one_hot(idx, E, dtype=xt.dtype)
        mu = jnp.mean(xt, axis=-1, keepdims=True)
        var = jnp.mean(jnp.square(xt - mu), axis=-1, keepdims=True)
        xn = (xt - mu) * jax.lax.rsqrt(var + LN_EPS) * ln_g + ln_b
        h = jnp.einsum('te,td,edf->tf', onehot, xn, W1) + b1[idx]
        h = jax.nn.relu(h)
        y = jnp.einsum('te,tf,efd->td', onehot, h, W2) + b2[idx]
        y = y * gates
        return y.reshape(tokens_shape + (y.shape[-1],))

    def _L1_attn_ref(hidden_states, in_proj_w, conv_w, conv_b, x_proj_w, dt_proj_w, dt_proj_b, A_log, Dskip, out_proj_w):
        import jax, jax.numpy as jnp
        import numpy as np
        from jax import lax
        D_MODEL = 128
        N_HEADS = 4
        D_STATE = 64
        D_CONV = 4
        EXPAND = 2
        D_INNER = EXPAND * D_MODEL
        DT_RANK = 64
        H_DIN = D_INNER // N_HEADS
        H_DT = DT_RANK // N_HEADS
        H_DS = D_STATE // N_HEADS
        BATCH, SEQ = (2, 128)
        b, L, _ = hidden_states.shape
        xz = hidden_states @ in_proj_w.T
        x, z = jnp.split(xz, 2, axis=-1)
        xp = jnp.pad(x, ((0, 0), (D_CONV - 1, 0), (0, 0)))
        w = conv_w[:, 0, :]
        xc = conv_b
        for k in range(D_CONV):
            xc = xc + xp[:, k:k + L, :] * w[:, k]
        x = jax.nn.silu(xc)
        xh = x.reshape(b, L, N_HEADS, H_DIN)
        xw = x_proj_w.reshape(N_HEADS, 2 * H_DS + H_DT, H_DIN)
        x_dbl = jnp.einsum('hod,blhd->blho', xw, xh)
        dt_r, Bm, Cm = jnp.split(x_dbl, [H_DT, H_DT + H_DS], axis=-1)
        dtw = dt_proj_w.reshape(N_HEADS, H_DIN, H_DT)
        delta = jnp.einsum('hdr,blhr->blhd', dtw, dt_r)
        delta = jax.nn.softplus(delta + dt_proj_b.reshape(N_HEADS, H_DIN))
        A = -jnp.exp(A_log).reshape(N_HEADS, H_DIN, H_DS)

        def step(s, inp):
            d_t, u_t, B_t, C_t = inp
            dA = jnp.exp(d_t[..., None] * A)
            s = s * dA + (d_t * u_t)[..., None] * B_t[:, :, None, :]
            y_t = jnp.einsum('bhdn,bhn->bhd', s, C_t)
            return (s, y_t)
        s0 = jnp.zeros((b, N_HEADS, H_DIN, H_DS), dtype=x.dtype)
        scan_in = (delta.transpose(1, 0, 2, 3), xh.transpose(1, 0, 2, 3), Bm.transpose(1, 0, 2, 3), Cm.transpose(1, 0, 2, 3))
        _, ys = lax.scan(step, s0, scan_in)
        y = ys.transpose(1, 0, 2, 3).reshape(b, L, D_INNER)
        y = y + x * Dskip
        y = y * jax.nn.silu(z)
        out = y @ out_proj_w.T
        return out

    def _L1_ffn_ref(hidden_states, w_router, w_gating, w_gate, w_up, w_down):
        import jax, jax.numpy as jnp
        import numpy as np
        B, S, H = (2, 128, 128)
        E, F = (8, 512)
        GATE_TEMP = 0.1
        x = hidden_states
        router_probs = jax.nn.softmax(jnp.einsum('bsh,he->bse', x, w_router), axis=-1)
        gate_weights = jax.nn.softmax(jnp.einsum('bsh,he->bse', x, w_gating) / GATE_TEMP, axis=-1)
        g = jnp.einsum('bsh,ehf->ebsf', x, w_gate)
        u = jnp.einsum('bsh,ehf->ebsf', x, w_up)
        h = jax.nn.silu(g) * u
        expert_out = jnp.einsum('ebsf,efh->ebsh', h, w_down)
        cw = router_probs * gate_weights
        cw = cw / (jnp.sum(cw, axis=-1, keepdims=True) + 1e-09)
        out = jnp.einsum('ebsh,bse->bsh', expert_out, cw)
        return out
    x = L0_attn_x
    xn = _layernorm(x, axis=-1)
    s = _L0_attn_ref(xn, L0_attn_W_in, L0_attn_W_conv, L0_attn_b_conv, L0_attn_W_xproj, L0_attn_W_dt, L0_attn_b_dt, L0_attn_A_log, L0_attn_ln_gamma, L0_attn_ln_beta, L0_attn_W_out, L0_attn_b_out)
    g = _silu(_L0_ffn_ref(xn, L0_ffn_Wr, L0_ffn_br, L0_ffn_ln_g, L0_ffn_ln_b, L0_ffn_W1, L0_ffn_b1, L0_ffn_W2, L0_ffn_b2))
    x = x + s * g
    xn = _layernorm(x, axis=-1)
    s = _L1_attn_ref(xn, L1_attn_in_proj_w, L1_attn_conv_w, L1_attn_conv_b, L1_attn_x_proj_w, L1_attn_dt_proj_w, L1_attn_dt_proj_b, L1_attn_A_log, L1_attn_Dskip, L1_attn_out_proj_w)
    g = _silu(_L1_ffn_ref(xn, L1_ffn_w_router, L1_ffn_w_gating, L1_ffn_w_gate, L1_ffn_w_up, L1_ffn_w_down))
    x = x + s * g
    return x

_drawn_inputs = setup_inputs


def setup_inputs(seed=0):
    import zlib

    import numpy as np

    out = dict(_drawn_inputs(seed))
    spreads = {'L0_attn_b_conv': (0.0, 0.8),
     'L0_attn_b_dt': (0.0, 0.8),
     'L0_attn_ln_gamma': (1.0, 0.6),
     'L0_attn_ln_beta': (0.0, 0.8),
     'L0_attn_b_out': (0.0, 0.8),
     'L0_ffn_br': (0.0, 0.8),
     'L0_ffn_ln_g': (1.0, 0.6),
     'L0_ffn_ln_b': (0.0, 0.8),
     'L0_ffn_b1': (0.0, 0.8),
     'L0_ffn_b2': (0.0, 0.8),
     'L1_attn_Dskip': (1.0, 0.6)}
    factors = {'L0_attn_W_in': 8.0,
     'L0_attn_W_conv': 8.0,
     'L0_attn_W_xproj': 8.0,
     'L0_attn_W_dt': 8.0,
     'L0_attn_A_log': 8.0,
     'L0_attn_W_out': 8.0,
     'L0_ffn_Wr': 8.0,
     'L0_ffn_W1': 8.0,
     'L0_ffn_W2': 8.0,
     'L1_attn_conv_b': 3.311,
     'L1_attn_x_proj_w': 8.0,
     'L1_attn_dt_proj_w': 8.0,
     'L1_attn_dt_proj_b': 8.0,
     'L1_attn_A_log': 8.0,
     'L1_ffn_w_router': 8.0}
    for name, (base, spread) in spreads.items():
        noise = np.random.default_rng([zlib.crc32(name.encode()), seed]).standard_normal(out[name].shape)
        drawn = base * np.exp(spread * noise) if base else spread * noise
        out[name] = jnp.asarray(drawn.astype(out[name].dtype))
    for name, factor in factors.items():
        out[name] = (out[name] * factor).astype(out[name].dtype)
    return out
```

```python
import concourse.bass as bass
from concourse import mybir
from contextlib import ExitStack

F32 = mybir.dt.float32
BF16 = mybir.dt.bfloat16
ALU = mybir.AluOpType
ACT = mybir.ActivationFunctionType
AXX = mybir.AxisListType.X

B, L, D = 8, 256, 128
NB = 2
T = NB * L
PAIRS = B // NB
TT = T // 128
E, FT = 8, 4
UNITS = E * FT
N = 16
KC = 4
J1 = 2
PC = 4
RING = 4
LAG = 3
LAG1 = 3
GATE_TEMP = 0.1
EPS = 1e-5
BIG = 2.0 ** 100

V0 = dict(conv=0, bconv=4, bdt=5, alog=6, gam=22, bet=23, lng=24, lnb=25, b1=26)
V0_COLS = 26 + UNITS
V1 = dict(conv=0, bconv=8, bdt=10, alog=12, dskip=44)
V1_COLS = 46


class Signal:

    def __init__(self, sem, per, start):
        self.sem, self.per, self.start = sem, per, start

    def at(self, i, n):
        assert n or self.start, self.sem
        return i * self.per + n + self.start


def chunk_after(u, chunks):
    first = 2
    pace = 1.5
    for n in range(chunks):
        if int(first + pace * n) == u:
            return n
    return None


def scan_ring(nc, ctx, mark=""):
    sb = lambda name: ctx.enter_context(nc.sbuf_tensor(mark + name, [128, RING, T], F32))
    return sb("decay"), sb("drive"), sb("state"), sb("product")


def layer0(nc, x, x1, crow, w):
    ctx = ExitStack()
    with ctx:
        sb = lambda name, shape, dt=F32: ctx.enter_context(nc.sbuf_tensor(name, shape, dt))
        starts = ('c_out', 'down_done', 'drive_ready', 'g_ready', 'product_ready', 'state_ready', 'summed', 'x1_out', 'x1_ready', 'yT_ready', 'yfT_ready', 'c_in0', 'c_in1', 'c_in2', 'c_in3')
        started = {}

        def sig(name, per=1):
            s = Signal(ctx.enter_context(nc.semaphore(name)), per, int(name in starts))
            if s.start:
                started[name] = s
            return s

        bank = [ctx.enter_context(nc.psum_tensor(f"bank{k}", [128, 512], F32)) for k in range(8)]

        ident = sb("ident", [128, 128])
        sel = sb("sel", [96, N * 128], BF16)
        big = sb("big", [E, E * 128], BF16)
        vec = sb("vec", [128, V0_COLS])
        iota = sb("iota", [128, TT, E])
        brb = sb("brb", [128, E])
        bout = sb("bout", [128, D])
        w_in = sb("w_in", [128, 2 * D])
        w_dt = sb("w_dt", [128, D])
        w_b = sb("w_b", [128, 96])
        w_c = sb("w_c", [128, N])
        w_out = sb("w_out", [128, D])
        w_r = sb("w_r", [128, E])
        b2 = sb("b2", [E, D])
        w1 = sb("w1", [128, E, FT * 128])
        w2 = sb("w2", [128, UNITS, D])
        negA = sb("negA", [128, N])
        half = sb("half", [128, TT])
        idle = sb("idle", [128, 1])

        xt = sb("xt", [128, TT, D])
        xn = sb("xn", [128, TT, D])
        xf = sb("xf", [128, TT, D])
        XNT = sb("XNT", [128, T])
        XFT = sb("XFT", [128, T])
        stats = sb("stats", [128, TT, 6])
        mv = sb("mv", [128, TT, 2])
        veps = sb("veps", [128, TT])
        rstd = sb("rstd", [128, TT])
        xpad = sb("xpad", [128, NB, KC - 1 + L])
        conv = sb("conv", [128, T])
        xs = sb("xs", [128, T])
        gate = sb("gate", [128, T])
        sp_a = sb("sp_a", [128, T])
        sp_e = sb("sp_e", [128, T])
        sp_u = sb("sp_u", [128, T])
        sp_l = sb("sp_l", [128, T])
        sp_r = sb("sp_r", [128, T])
        sp_x = sb("sp_x", [128, T])
        delta = sb("delta", [128, T])
        dx = sb("dx", [128, T])
        Bst = sb("Bst", [96, T], BF16)
        Bres = sb("Bres", [96, T])
        Bmid = sb("Bmid", [96, T], BF16)
        Crows = sb("Crows", [N, T])
        Cb = sb("Cb", [128, RING, PC, T])
        decay, drive, state, product = scan_ring(nc, ctx)
        lg = sb("lg", [128, TT, E])
        lmax = sb("lmax", [128, TT])
        lexp = sb("lexp", [128, TT, E])
        lsum = sb("lsum", [128, TT])
        pmax = sb("pmax", [128, TT])
        eq = sb("eq", [128, TT, E])
        onehot = sb("onehot", [128, TT, E])
        ohT = sb("ohT", [E, T])
        ohm = sb("ohm", [E, T], BF16)
        hid = sb("hid", [128, 2, T])
        yfT = sb("yfT", [128, T])
        g = sb("g", [128, TT, D])
        yT = sb("yT", [128, T])
        yn = sb("yn", [128, TT, D])
        ynT = sb("ynT", [128, T])
        so = sb("so", [128, TT, D])

        DVE_STEPS, ACT_STEPS = 25, 2
        consts_in, experts_in = sig("consts_in"), sig("experts_in")
        x_in = sig("x_in", 16)
        x1_out = sig("x1_out", 16)
        c_out = sig("c_out", 16)
        c_in = [sig(f"c_in{k}", 16) for k in range(RING)]
        dve_step = sig("dve_step", DVE_STEPS)
        act_step = sig("act_step", ACT_STEPS)
        setup_dve, setup_act = sig("setup_dve"), sig("setup_act")
        var_ready, rstd_ready = sig("var_ready", 3), sig("rstd_ready", 3)
        xn_ready, xf_ready = sig("xn_ready"), sig("xf_ready")
        xnT_ps, xfT_ps, XNT_ready, XFT_ready = sig("xnT_ps"), sig("xfT_ps"), sig("XNT_ready"), sig("XFT_ready")
        xin_ps, z_ps, logit_ps = sig("xin_ps"), sig("z_ps"), sig("logit_ps")
        xpad_ready, conv_ready, xs_ready, gate_ready = sig("xpad_ready"), sig("conv_ready"), sig("xs_ready"), sig("gate_ready")
        lmax_sub, lexp_ready = sig("lmax_sub"), sig("lexp_ready")
        onehot_ready, ohT_ps, ohT_ready = sig("onehot_ready"), sig("ohT_ps"), sig("ohT_ready")
        dt_ps, b_ps, c_ps = sig("dt_ps"), sig("b_ps"), sig("c_ps")
        sp_e_ready, sp_u_ready, sp_r_ready, delta_ready = sig("sp_e_ready"), sig("sp_u_ready"), sig("sp_r_ready"), sig("delta_ready")
        crows_ready, bst_ready = sig("crows_ready"), sig("bst_ready")
        bc_ps, drive_ready, decay_ready = sig("bc_ps", N), sig("drive_ready", N), sig("decay_ready", N)
        state_ready, product_ready, summed = sig("state_ready", N), sig("product_ready", N), sig("summed", N)
        hid_ps, hid_ready, down_done = sig("hid_ps", UNITS), sig("hid_ready", UNITS), sig("down_done", UNITS)
        ffn_ps, yfT_ready, yf_ps, g_ready = sig("ffn_ps"), sig("yfT_ready"), sig("yf_ps"), sig("g_ready")
        yT_ready, y_ps, yn_ready, ynT_ps, ynT_ready = sig("yT_ready"), sig("y_ps"), sig("yn_ready"), sig("ynT_ps"), sig("ynT_ready")
        s_ps, x1_ready = sig("s_ps"), sig("x1_ready")

        SMALL = 12
        EXPERT_LOADS = 2 * E
        block = ctx.enter_context(nc.Block())

        def tiles(ap):
            return ap[:, :].rearrange("p (k d) -> p k d", k=TT)

        def by_batch(ap):
            return ap.rearrange("p (b l) -> p b l", b=NB)

        @block.sync
        def _(sp):
            for name in starts:
                sp.sem_inc(started[name].sem, 1)
            for name, dst in (("ident", ident), ("vec0", vec), ("w_in0", w_in), ("w_r0", w_r), ("br0", brb),
                              ("iota", iota), ("w_dt0", w_dt), ("w_b0", w_b), ("w_c0", w_c), ("sel0", sel),
                              ("big", big), ("w_out0", w_out)):
                src = w[name]
                if name == "br0":
                    src = src.to_broadcast((128, E))
                to = dst[:, :, :] if name == "iota" else dst[:, :]
                sp.dma_start(to, src).then_inc(consts_in.sem, 16)
            sp.dma_start(b2[:, :], w["b2"]).then_inc(experts_in.sem, 16)
            sp.dma_start(bout[:, :], w["b_out0"].to_broadcast((128, D))).then_inc(experts_in.sem, 16)
            for e in range(E):
                sp.dma_start(w1[:, e, :], w["W1"][e]).then_inc(experts_in.sem, 16)
                sp.dma_start(w2[:, FT * e:FT * e + FT, :],
                             w["W2"][e].rearrange("(f p) d -> p f d", p=128)).then_inc(experts_in.sem, 16)
            for i in range(PAIRS):
                sp.wait_ge(x1_ready.sem, x1_ready.at(i, 0))
                sp.dma_start(xt[:, :, :], x[i * T:i * T + T, :].rearrange("(k p) d -> p k d", p=128)).then_inc(x_in.sem, 16)
                sp.wait_ge(crows_ready.sem, crows_ready.at(i, 1))
                for k in range(RING):
                    sp.wait_ge(c_in[k].sem, c_in[k].at(i, 0))
                sp.dma_start(crow[:, :], Crows[:, :]).then_inc(c_out.sem, 16)
                sp.wait_ge(c_out.sem, c_out.at(i, 16))
                for k in range(RING):
                    sp.wait_ge(product_ready.sem, product_ready.at(i, 0))
                    src = crow[PC * k:PC * k + PC, :].rearrange("(a r) t -> a r t", a=1)
                    sp.dma_start(Cb[:, k, :, :], src.to_broadcast((128, PC, T))).then_inc(c_in[k].sem, 16)
                sp.wait_ge(x1_ready.sem, x1_ready.at(i, 1))
                sp.dma_start(x1[i * T:i * T + T, :].rearrange("(k p) d -> p k d", p=128), so[:, :, :]).then_inc(x1_out.sem, 16)
            sp.wait_ge(x1_out.sem, x1_out.at(PAIRS, 0))

        @block.vector
        def _(dve):
            v = nc.vector
            steps = [0]

            with ExitStack():
                v.memset(xpad[:, :, 0:KC - 1], 0.0).then_inc(setup_dve.sem, 1)
                v.memset(by_batch(decay[:, 0, :])[:, :, 0:1], 0.0).then_inc(setup_dve.sem, 1)
                for k in range(1, RING):
                    v.memset(by_batch(decay[:, k, :])[:, :, 0:1], 0.0).then_inc(setup_dve.sem, 1)
                v.memset(half[:, :], -0.5).then_inc(setup_dve.sem, 1)
                dve.wait_ge(setup_act.sem, 1)
                v.tensor_scalar(negA[:, :], negA[:, :], -1.0, None, ALU.mult).then_inc(setup_dve.sem, 1)
                dve.wait_ge(setup_dve.sem, 7)

            with dve.Fori(0, PAIRS) as i:
                def step(ins):
                    steps[0] += 1
                    ins.then_inc(dve_step.sem, 1)
                    dve.wait_ge(dve_step.sem, dve_step.at(i, steps[0]))

                def normalise(dst, src, n, ready):
                    for k in range(TT):
                        last = v.bn_stats(stats[:, k, :], src[:, k, :])
                    step(last)
                    v.memset(idle[:, :], 0.0)
                    for k in range(TT):
                        last = v.bn_aggr(mv[:, k, :], stats[:, k, :])
                    step(last)
                    v.tensor_scalar(veps[:, :], mv[:, :, 1], EPS, None, ALU.add).then_inc(var_ready.sem, 1)
                    dve.wait_ge(rstd_ready.sem, rstd_ready.at(i, n + 1))
                    for k in range(TT):
                        last = v.tensor_scalar(dst[:, k, :], src[:, k, :], mv[:, k, 0:1], rstd[:, k:k + 1],
                                               ALU.subtract, ALU.mult)
                    last.then_inc(ready.sem, 1)

                dve.wait_ge(x_in.sem, x_in.at(i, 16))
                normalise(xn, xt, 0, xn_ready)
                dve.wait_ge(xn_ready.sem, xn_ready.at(i, 1))
                normalise(xf, xn, 1, xf_ready)
                dve.wait_ge(xpad_ready.sem, xpad_ready.at(i, 1))
                cv = by_batch(conv[:, :])
                step(v.tensor_scalar(cv, xpad[:, :, 0:L], vec[:, V0["conv"]:V0["conv"] + 1],
                                     vec[:, V0["bconv"]:V0["bconv"] + 1], ALU.mult, ALU.add))
                for k in range(1, KC):
                    ins = v.scalar_tensor_tensor(out=cv, in0=xpad[:, :, k:k + L],
                                                 scalar=vec[:, V0["conv"] + k:V0["conv"] + k + 1],
                                                 in1=cv, op0=ALU.mult, op1=ALU.add)
                    if k < KC - 1:
                        step(ins)
                    else:
                        ins.then_inc(conv_ready.sem, 1)
                dve.wait_ge(logit_ps.sem, logit_ps.at(i, 1))
                br_all = brb[:, :].rearrange("p (a e) -> p a e", a=1).to_broadcast((128, TT, E))
                step(v.tensor_tensor(lg[:, :, :], bank[4][:, 0:TT * E].rearrange("p (k e) -> p k e", k=TT), br_all, ALU.add))
                step(v.tensor_reduce(lmax[:, :], lg[:, :, :], AXX, ALU.max))
                over_e = lambda ap: ap[:, :].rearrange("p (k a) -> p k a", a=1).to_broadcast((128, TT, E))
                v.tensor_tensor(lg[:, :, :], lg[:, :, :], over_e(lmax), ALU.subtract).then_inc(lmax_sub.sem, 1)
                dve.wait_ge(xs_ready.sem, xs_ready.at(i, 1))
                dve.wait_ge(z_ps.sem, z_ps.at(i, 1))
                v.tensor_tensor(gate[:, :], xs[:, :], bank[7][:, :], ALU.mult).then_inc(gate_ready.sem, 1)
                dve.wait_ge(lexp_ready.sem, lexp_ready.at(i, 1))
                step(v.tensor_reduce(lsum[:, :], lexp[:, :, :], AXX, ALU.add))
                step(v.reciprocal(pmax[:, :], lsum[:, :]))
                step(v.tensor_scalar(eq[:, :, :], lg[:, :, :], 0.0, -float(E), ALU.is_equal, ALU.mult))
                step(v.tensor_tensor(eq[:, :, :], eq[:, :, :], iota[:, :, :], ALU.add))
                step(v.tensor_reduce(lmax[:, :], eq[:, :, :], AXX, ALU.min))
                v.tensor_tensor(onehot[:, :, :], eq[:, :, :], over_e(lmax), ALU.is_equal).then_inc(onehot_ready.sem, 1)
                dve.wait_ge(ohT_ps.sem, ohT_ps.at(i, 1))
                v.tensor_scalar(ohm[:, :], bank[5][0:E, :], 1.0, None, ALU.subtract)
                v.tensor_copy(ohT[:, :], bank[5][0:E, :]).then_inc(ohT_ready.sem, 1)
                dve.wait_ge(b_ps.sem, b_ps.at(i, 1))
                step(v.tensor_copy(Bst[:, :], bank[7][0:96, :]))
                step(v.tensor_tensor(Bres[:, :], bank[7][0:96, :], Bst[:, :], ALU.subtract))
                v.tensor_copy(Bst[32:64, :], Bres[32:64, :])
                step(v.tensor_copy(Bmid[64:96, :], Bres[64:96, :]))
                v.tensor_tensor(Bst[64:96, :], Bres[64:96, :], Bmid[64:96, :], ALU.subtract).then_inc(bst_ready.sem, 1)
                dve.wait_ge(sp_e_ready.sem, sp_e_ready.at(i, 1))
                v.tensor_scalar(sp_u[:, :], sp_e[:, :], 1.0, None, ALU.add).then_inc(sp_u_ready.sem, 1)
                dve.wait_ge(sp_u_ready.sem, sp_u_ready.at(i, 1))
                step(v.scalar_tensor_tensor(out=sp_e[:, :], in0=sp_u[:, :], scalar=1.0, in1=sp_e[:, :],
                                            op0=ALU.subtract, op1=ALU.subtract))
                dve.wait_ge(sp_r_ready.sem, sp_r_ready.at(i, 1))
                step(v.tensor_tensor(sp_e[:, :], sp_e[:, :], sp_r[:, :], ALU.mult))
                step(v.tensor_tensor(sp_l[:, :], sp_l[:, :], sp_e[:, :], ALU.subtract))
                v.tensor_tensor(delta[:, :], sp_x[:, :], sp_l[:, :], ALU.add).then_inc(delta_ready.sem, 1)
                dve.wait_ge(delta_ready.sem, delta_ready.at(i, 1))
                step(v.tensor_tensor(dx[:, :], delta[:, :], gate[:, :], ALU.mult))

                def form_drive(n):
                    dve.wait_ge(bc_ps.sem, bc_ps.at(i, n + 1))
                    v.tensor_tensor(drive[:, n % RING, :], dx[:, :], bank[n % 2][:, :], ALU.mult).then_inc(drive_ready.sem, 1)

                form_drive(0)
                for n in range(N):
                    if n + 1 < N:
                        form_drive(n + 1)
                    dve.wait_ge(decay_ready.sem, decay_ready.at(i, n + 1))
                    dve.wait_ge(drive_ready.sem, drive_ready.at(i, n + 1))
                    dve.wait_ge(product_ready.sem, product_ready.at(i, max(n - RING + 1, 0)))
                    v.tensor_tensor_scan(state[:, n % RING, :], decay[:, n % RING, :], drive[:, n % RING, :], 0.0,
                                         ALU.mult, ALU.add).then_inc(state_ready.sem, 1)
                dve.wait_ge(summed.sem, summed.at(i, N))
                v.tensor_tensor(yT[:, :], XNT[:, :], bank[2][:, :], ALU.add).then_inc(yT_ready.sem, 1)
                dve.wait_ge(y_ps.sem, y_ps.at(i, 1))
                normalise(yn, tiles(bank[6]), 2, yn_ready)
                dve.wait_ge(ynT_ps.sem, ynT_ps.at(i, 1))
                v.tensor_scalar(ynT[:, :], bank[7][:, :], vec[:, V0["gam"]:V0["gam"] + 1],
                                vec[:, V0["bet"]:V0["bet"] + 1], ALU.mult, ALU.add).then_inc(ynT_ready.sem, 1)
                dve.wait_ge(s_ps.sem, s_ps.at(i, 1))
                bo = bout[:, :].rearrange("p (a d) -> p a d", a=1).to_broadcast((128, TT, D))
                dve.wait_ge(x1_out.sem, x1_out.at(i, 0))
                step(v.tensor_tensor(so[:, :, :], tiles(bank[6]), bo, ALU.add))
                dve.wait_ge(g_ready.sem, g_ready.at(i, 1))
                step(v.tensor_tensor(so[:, :, :], so[:, :, :], g[:, :, :], ALU.mult))
                v.tensor_tensor(so[:, :, :], so[:, :, :], xt[:, :, :], ALU.add).then_inc(x1_ready.sem, 1)
                assert steps[0] == DVE_STEPS, steps

        @block.gpsimd
        def _(pool):
            p = nc.gpsimd
            pool.wait_ge(setup_dve.sem, 7)
            with pool.Fori(0, PAIRS) as i:
                def inverse_root(n):
                    pool.wait_ge(var_ready.sem, var_ready.at(i, n + 1))
                    p.tensor_tensor(rstd[:, :], veps[:, :], half[:, :], ALU.pow).then_inc(rstd_ready.sem, 1)

                inverse_root(0)
                inverse_root(1)
                for n in range(N):
                    pool.wait_ge(state_ready.sem, state_ready.at(i, n + 1))
                    if n % PC == 0:
                        pool.wait_ge(c_in[n // PC].sem, c_in[n // PC].at(i, 16))
                    pool.wait_ge(summed.sem, summed.at(i, max(n - RING + 1, 0)))
                    p.tensor_tensor(product[:, n % RING, :], state[:, n % RING, :], Cb[:, n // PC, n % PC, :],
                                    ALU.mult).then_inc(product_ready.sem, 1)
                inverse_root(2)

        @block.scalar
        def _(act):
            a = nc.scalar
            steps = [0]
            act.wait_ge(consts_in.sem, 16 * SMALL)
            a.activation(negA[:, :], vec[:, V0["alog"]:V0["alog"] + N], ACT.Exp).then_inc(setup_act.sem, 1)
            act.wait_ge(setup_dve.sem, 7)
            with act.Fori(0, PAIRS) as i:
                def step(ins):
                    steps[0] += 1
                    ins.then_inc(act_step.sem, 1)
                    act.wait_ge(act_step.sem, act_step.at(i, steps[0]))

                act.wait_ge(xnT_ps.sem, xnT_ps.at(i, 1))
                a.activation(XNT[:, :], bank[6][:, :], ACT.Copy).then_inc(XNT_ready.sem, 1)
                act.wait_ge(xfT_ps.sem, xfT_ps.at(i, 1))
                a.activation(XFT[:, :], bank[7][:, :], ACT.Identity, bias=vec[:, V0["lnb"]:V0["lnb"] + 1],
                             scale=vec[:, V0["lng"]:V0["lng"] + 1]).then_inc(XFT_ready.sem, 1)
                act.wait_ge(xin_ps.sem, xin_ps.at(i, 1))
                a.activation(xpad[:, :, KC - 1:], by_batch(bank[6][:, :]), ACT.Copy).then_inc(xpad_ready.sem, 1)
                act.wait_ge(conv_ready.sem, conv_ready.at(i, 1))
                a.activation(xs[:, :], conv[:, :], ACT.Silu).then_inc(xs_ready.sem, 1)
                act.wait_ge(lmax_sub.sem, lmax_sub.at(i, 1))
                a.activation(lexp[:, :, :], lg[:, :, :], ACT.Exp).then_inc(lexp_ready.sem, 1)
                act.wait_ge(c_ps.sem, c_ps.at(i, 1))
                act.wait_ge(c_out.sem, c_out.at(i, 0))
                a.activation(Crows[:, :], bank[3][0:N, :], ACT.Copy).then_inc(crows_ready.sem, 1)
                bdt = vec[:, V0["bdt"]:V0["bdt"] + 1]
                act.wait_ge(dt_ps.sem, dt_ps.at(i, 1))
                step(a.activation(sp_a[:, :], bank[6][:, :], ACT.Abs, bias=bdt))
                a.activation(sp_x[:, :], bank[6][:, :], ACT.Relu, bias=bdt)
                a.activation(sp_e[:, :], sp_a[:, :], ACT.Exp, scale=-1.0).then_inc(sp_e_ready.sem, 1)
                act.wait_ge(sp_u_ready.sem, sp_u_ready.at(i, 1))
                step(a.activation(sp_l[:, :], sp_u[:, :], ACT.Ln))
                a.activation(sp_r[:, :], sp_l[:, :], ACT.Exp, scale=-1.0).then_inc(sp_r_ready.sem, 1)
                act.wait_ge(delta_ready.sem, delta_ready.at(i, 1))

                def form_decay(n):
                    act.wait_ge(state_ready.sem, state_ready.at(i, max(n - RING + 1, 0)))
                    a.activation(by_batch(decay[:, n % RING, :])[:, :, 1:], by_batch(delta[:, :])[:, :, 1:], ACT.Exp,
                                 scale=negA[:, n:n + 1]).then_inc(decay_ready.sem, 1)

                for n in range(RING - 1):
                    form_decay(n)
                for u in range(UNITS):
                    act.wait_ge(hid_ps.sem, hid_ps.at(i, u + 1))
                    act.wait_ge(down_done.sem, down_done.at(i, max(u - 1, 0)))
                    a.activation(hid[:, u % 2, :], bank[4 + u % 2][:, :], ACT.Relu,
                                 bias=vec[:, V0["b1"] + u:V0["b1"] + u + 1]).then_inc(hid_ready.sem, 1)
                    n = chunk_after(u, N)
                    if n is not None and n + RING - 1 < N:
                        form_decay(n + RING - 1)
                act.wait_ge(ffn_ps.sem, ffn_ps.at(i, 1))
                a.activation(yfT[:, :], bank[3][:, :], ACT.Copy).then_inc(yfT_ready.sem, 1)
                act.wait_ge(yf_ps.sem, yf_ps.at(i, 1))
                for k in range(TT):
                    last = a.activation(g[:, k, :], bank[4][:, 128 * k:128 * k + 128], ACT.Silu, scale=pmax[:, k:k + 1])
                last.then_inc(g_ready.sem, 1)
                assert steps[0] == ACT_STEPS, steps

        @block.tensor
        def _(pe):
            t = nc.tensor
            pe.wait_ge(consts_in.sem, 16 * SMALL)
            pe.wait_ge(experts_in.sem, 16 * (EXPERT_LOADS + 2))
            with pe.Fori(0, PAIRS) as i:
                def transposes(dst, src, done):
                    for k in range(TT):
                        last = t.transpose(dst[:, 128 * k:128 * k + 128], src(k), ident[:, :])
                    last.then_inc(done.sem, 1)

                pe.wait_ge(xn_ready.sem, xn_ready.at(i, 1))
                pe.wait_ge(x1_ready.sem, x1_ready.at(i, 0))
                transposes(bank[6], lambda k: xn[:, k, :], xnT_ps)
                pe.wait_ge(xf_ready.sem, xf_ready.at(i, 1))
                transposes(bank[7], lambda k: xf[:, k, :], xfT_ps)
                pe.wait_ge(XNT_ready.sem, XNT_ready.at(i, 1))
                t.matmul(bank[6][:, :], w_in[:, 0:D], XNT[:, :], start=True, stop=True).then_inc(xin_ps.sem, 1)
                pe.wait_ge(g_ready.sem, g_ready.at(i, 0))
                for k in range(TT):
                    last = t.matmul(bank[4][:, E * k:E * k + E], XNT[:, 128 * k:128 * k + 128], w_r[:, :],
                                    start=True, stop=True)
                last.then_inc(logit_ps.sem, 1)
                pe.wait_ge(XFT_ready.sem, XFT_ready.at(i, 1))
                t.matmul(bank[7][:, :], w_in[:, D:2 * D], XNT[:, :], start=True, stop=True).then_inc(z_ps.sem, 1)
                pe.wait_ge(gate_ready.sem, gate_ready.at(i, 1))
                pe.wait_ge(xpad_ready.sem, xpad_ready.at(i, 1))
                t.matmul(bank[6][:, :], w_dt[:, :], gate[:, :], start=True, stop=True).then_inc(dt_ps.sem, 1)
                t.matmul(bank[7][0:96, :], w_b[:, :], gate[:, :], start=True, stop=True).then_inc(b_ps.sem, 1)
                pe.wait_ge(yfT_ready.sem, yfT_ready.at(i, 0))
                t.matmul(bank[3][0:N, :], w_c[:, :], gate[:, :], start=True, stop=True).then_inc(c_ps.sem, 1)
                pe.wait_ge(onehot_ready.sem, onehot_ready.at(i, 1))
                for k in range(TT):
                    last = t.transpose(bank[5][0:E, 128 * k:128 * k + 128], onehot[:, k, :], ident[:, :])
                last.then_inc(ohT_ps.sem, 1)
                pe.wait_ge(ohT_ready.sem, ohT_ready.at(i, 1))

                def hidden(u):
                    if u >= 2:
                        pe.wait_ge(hid_ready.sem, hid_ready.at(i, u - 1))
                    e, f = u // FT, u % FT
                    t.matmul(bank[4 + u % 2][:, :], w1[:, e, 128 * f:128 * f + 128], XFT[:, :], start=True, stop=False)
                    t.matmul(bank[4 + u % 2][:, :], big[:, 128 * e:128 * e + 128], ohm[:, :],
                             start=False, stop=True).then_inc(hid_ps.sem, 1)

                def down(u):
                    if u == 0:
                        pe.wait_ge(crows_ready.sem, crows_ready.at(i, 1))
                    pe.wait_ge(hid_ready.sem, hid_ready.at(i, u + 1))
                    t.matmul(bank[3][:, :], w2[:, u, :], hid[:, u % 2, :], start=(u == 0), stop=False).then_inc(down_done.sem, 1)

                def spread_b(n):
                    if n == 0:
                        pe.wait_ge(bst_ready.sem, bst_ready.at(i, 1))
                    pe.wait_ge(drive_ready.sem, drive_ready.at(i, max(n - 1, 0)))
                    t.matmul(bank[n % 2][:, :], sel[:, 128 * n:128 * n + 128], Bst[:, :], start=True, stop=True).then_inc(bc_ps.sem, 1)

                def sum_state(n):
                    if n == 0:
                        pe.wait_ge(yT_ready.sem, yT_ready.at(i, 0))
                    pe.wait_ge(product_ready.sem, product_ready.at(i, n + 1))
                    t.matmul(bank[2][:, :], ident[:, :], product[:, n % RING, :], start=(n == 0), stop=(n == N - 1)).then_inc(summed.sem, 1)

                for u in range(UNITS):
                    hidden(u)
                    if u >= 1:
                        down(u - 1)
                    n = chunk_after(u, N + LAG)
                    if n is not None:
                        if n < N:
                            spread_b(n)
                        if n >= LAG:
                            sum_state(n - LAG)
                down(UNITS - 1)
                t.matmul(bank[3][:, :], b2[:, :], ohT[:, :], start=False, stop=True).then_inc(ffn_ps.sem, 1)
                pe.wait_ge(yT_ready.sem, yT_ready.at(i, 1))
                pe.wait_ge(delta_ready.sem, delta_ready.at(i, 1))
                transposes(bank[6], lambda k: yT[:, 128 * k:128 * k + 128], y_ps)
                pe.wait_ge(yfT_ready.sem, yfT_ready.at(i, 1))
                transposes(bank[4], lambda k: yfT[:, 128 * k:128 * k + 128], yf_ps)
                pe.wait_ge(yn_ready.sem, yn_ready.at(i, 1))
                transposes(bank[7], lambda k: yn[:, k, :], ynT_ps)
                pe.wait_ge(ynT_ready.sem, ynT_ready.at(i, 1))
                for k in range(TT):
                    last = t.matmul(bank[6][:, 128 * k:128 * k + 128], ynT[:, 128 * k:128 * k + 128], w_out[:, :],
                                    start=True, stop=True)
                last.then_inc(s_ps.sem, 1)


def layer1(nc, x, out, crow, cwrow, w):
    ctx = ExitStack()
    with ctx:
        sb = lambda name, shape, dt=F32: ctx.enter_context(nc.sbuf_tensor("q_" + name, shape, dt))
        starts = ('c_in0', 'c_in1', 'c_in2', 'c_in3', 'c_out', 'cw_in', 'delta_ready', 'down_done', 'drive_ready', 'g_ready', 'hid_ready', 'product_ready', 'state_ready', 'summed', 'up_ps', 'x_out', 'x_ready', 'xw_ready', 'yz_ready')
        started = {}

        def sig(name, per=1):
            s = Signal(ctx.enter_context(nc.semaphore("q_" + name)), per, int(name in starts))
            if s.start:
                started[name] = s
            return s

        bank = [ctx.enter_context(nc.psum_tensor(f"q_bank{k}", [128, 512], F32)) for k in range(8)]

        ident = sb("ident", [128, 128])
        sel = sb("sel", [96, N * 128], BF16)
        vec = sb("vec", [128, V1_COLS])
        w_in = sb("w_in", [128, 2 * J1 * 128])
        w_b = sb("w_b", [128, J1 * 96])
        w_cd = sb("w_cd", [128, J1 * 64])
        w_dt = sb("w_dt", [64, J1 * 128])
        w_out = sb("w_out", [128, J1, D])
        w_r = sb("w_r", [128, 2 * E])
        wg = sb("wg", [128, E, FT * 128])
        wu = sb("wu", [128, E, FT * 128])
        wd = sb("wd", [128, UNITS, D])
        negA = sb("negA", [128, J1 * N])
        half = sb("half", [128, TT])
        idle = sb("idle", [128, 1])

        xt = sb("xt", [128, TT, D])
        xn = sb("xn", [128, TT, D])
        XNT = sb("XNT", [128, T])
        stats = sb("stats", [128, TT, 6])
        mv = sb("mv", [128, TT, 2])
        veps = sb("veps", [128, TT])
        rstd = sb("rstd", [128, TT])
        xpad = sb("xpad", [128, J1, NB, KC - 1 + L])
        conv = sb("conv", [128, J1, T])
        xs = sb("xs", [128, J1, T])
        sz = sb("sz", [128, J1, T])
        cd = sb("cd", [64, J1, T])
        sp_a = sb("sp_a", [128, T])
        sp_e = sb("sp_e", [128, T])
        sp_u = sb("sp_u", [128, T])
        sp_l = sb("sp_l", [128, T])
        sp_r = sp_a
        sp_x = sb("sp_x", [128, T])
        delta = sb("delta", [128, J1, T])
        dx = sb("dx", [128, J1, T])
        Bst = sb("Bst", [96, J1, T], BF16)
        Bres = sb("Bres", [96, T])
        Bmid = sb("Bmid", [96, T], BF16)
        Cb = sb("Cb", [128, RING, PC, T])
        decay, drive, state, product = scan_ring(nc, ctx, "q_")
        lg = sb("lg", [128, 2 * TT, E])
        lmax = sb("lmax", [128, 2 * TT])
        lexp = sb("lexp", [128, 2 * TT, E])
        lsum = sb("lsum", [128, 2 * TT])
        linv = sb("linv", [128, 2 * TT])
        cw = sb("cw", [128, TT, E])
        cwT = sb("cwT", [E, T])
        cwb = sb("cwb", [128, E, T])
        xw = sb("xw", [128, 2, T])
        sg = sb("sg", [128, 2, T])
        hid = sb("hid", [128, 2, T])
        yfT = sb("yfT", [128, T])
        g = xn
        yz = conv
        so = sb("so", [128, TT, D])

        DVE_STEPS, ACT_STEPS = 33, 4
        C = J1 * N
        consts_in, experts_in = sig("consts_in"), sig("experts_in")
        x_in, x_out = sig("x_in", 16), sig("x_out", 16)
        c_out = sig("c_out", 16 * J1)
        c_in = [sig(f"c_in{k}", 32 * J1) for k in range(RING)]
        cw_out, cw_in = sig("cw_out", 16), sig("cw_in", 16)
        dve_step, act_step = sig("dve_step", DVE_STEPS), sig("act_step", ACT_STEPS)
        setup_dve, setup_act = sig("setup_dve"), sig("setup_act")
        var_ready, rstd_ready = sig("var_ready"), sig("rstd_ready")
        xn_ready, xnT_ps, XNT_ready = sig("xn_ready"), sig("xnT_ps"), sig("XNT_ready")
        in_ps, logit_ps = sig("in_ps", 2 * J1), sig("logit_ps")
        xpad_ready, sz_ready, conv_ready, xs_ready = sig("xpad_ready", J1), sig("sz_ready", J1), sig("conv_ready", J1), sig("xs_ready", J1)
        lmax_sub, lexp_ready, cw_ready = sig("lmax_sub"), sig("lexp_ready"), sig("cw_ready")
        cwT_ps, cwT_ready = sig("cwT_ps"), sig("cwT_ready")
        b_ps, cd_ps, cd_ready, bst_ready, dt_ps = sig("b_ps", J1), sig("cd_ps", J1), sig("cd_ready", J1), sig("bst_ready", J1), sig("dt_ps", J1)
        sp_x_ready, sp_e_ready, sp_u_ready, sp_r_ready, delta_ready = sig("sp_x_ready", J1), sig("sp_e_ready", J1), sig("sp_u_ready", J1), sig("sp_r_ready", J1), sig("delta_ready", J1)
        bc_ps, drive_ready, decay_ready = sig("bc_ps", C), sig("drive_ready", C), sig("decay_ready", C)
        state_ready, product_ready, summed = sig("state_ready", C), sig("product_ready", C), sig("summed", C)
        xw_ready = sig("xw_ready", E)
        gate_ps, up_ps, sg_ready = sig("gate_ps", UNITS), sig("up_ps", UNITS), sig("sg_ready", UNITS)
        hid_ready, down_done = sig("hid_ready", UNITS), sig("down_done", UNITS)
        yfT_ready, yf_ps, g_ready = sig("yfT_ready"), sig("yf_ps"), sig("g_ready")
        yz_ready, s_ps, x_ready = sig("yz_ready", J1), sig("s_ps"), sig("x_ready")

        CONST_LOADS = 9
        EXPERT_LOADS = 3 * E
        block = ctx.enter_context(nc.Block())

        def tiles(ap):
            return ap[:, :].rearrange("p (k d) -> p k d", k=TT)

        def by_batch(ap):
            return ap.rearrange("p (b l) -> p b l", b=NB)

        def column(name, k=0):
            return vec[:, V1[name] + k:V1[name] + k + 1]

        @block.sync
        def _(sp):
            for name in starts:
                sp.sem_inc(started[name].sem, 1)
            for name, dst in (("ident", ident), ("vec1", vec), ("w_in1", w_in), ("w_r1", w_r),
                              ("w_b1", w_b), ("w_cd1", w_cd), ("sel1", sel)):
                sp.dma_start(dst[:, :], w[name]).then_inc(consts_in.sem, 16)
            sp.dma_start(w_dt[:, :], w["w_dt1"]).then_inc(consts_in.sem, 16)
            sp.dma_start(w_out[:, :, :], w["w_out1"].rearrange("(j p) d -> p j d", p=128)).then_inc(consts_in.sem, 16)
            for e in range(E):
                sp.dma_start(wg[:, e, :], w["Wg"][e]).then_inc(experts_in.sem, 16)
                sp.dma_start(wu[:, e, :], w["Wu"][e]).then_inc(experts_in.sem, 16)
                sp.dma_start(wd[:, FT * e:FT * e + FT, :],
                             w["Wd"][e].rearrange("(f p) d -> p f d", p=128)).then_inc(experts_in.sem, 16)
            for i in range(PAIRS):
                sp.wait_ge(x_ready.sem, x_ready.at(i, 0))
                sp.dma_start(xt[:, :, :], x[i * T:i * T + T, :].rearrange("(k p) d -> p k d", p=128)).then_inc(x_in.sem, 16)
                sp.wait_ge(cwT_ready.sem, cwT_ready.at(i, 1))
                sp.wait_ge(cw_in.sem, cw_in.at(i, 0))
                sp.dma_start(cwrow[:, :], cwT[:, :]).then_inc(cw_out.sem, 16)
                sp.wait_ge(cw_out.sem, cw_out.at(i, 16))
                sp.wait_ge(xw_ready.sem, xw_ready.at(i, 0))
                sp.dma_start(cwb[:, :, :], cwrow.rearrange("(a e) t -> a e t", a=1).to_broadcast((128, E, T))).then_inc(cw_in.sem, 16)
                for j in range(J1):
                    sp.wait_ge(cd_ready.sem, cd_ready.at(i, j + 1))
                    for k in range(RING):
                        sp.wait_ge(c_in[k].sem, c_in[k].at(i, 0))
                    sp.dma_start(crow[j], cd[0:32, j, :]).then_inc(c_out.sem, 16)
                for j in range(J1):
                    sp.wait_ge(c_out.sem, c_out.at(i, 16 * J1))
                    for k in range(RING):
                        sp.wait_ge(product_ready.sem, product_ready.at(i, PC * (k + 1) if j else 0))
                        for h in range(2):
                            src = crow[j, N * h + PC * k:N * h + PC * k + PC, :].rearrange("(a r) t -> a r t", a=1)
                            sp.dma_start(Cb[64 * h:64 * h + 64, k, :, :], src.to_broadcast((64, PC, T))).then_inc(c_in[k].sem, 16)
                sp.wait_ge(x_ready.sem, x_ready.at(i, 1))
                sp.dma_start(out[i * T:i * T + T, :].rearrange("(k p) d -> p k d", p=128), so[:, :, :]).then_inc(x_out.sem, 16)
            sp.wait_ge(x_out.sem, x_out.at(PAIRS, 0))

        @block.vector
        def _(dve):
            v = nc.vector
            steps = [0]
            v.memset(xpad[:, :, :, 0:KC - 1].rearrange("p j b l -> p (j b) l"), 0.0).then_inc(setup_dve.sem, 1)
            for k in range(RING):
                v.memset(by_batch(decay[:, k, :])[:, :, 0:1], 0.0).then_inc(setup_dve.sem, 1)
            v.memset(half[:, :], -0.5).then_inc(setup_dve.sem, 1)
            dve.wait_ge(setup_act.sem, 1)
            v.tensor_scalar(negA[:, :], negA[:, :], -1.0, None, ALU.mult).then_inc(setup_dve.sem, 1)
            dve.wait_ge(setup_dve.sem, 7)

            with dve.Fori(0, PAIRS) as i:
                def step(ins):
                    steps[0] += 1
                    ins.then_inc(dve_step.sem, 1)
                    dve.wait_ge(dve_step.sem, dve_step.at(i, steps[0]))

                dve.wait_ge(x_in.sem, x_in.at(i, 16))
                for k in range(TT):
                    last = v.bn_stats(stats[:, k, :], xt[:, k, :])
                step(last)
                v.memset(idle[:, :], 0.0)
                for k in range(TT):
                    last = v.bn_aggr(mv[:, k, :], stats[:, k, :])
                step(last)
                v.tensor_scalar(veps[:, :], mv[:, :, 1], EPS, None, ALU.add).then_inc(var_ready.sem, 1)
                dve.wait_ge(rstd_ready.sem, rstd_ready.at(i, 1))
                for k in range(TT):
                    last = v.tensor_scalar(xn[:, k, :], xt[:, k, :], mv[:, k, 0:1], rstd[:, k:k + 1], ALU.subtract, ALU.mult)
                last.then_inc(xn_ready.sem, 1)
                over_e = lambda ap: ap.rearrange("p (k a) -> p k a", a=1).to_broadcast((128, ap.shape[1], E))
                dve.wait_ge(logit_ps.sem, logit_ps.at(i, 1))
                lps = bank[3][:, 0:2 * TT * E].rearrange("p (k e) -> p k e", e=E)
                step(v.tensor_reduce(lmax[:, :], lps, AXX, ALU.max))
                v.tensor_tensor(lg[:, :, :], lps, over_e(lmax[:, :]), ALU.subtract).then_inc(lmax_sub.sem, 1)

                def convolve(j):
                    dve.wait_ge(xpad_ready.sem, xpad_ready.at(i, j + 1))
                    cv = by_batch(conv[:, j, :])
                    step(v.tensor_scalar(cv, xpad[:, j, :, 0:L], column("conv", KC * j), column("bconv", j), ALU.mult, ALU.add))
                    for k in range(1, KC):
                        ins = v.scalar_tensor_tensor(out=cv, in0=xpad[:, j, :, k:k + L], scalar=column("conv", KC * j + k),
                                                     in1=cv, op0=ALU.mult, op1=ALU.add)
                        if k < KC - 1:
                            step(ins)
                        else:
                            ins.then_inc(conv_ready.sem, 1)

                convolve(0)
                dve.wait_ge(lexp_ready.sem, lexp_ready.at(i, 1))
                step(v.tensor_reduce(lsum[:, :], lexp[:, :, :], AXX, ALU.add))
                step(v.reciprocal(linv[:, :], lsum[:, :]))
                step(v.tensor_tensor(lexp[:, :, :], lexp[:, :, :], over_e(linv[:, :]), ALU.mult))
                step(v.tensor_tensor(cw[:, :, :], lexp[:, 0:TT, :], lexp[:, TT:, :], ALU.mult))
                step(v.tensor_reduce(lsum[:, 0:TT], cw[:, :, :], AXX, ALU.add))
                step(v.tensor_scalar(lsum[:, 0:TT], lsum[:, 0:TT], 1e-9, None, ALU.add))
                step(v.reciprocal(linv[:, 0:TT], lsum[:, 0:TT]))
                v.tensor_tensor(cw[:, :, :], cw[:, :, :], over_e(linv[:, 0:TT]), ALU.mult).then_inc(cw_ready.sem, 1)
                convolve(1)
                dve.wait_ge(cwT_ps.sem, cwT_ps.at(i, 1))
                v.tensor_copy(cwT[:, :], bank[3][0:E, :]).then_inc(cwT_ready.sem, 1)
                for j in range(J1):
                    dve.wait_ge(b_ps.sem, b_ps.at(i, j + 1))
                    step(v.tensor_copy(Bst[:, j, :], bank[7][0:96, :]))
                    step(v.tensor_tensor(Bres[:, :], bank[7][0:96, :], Bst[:, j, :], ALU.subtract))
                    v.tensor_copy(Bst[32:64, j, :], Bres[32:64, :])
                    step(v.tensor_copy(Bmid[64:96, :], Bres[64:96, :]))
                    v.tensor_tensor(Bst[64:96, j, :], Bres[64:96, :], Bmid[64:96, :], ALU.subtract).then_inc(bst_ready.sem, 1)
                    dve.wait_ge(sp_e_ready.sem, sp_e_ready.at(i, j + 1))
                    v.tensor_scalar(sp_u[:, :], sp_e[:, :], 1.0, None, ALU.add).then_inc(sp_u_ready.sem, 1)
                    dve.wait_ge(sp_u_ready.sem, sp_u_ready.at(i, j + 1))
                    step(v.scalar_tensor_tensor(out=sp_e[:, :], in0=sp_u[:, :], scalar=1.0, in1=sp_e[:, :],
                                                op0=ALU.subtract, op1=ALU.subtract))
                    dve.wait_ge(sp_r_ready.sem, sp_r_ready.at(i, j + 1))
                    step(v.tensor_tensor(sp_e[:, :], sp_e[:, :], sp_r[:, :], ALU.mult))
                    step(v.tensor_tensor(sp_l[:, :], sp_l[:, :], sp_e[:, :], ALU.subtract))
                    v.tensor_tensor(delta[:, j, :], sp_x[:, :], sp_l[:, :], ALU.add).then_inc(delta_ready.sem, 1)
                    dve.wait_ge(delta_ready.sem, delta_ready.at(i, j + 1))
                    step(v.tensor_tensor(dx[:, j, :], delta[:, j, :], xs[:, j, :], ALU.mult))

                def form_drive(c):
                    dve.wait_ge(bc_ps.sem, bc_ps.at(i, c + 1))
                    v.tensor_tensor(drive[:, c % RING, :], dx[:, c // N, :], bank[c % 2][:, :], ALU.mult).then_inc(drive_ready.sem, 1)

                def scan(c):
                    dve.wait_ge(decay_ready.sem, decay_ready.at(i, c + 1))
                    dve.wait_ge(drive_ready.sem, drive_ready.at(i, c + 1))
                    dve.wait_ge(product_ready.sem, product_ready.at(i, max(c - RING + 1, 0)))
                    v.tensor_tensor_scan(state[:, c % RING, :], decay[:, c % RING, :], drive[:, c % RING, :], 0.0,
                                         ALU.mult, ALU.add).then_inc(state_ready.sem, 1)

                def hidden_product(u):
                    dve.wait_ge(sg_ready.sem, sg_ready.at(i, u + 1))
                    dve.wait_ge(up_ps.sem, up_ps.at(i, u + 1))
                    dve.wait_ge(down_done.sem, down_done.at(i, max(u - 1, 0)))
                    v.tensor_tensor(hid[:, u % 2, :], sg[:, u % 2, :], bank[6][:, :], ALU.mult).then_inc(hid_ready.sem, 1)

                def gated_y(j):
                    dve.wait_ge(summed.sem, summed.at(i, N * (j + 1)))
                    step(v.scalar_tensor_tensor(out=yz[:, j, :], in0=xs[:, j, :], scalar=column("dskip", j),
                                                in1=bank[2][:, :], op0=ALU.mult, op1=ALU.add))
                    v.tensor_tensor(yz[:, j, :], yz[:, j, :], sz[:, j, :], ALU.mult).then_inc(yz_ready.sem, 1)

                for u in range(UNITS + LAG1 + 2):
                    if u < UNITS:
                        hidden_product(u)
                    if u < C:
                        form_drive(u)
                    if 1 <= u <= C:
                        scan(u - 1)
                    if u % N == LAG1 and u > N:
                        gated_y(u // N - 1)
                dve.wait_ge(s_ps.sem, s_ps.at(i, 1))
                dve.wait_ge(g_ready.sem, g_ready.at(i, 1))
                dve.wait_ge(x_out.sem, x_out.at(i, 0))
                step(v.tensor_tensor(so[:, :, :], tiles(bank[7]), g[:, :, :], ALU.mult))
                v.tensor_tensor(so[:, :, :], so[:, :, :], xt[:, :, :], ALU.add).then_inc(x_ready.sem, 1)
                assert steps[0] == DVE_STEPS, steps

        @block.gpsimd
        def _(pool):
            p = nc.gpsimd
            pool.wait_ge(setup_dve.sem, 7)
            with pool.Fori(0, PAIRS) as i:
                pool.wait_ge(var_ready.sem, var_ready.at(i, 1))
                p.tensor_tensor(rstd[:, :], veps[:, :], half[:, :], ALU.pow).then_inc(rstd_ready.sem, 1)

                def weigh_tokens(e):
                    if e == 0:
                        pool.wait_ge(cw_in.sem, cw_in.at(i, 16))
                        pool.wait_ge(XNT_ready.sem, XNT_ready.at(i, 1))
                    pool.wait_ge(up_ps.sem, up_ps.at(i, max(FT * (e - 1), 0)))
                    p.tensor_tensor(xw[:, e % 2, :], XNT[:, :], cwb[:, e, :], ALU.mult).then_inc(xw_ready.sem, 1)

                weigh_tokens(0)
                weigh_tokens(1)
                for c in range(C):
                    pool.wait_ge(state_ready.sem, state_ready.at(i, c + 1))
                    if c % PC == 0:
                        pool.wait_ge(c_in[c // PC % RING].sem, c_in[c // PC % RING].at(i, 32 * (c // N + 1)))
                    pool.wait_ge(summed.sem, summed.at(i, max(c - RING + 1, 0)))
                    p.tensor_tensor(product[:, c % RING, :], state[:, c % RING, :], Cb[:, c // PC % RING, c % PC, :],
                                    ALU.mult).then_inc(product_ready.sem, 1)
                    if c % FT == FT - 1 and c // FT + 2 < E:
                        weigh_tokens(c // FT + 2)

        @block.scalar
        def _(act):
            a = nc.scalar
            steps = [0]
            act.wait_ge(consts_in.sem, 16 * CONST_LOADS)
            a.activation(negA[:, :], vec[:, V1["alog"]:V1["alog"] + J1 * N], ACT.Exp).then_inc(setup_act.sem, 1)
            act.wait_ge(setup_dve.sem, 7)
            with act.Fori(0, PAIRS) as i:
                def step(ins):
                    steps[0] += 1
                    ins.then_inc(act_step.sem, 1)
                    act.wait_ge(act_step.sem, act_step.at(i, steps[0]))

                act.wait_ge(xnT_ps.sem, xnT_ps.at(i, 1))
                a.activation(XNT[:, :], bank[7][:, :], ACT.Copy).then_inc(XNT_ready.sem, 1)
                for j in range(J1):
                    act.wait_ge(in_ps.sem, in_ps.at(i, j + 1))
                    a.activation(xpad[:, j, :, KC - 1:], by_batch(bank[4 + j][:, :]), ACT.Copy).then_inc(xpad_ready.sem, 1)
                act.wait_ge(lmax_sub.sem, lmax_sub.at(i, 1))
                a.activation(lexp[:, 0:TT, :], lg[:, 0:TT, :], ACT.Exp)
                a.activation(lexp[:, TT:, :], lg[:, TT:, :], ACT.Exp, scale=1.0 / GATE_TEMP).then_inc(lexp_ready.sem, 1)
                for j in range(J1):
                    act.wait_ge(in_ps.sem, in_ps.at(i, J1 + j + 1))
                    a.activation(sz[:, j, :], bank[6 + j][:, :], ACT.Silu).then_inc(sz_ready.sem, 1)
                for j in range(J1):
                    act.wait_ge(conv_ready.sem, conv_ready.at(i, j + 1))
                    a.activation(xs[:, j, :], conv[:, j, :], ACT.Silu).then_inc(xs_ready.sem, 1)
                for j in range(J1):
                    act.wait_ge(cd_ps.sem, cd_ps.at(i, j + 1))
                    act.wait_ge(c_out.sem, c_out.at(i, 0))
                    a.activation(cd[:, j, :], bank[2][0:64, :], ACT.Copy).then_inc(cd_ready.sem, 1)
                    act.wait_ge(dt_ps.sem, dt_ps.at(i, j + 1))
                    act.wait_ge(delta_ready.sem, delta_ready.at(i, j))
                    step(a.activation(sp_a[:, :], bank[7][:, :], ACT.Abs, bias=column("bdt", j)))
                    a.activation(sp_x[:, :], bank[7][:, :], ACT.Relu, bias=column("bdt", j)).then_inc(sp_x_ready.sem, 1)
                    a.activation(sp_e[:, :], sp_a[:, :], ACT.Exp, scale=-1.0).then_inc(sp_e_ready.sem, 1)
                    act.wait_ge(sp_u_ready.sem, sp_u_ready.at(i, j + 1))
                    step(a.activation(sp_l[:, :], sp_u[:, :], ACT.Ln))
                    a.activation(sp_r[:, :], sp_l[:, :], ACT.Exp, scale=-1.0).then_inc(sp_r_ready.sem, 1)
                act.wait_ge(delta_ready.sem, delta_ready.at(i, J1))

                def form_decay(c):
                    act.wait_ge(state_ready.sem, state_ready.at(i, max(c - RING + 1, 0)))
                    a.activation(by_batch(decay[:, c % RING, :])[:, :, 1:], by_batch(delta[:, c // N, :])[:, :, 1:], ACT.Exp,
                                 scale=negA[:, c:c + 1]).then_inc(decay_ready.sem, 1)

                for c in range(RING):
                    form_decay(c)
                for u in range(UNITS):
                    act.wait_ge(gate_ps.sem, gate_ps.at(i, u + 1))
                    act.wait_ge(hid_ready.sem, hid_ready.at(i, max(u - 1, 0)))
                    a.activation(sg[:, u % 2, :], bank[4 + u % 2][:, :], ACT.Silu).then_inc(sg_ready.sem, 1)
                    if RING <= u + 3 < C and u + 3 >= RING:
                        form_decay(u + 3)
                step_free = down_done.at(i, UNITS)
                act.wait_ge(down_done.sem, step_free)
                a.activation(yfT[:, :], bank[3][:, :], ACT.Copy).then_inc(yfT_ready.sem, 1)
                act.wait_ge(yf_ps.sem, yf_ps.at(i, 1))
                a.activation(g[:, :, :], tiles(bank[4]), ACT.Silu).then_inc(g_ready.sem, 1)
                assert steps[0] == ACT_STEPS, steps

        @block.tensor
        def _(pe):
            t = nc.tensor
            pe.wait_ge(consts_in.sem, 16 * CONST_LOADS)
            pe.wait_ge(experts_in.sem, 16 * EXPERT_LOADS)
            with pe.Fori(0, PAIRS) as i:
                def transposes(dst, src, done):
                    for k in range(TT):
                        last = t.transpose(dst[:, 128 * k:128 * k + 128], src(k), ident[:, :])
                    last.then_inc(done.sem, 1)

                pe.wait_ge(xn_ready.sem, xn_ready.at(i, 1))
                pe.wait_ge(x_ready.sem, x_ready.at(i, 0))
                transposes(bank[7], lambda k: xn[:, k, :], xnT_ps)
                pe.wait_ge(XNT_ready.sem, XNT_ready.at(i, 1))
                pe.wait_ge(g_ready.sem, g_ready.at(i, 0))
                for m in range(2 * J1):
                    t.matmul(bank[4 + m][:, :], w_in[:, 128 * m:128 * m + 128], XNT[:, :], start=True, stop=True).then_inc(in_ps.sem, 1)
                    if m == J1 - 1:
                        for k in range(2 * TT):
                            kind, tile = k // TT, k % TT
                            last = t.matmul(bank[3][:, E * k:E * k + E], XNT[:, 128 * tile:128 * tile + 128],
                                            w_r[:, E * kind:E * kind + E], start=True, stop=True)
                        last.then_inc(logit_ps.sem, 1)
                pe.wait_ge(cw_ready.sem, cw_ready.at(i, 1))
                for k in range(TT):
                    last = t.transpose(bank[3][0:E, 128 * k:128 * k + 128], cw[:, k, :], ident[:, :])
                last.then_inc(cwT_ps.sem, 1)
                pe.wait_ge(yz_ready.sem, yz_ready.at(i, 0))
                pe.wait_ge(sz_ready.sem, sz_ready.at(i, J1))
                for j in range(J1):
                    pe.wait_ge(xs_ready.sem, xs_ready.at(i, j + 1))
                    if j:
                        pe.wait_ge(delta_ready.sem, delta_ready.at(i, j))
                    t.matmul(bank[7][0:96, :], w_b[:, 96 * j:96 * j + 96], xs[:, j, :], start=True, stop=True).then_inc(b_ps.sem, 1)
                    t.matmul(bank[2][0:64, :], w_cd[:, 64 * j:64 * j + 64], xs[:, j, :], start=True, stop=True).then_inc(cd_ps.sem, 1)
                    pe.wait_ge(cd_ready.sem, cd_ready.at(i, j + 1))
                    pe.wait_ge(bst_ready.sem, bst_ready.at(i, j + 1))
                    t.matmul(bank[7][:, :], w_dt[32:64, 128 * j:128 * j + 128], cd[32:64, j, :], start=True, stop=True).then_inc(dt_ps.sem, 1)
                pe.wait_ge(cwT_ready.sem, cwT_ready.at(i, 1))

                def gate(u):
                    if u >= 2:
                        pe.wait_ge(sg_ready.sem, sg_ready.at(i, u - 1))
                    e, f = u // FT, u % FT
                    t.matmul(bank[4 + u % 2][:, :], wg[:, e, 128 * f:128 * f + 128], XNT[:, :], start=True, stop=True).then_inc(gate_ps.sem, 1)

                def up(u):
                    e, f = u // FT, u % FT
                    if f == 0:
                        pe.wait_ge(xw_ready.sem, xw_ready.at(i, e + 1))
                    pe.wait_ge(hid_ready.sem, hid_ready.at(i, u))
                    t.matmul(bank[6][:, :], wu[:, e, 128 * f:128 * f + 128], xw[:, e % 2, :], start=True, stop=True).then_inc(up_ps.sem, 1)

                def down(u):
                    pe.wait_ge(hid_ready.sem, hid_ready.at(i, u + 1))
                    t.matmul(bank[3][:, :], wd[:, u, :], hid[:, u % 2, :], start=(u == 0), stop=(u == UNITS - 1)).then_inc(down_done.sem, 1)

                def spread_b(c):
                    if c == 0:
                        pe.wait_ge(bst_ready.sem, bst_ready.at(i, J1))
                    pe.wait_ge(drive_ready.sem, drive_ready.at(i, max(c - 1, 0)))
                    n = c % N
                    t.matmul(bank[c % 2][:, :], sel[:, 128 * n:128 * n + 128], Bst[:, c // N, :], start=True, stop=True).then_inc(bc_ps.sem, 1)

                def sum_state(c):
                    if c % N == 0:
                        pe.wait_ge(yz_ready.sem, yz_ready.at(i, c // N))
                    pe.wait_ge(product_ready.sem, product_ready.at(i, c + 1))
                    t.matmul(bank[2][:, :], ident[:, :], product[:, c % RING, :], start=(c % N == 0), stop=(c % N == N - 1)).then_inc(summed.sem, 1)

                for u in range(UNITS + LAG1 + 1):
                    if u < UNITS:
                        gate(u)
                    if 1 <= u <= UNITS:
                        down(u - 1)
                    if u < UNITS:
                        up(u)
                    if u < C:
                        spread_b(u)
                    if LAG1 <= u < C + LAG1:
                        sum_state(u - LAG1)
                pe.wait_ge(yfT_ready.sem, yfT_ready.at(i, 1))
                transposes(bank[4], lambda k: yfT[:, 128 * k:128 * k + 128], yf_ps)
                pe.wait_ge(yz_ready.sem, yz_ready.at(i, J1))
                for k in range(TT):
                    for j in range(J1):
                        last = t.matmul(bank[7][:, 128 * k:128 * k + 128], yz[:, j, 128 * k:128 * k + 128], w_out[:, j, :],
                                        start=(j == 0), stop=(j == J1 - 1))
                last.then_inc(s_ps.sem, 1)


CONSTS = {
    "ident": ((128, 128), F32), "vec0": ((128, V0_COLS), F32), "w_in0": ((128, 2 * D), F32),
    "w_r0": ((128, E), F32), "br0": ((1, E), F32), "iota": ((128, TT, E), F32), "w_dt0": ((128, D), F32),
    "w_b0": ((128, 96), F32), "w_c0": ((128, N), F32), "sel0": ((96, N * 128), BF16), "big": ((E, E * 128), BF16),
    "w_out0": ((128, D), F32), "b2": ((E, D), F32), "b_out0": ((1, D), F32),
    "W1": ((E, D, FT * 128), F32), "W2": ((E, FT * 128, D), F32),
    "vec1": ((128, V1_COLS), F32), "w_in1": ((128, 2 * J1 * 128), F32), "w_r1": ((128, 2 * E), F32),
    "w_b1": ((128, J1 * 96), F32), "w_cd1": ((128, J1 * 64), F32), "w_dt1": ((64, J1 * 128), F32),
    "sel1": ((96, N * 128), BF16), "w_out1": ((J1 * 128, D), F32),
    "Wg": ((E, D, FT * 128), F32), "Wu": ((E, D, FT * 128), F32), "Wd": ((E, FT * 128, D), F32),
}


def program(nc, x, out, w):
    crow = nc.dram_tensor("crow", (N, T), F32, kind="Internal").ap()
    x1 = nc.dram_tensor("x1", (B * L, D), F32, kind="Internal").ap()
    crow1 = nc.dram_tensor("crow1", (J1, 2 * N, T), F32, kind="Internal").ap()
    cwrow = nc.dram_tensor("cwrow", (E, T), F32, kind="Internal").ap()
    layer0(nc, x, x1, crow, w)
    layer1(nc, x1, out, crow1, cwrow, w)


def kernel(**inputs):
    import numpy as np
    import ml_dtypes
    import concourse.bacc as bacc
    from concourse.bass_utils import run_bass_kernel_spmd

    a = {k: np.asarray(v) for k, v in inputs.items()}
    col = lambda v: v.reshape(1, -1).T if v.ndim == 1 else v
    c = {}
    c["ident"] = np.eye(128, dtype=np.float32)
    c["vec0"] = np.concatenate([a["L0_attn_W_conv"][:, 0, :], col(a["L0_attn_b_conv"]), col(a["L0_attn_b_dt"]),
                                a["L0_attn_A_log"], col(a["L0_attn_ln_gamma"]), col(a["L0_attn_ln_beta"]),
                                col(a["L0_ffn_ln_g"]), col(a["L0_ffn_ln_b"]), a["L0_ffn_b1"].reshape(UNITS, 128).T], axis=1)
    c["w_in0"] = a["L0_attn_W_in"].T
    c["w_r0"] = a["L0_ffn_Wr"]
    c["br0"] = a["L0_ffn_br"].reshape(1, E)
    c["iota"] = np.tile(np.arange(E, dtype=np.float32), (128, TT, 1))
    c["w_dt0"] = a["L0_attn_W_dt"].T
    bt = a["L0_attn_W_xproj"][:N].T
    strip = np.concatenate([bt, np.zeros_like(bt)], axis=1)
    c["w_b0"] = np.concatenate([strip] * 3, axis=1)
    c["w_c0"] = a["L0_attn_W_xproj"][N:].T
    sel = np.zeros((3, 32, N, 128), np.float32)
    for n in range(N):
        sel[:, n, n, :] = 1.0
    c["sel0"] = sel.reshape(96, N * 128).astype(ml_dtypes.bfloat16)
    big = np.zeros((E, E, 128), np.float32)
    for e in range(E):
        big[e, e, :] = BIG
    c["big"] = big.reshape(E, E * 128).astype(ml_dtypes.bfloat16)
    c["w_out0"] = a["L0_attn_W_out"].T
    c["b2"] = a["L0_ffn_b2"]
    c["b_out0"] = a["L0_attn_b_out"].reshape(1, D)
    c["W1"], c["W2"] = a["L0_ffn_W1"], a["L0_ffn_W2"]

    per_tile = lambda v: v.reshape(J1, 128, -1).transpose(1, 0, 2).reshape(128, -1)
    c["vec1"] = np.concatenate([per_tile(v) for v in (
        a["L1_attn_conv_w"][:, 0, :], a["L1_attn_conv_b"], a["L1_attn_dt_proj_b"], a["L1_attn_A_log"], a["L1_attn_Dskip"])], axis=1)
    c["w_in1"] = a["L1_attn_in_proj_w"].T
    c["w_r1"] = np.concatenate([a["L1_ffn_w_router"], a["L1_ffn_w_gating"]], axis=1)
    xp = a["L1_attn_x_proj_w"].reshape(2 * J1, 3 * N, 64)
    dp = a["L1_attn_dt_proj_w"].reshape(2 * J1, 64, N)
    w_b, w_cd, w_dt = np.zeros((128, J1, 3, 32), np.float32), np.zeros((128, J1, 64), np.float32), np.zeros((64, J1, 128), np.float32)
    sel = np.zeros((3, 32, N, 128), np.float32)
    for h in range(2):
        ch, row = slice(64 * h, 64 * h + 64), slice(N * h, N * h + N)
        for j in range(J1):
            w_b[ch, j, :, row] = xp[2 * j + h, N:2 * N].T[:, None, :]
            w_cd[ch, j, row] = xp[2 * j + h, 2 * N:].T
            w_cd[ch, j, 32 + N * h:32 + N * h + N] = xp[2 * j + h, :N].T
            w_dt[32 + N * h:32 + N * h + N, j, ch] = dp[2 * j + h].T
        for n in range(N):
            sel[:, N * h + n, n, ch] = 1.0
    c["w_b1"], c["w_cd1"], c["w_dt1"] = w_b.reshape(128, -1), w_cd.reshape(128, -1), w_dt.reshape(64, -1)
    c["sel1"] = sel.reshape(96, N * 128).astype(ml_dtypes.bfloat16)
    c["w_out1"] = a["L1_attn_out_proj_w"].T
    c["Wg"], c["Wu"], c["Wd"] = a["L1_ffn_w_gate"], a["L1_ffn_w_up"], a["L1_ffn_w_down"]

    nc = bacc.Bacc("TRN2", target_bir_lowering=False, num_devices=1)
    arrays = {"x_dram": np.ascontiguousarray(a["L0_attn_x"].reshape(B * L, D))}
    x = nc.dram_tensor("x_dram", (B * L, D), F32, kind="ExternalInput").ap()
    w = {}
    for name, (shape, dt) in CONSTS.items():
        arrays[name + "_dram"] = np.ascontiguousarray(c[name])
        assert arrays[name + "_dram"].shape == shape, name
        w[name] = nc.dram_tensor(name + "_dram", shape, dt, kind="ExternalInput").ap()
    out = nc.dram_tensor("out_dram", (B * L, D), F32, kind="ExternalOutput").ap()
    program(nc, x, out, w)
    r = run_bass_kernel_spmd(nc, [arrays], core_ids=[0])
    return r.results[0]["out_dram"].reshape(B, L, D)
```

```python
import concourse.bass as bass
from concourse import mybir
from contextlib import ExitStack

F32 = mybir.dt.float32
F32R = mybir.dt.float32r
BF16 = mybir.dt.bfloat16
ALU = mybir.AluOpType
ACT = mybir.ActivationFunctionType
AXX = mybir.AxisListType.X

B, L, D = 8, 256, 128
NB = 2
T = NB * L
PAIRS = B // NB
TT = T // 128
E, FT = 8, 4
UNITS = E * FT
N = 16
KC = 4
J1 = 2
C1 = J1 * N
PC = 2
RING = 4
PIECES = 2
CWR = 2
AHEAD = 2
DOWN_LAG = 2
GROUP = 4
LAG = 3
GATE_TEMP = 0.1
EPS = 1e-5
BIG = 2.0 ** 100

V0 = dict(conv=0, bconv=4, bdt=5, alog=6, gam=22, bet=23, lng=24, lnb=25, b1=26)
V0_COLS = 26 + UNITS
V1 = dict(conv=0, bconv=8, bdt=10, alog=12, dskip=44)
V1_COLS = 46

CHUNKS0 = [int(1 + 1.3 * c) for c in range(N + LAG)]
CHUNKS1 = [int(1 + 0.86 * c) for c in range(C1 + LAG)]
END1 = max(UNITS + DOWN_LAG, CHUNKS1[-1] + 1)
HEAD0 = dict(norm=1, xnT=3, xfT=5, xin=7, logits=9, z=13, onehot=15, dt=17, b=19, c=21, ln=23)
HEAD1 = dict(norm=1, xnT=3, x0=5, x1=7, logits=9, z0=12, z1=13, cwT=16, b0=17, cd0=18, dt0=20, b1=22, cd1=23, dt1=24, ln=26)
TAIL0 = dict(y=27, norm=28, ynT=29, s=31)

SETUP_DVE = 12
DVE0, DVE1, POOL0, POOL1, ACT0, ACT1 = 19, 20, 8, 16, 1, 2


def now(slots, u):
    if isinstance(slots, dict):
        return [name for name, at in slots.items() if at == u]
    return [c for c, at in enumerate(slots) if at == u]


class Signal:

    def __init__(self, sem, per0, per1, start):
        self.sem, self.per0, self.per1, self.start = sem, per0, per1, start

    def at0(self, i, n):
        return i * self.per0 + n + self.start

    def at1(self, i, n):
        return i * self.per1 + n + self.start + PAIRS * self.per0


class Chain:

    def __init__(self, eng, sem):
        self.eng, self.sem, self.base, self.i, self.per, self.n = eng, sem, 0, 0, 0, 0

    def turn(self, i, per):
        self.base, self.i, self.per, self.n = self.base + self.n, i, per, 0

    def turned(self, turns):
        assert self.n == self.per, (self.n, self.per)
        self.base, self.i, self.n = self.base + turns * self.per, 0, 0
        self.per = 0

    def __call__(self, ins):
        self.n += 1
        ins.then_inc(self.sem, 1)
        self.eng.wait_ge(self.sem, self.i * self.per + self.base + self.n)


def build(nc, x, out, x1, crow, cwrow, w):
    ctx = ExitStack()
    with ctx:
        sb = lambda name, shape, dt=F32: ctx.enter_context(nc.sbuf_tensor(name, shape, dt))
        def tiles(ap):
            return ap.rearrange("p (k d) -> p k d", k=TT)

        signals = []

        def sig(name, per0=1, per1=1, start=1):
            signals.append(Signal(ctx.enter_context(nc.semaphore(name)), per0, per1, start))
            return signals[-1]

        bank = [ctx.enter_context(nc.psum_tensor(f"bank{k}", [128, 512], F32)) for k in range(8)]
        B_BANK, Y_BANK, OUT_BANK, HID_BANK, UP_BANK, HEAD_BANK = 0, 1, 2, 3, 5, 7

        ident = sb("ident", [128, 128])
        sel = sb("sel", [96, N * 128], BF16)
        big = sb("big", [E, E], BF16)
        vec0, vec1 = sb("vec0", [128, V0_COLS]), sb("vec1", [128, V1_COLS])
        iota = sb("iota", [128, TT, E])
        brb, bout, b2 = sb("brb", [128, E]), sb("bout", [128, D]), sb("b2", [E, D])
        w_in0, w_dt0, w_b0, w_c0 = sb("w_in0", [128, 2 * D]), sb("w_dt0", [128, D]), sb("w_b0", [128, 96]), sb("w_c0", [128, N])
        w_out0, w_r0 = sb("w_out0", [128, D]), sb("w_r0", [128, E])
        w_in1, w_b1, w_cd1 = sb("w_in1", [128, 2 * J1 * 128]), sb("w_b1", [128, J1 * 96]), sb("w_cd1", [128, J1 * 64])
        w_dt1, w_out1, w_r1 = sb("w_dt1", [64, J1 * 128]), sb("w_out1", [128, J1, D]), sb("w_r1", [128, 2 * E])
        wh = sb("wh", [128, E, FT * 128], F32R)
        wl = sb("wl", [128, E, FT * 128], F32R)
        wd = sb("wd", [128, UNITS, D])
        wu = sb("wu", [128, E, FT * 128])
        xw = sb("xw", [128, 2, T])
        stage = xw
        negA0, negA1 = sb("negA0", [128, N]), sb("negA1", [128, J1 * N])
        half, ones, halves = sb("half", [128, TT]), sb("ones", [128, 1]), sb("halves", [128, 1])
        idle = sb("idle", [128, 1])

        xt, xn = sb("xt", [128, TT, D]), sb("xn", [128, TT, D])
        XNT = sb("XNT", [128, T])
        stats, mv = sb("stats", [128, TT, 6]), sb("mv", [128, TT, 2])
        veps, rstd = sb("veps", [128, TT]), sb("rstd", [128, TT])
        veps_t, rstd_t = sb("veps_t", [128, TT]), sb("rstd_t", [128, TT])
        xpad = sb("xpad", [128, J1, NB, KC - 1 + L])
        xs = sb("xs", [128, J1, T])
        sz = sb("sz", [128, J1, T])
        lg, lexp = sb("lg", [128, 2 * TT, E]), sb("lexp", [128, 2 * TT, E])
        lmax, lsum, linv = sb("lmax", [128, 2 * TT]), sb("lsum", [128, 2 * TT]), sb("linv", [128, 2 * TT])
        eq, onehot, cw = sb("eq", [128, TT, E]), sb("onehot", [128, TT, E]), sb("cw", [128, TT, E])
        ohT = sb("ohT", [E, T])
        cwT = ohT
        sp_e, sp_u = sb("sp_e", [128, J1, T]), sb("sp_u", [128, J1, T])
        sp_l, sp_x = sb("sp_l", [128, J1, T]), sb("sp_x", [128, J1, T])
        conv, th = sp_l, sp_u[:, 0, :]
        Bnew, Bmid = sb("Bnew", [96, J1, T], BF16), sb("Bmid", [96, T], BF16)
        Bres = xn[0:96, :, :].rearrange("p k d -> p (k d)")
        cd = sb("cd", [64, J1, T])

        XH, XL, XR = sb("XH", [128, T], F32R), sb("XL", [128, T], F32R), sb("XR", [128, T])
        ohm = sb("ohm", [E, T], BF16)
        hp = sb("hp", [128, TT])
        delta, dx = sb("delta", [128, J1, T]), sb("dx", [128, J1, T])
        Bst = sb("Bst", [96, J1, T], BF16)
        Cb = sb("Cb", [128, PIECES, PC, T])
        decay, state = sb("decay", [128, RING, T]), sb("state", [128, RING, T])
        drive, product, addend = sb("drive", [128, 2, T]), sb("product", [128, 2, T]), sb("addend", [128, T])
        xd, szm = sb("xd", [128, J1, T]), sb("szm", [128, J1, T])
        cwb = sb("cwb", [128, CWR, T])
        sg, gg, hid = sb("sg", [128, 2, T]), sb("gg", [128, 2, T]), sb("hid", [128, 2, T])
        xf, XFT, ohF = tiles(sg[:, 0, :]), sg[:, 1, :], gg[0:E, 0, :]

        yT, ynT = xd, xd[:, 1, :]
        xr, so = sb("xr", [128, TT, D]), sb("so", [128, TT, D])
        yn = so
        yfT = sb("yfT", [128, T])
        g = tg = tiles(yfT[:, :])

        consts_in, late_in = sig("consts_in"), sig("late_in")
        stage_in, wh_ready, wl_ready = sig("stage_in"), sig("wh_ready"), sig("wl_ready")
        wd_in = [sig(f"wd_in{e}") for e in range(E)]
        wu_in = sig("wu_in")
        setup_act, setup_dve = sig("setup_act"), sig("setup_dve")
        dve_step, pool_step, act_step = (ctx.enter_context(nc.semaphore(n)) for n in ("dve_step", "pool_step", "act_step"))
        x_in, r_in, x_out = sig("x_in", 16, 16), sig("r_in", 16, 16), sig("x_out", 16, 16)
        rows_out = sig("rows_out", 16, 16 * J1)
        piece_in = [sig(f"piece_in{k}", 16 * (N // PC // PIECES), 32 * (C1 // PC // PIECES)) for k in range(PIECES)]
        cw_out = sig("cw_out", 0, 16)
        cw_in = [sig(f"cw_in{k}", 0, 16 * (E // CWR)) for k in range(CWR)]
        var_ready, rstd_ready = sig("var_ready", 2, 1), sig("rstd_ready", 2, 1)
        xn_ready, xf_ready = sig("xn_ready"), sig("xf_ready", 1, 0)
        head_ps = sig("head_ps", 9, 13)
        head_read = sig("head_read", 9, 13)
        conv_ready, th_ready, xs_ready = sig("conv_ready", 1, J1), sig("th_ready", 1, J1), sig("xs_ready", 1, J1)
        tz_ready, sz_ready = sig("tz_ready", 0, J1), sig("sz_ready", 0, J1)
        tap_ready = sig("tap_ready", 1, J1)
        lmax_sub, choice_ready = sig("lmax_sub"), sig("choice_ready")
        bnew_ready = sig("bnew_ready", 1, J1)
        sp_e_ready, sp_u_ready, sp_c_ready, sp_x_ready = (sig(n, 1, J1) for n in ("sp_e_ready", "sp_u_ready", "sp_c_ready", "sp_x_ready"))
        sp_l_ready, ohF_ready = sig("sp_l_ready"), sig("ohF_ready", 1, 0)
        xh_ready, xl_ready, xr_ready, ohm_ready = sig("xh_ready"), sig("xl_ready"), sig("xr_ready"), sig("ohm_ready", 1, 0)
        delta_ready, dx_ready, bst_ready = sig("delta_ready"), sig("dx_ready"), sig("bst_ready")
        kept_ready, hp_ready = sig("kept_ready", 0, 1), sig("hp_ready", 1, 0)
        b_ps, drive_ready, decay_ready = sig("b_ps", N, C1), sig("drive_ready", N, C1), sig("decay_ready", N, C1)
        state_ready, state_used = sig("state_ready", N, C1), sig("state_used", N, C1)
        group_ready, summed = sig("group_ready", N // GROUP, C1 // GROUP), sig("summed", N // GROUP, C1 // GROUP)
        hid_ps, hid_ready, down_done = sig("hid_ps", UNITS, UNITS), sig("hid_ready", UNITS, UNITS, AHEAD), sig("down_done", UNITS, UNITS, AHEAD)
        xw_ready, tanh_ready, gg_ready, up_ps = sig("xw_ready", 0, E), sig("tanh_ready", 0, UNITS), sig("gg_ready", 0, UNITS, AHEAD), sig("up_ps", 0, UNITS)
        mix_ps, yfT_ready, yf_ps, tg_ready, g_ready = sig("mix_ps", 1, 0), sig("yfT_ready"), sig("yf_ps"), sig("tg_ready"), sig("g_ready")
        yT_ready, y_ps, yn_ready, ynT_ps, ynT_ready = sig("yT_ready", 1, J1), sig("y_ps", 1, 0), sig("yn_ready", 1, 0), sig("ynT_ps", 1, 0), sig("ynT_ready", 1, 0)
        tvar_ready, trstd_ready = sig("tvar_ready", 1, 0), sig("trstd_ready", 1, 0)
        yz_ready = sig("yz_ready", 0, J1)
        s_ps, s_read, out_ready = sig("s_ps"), sig("s_read"), sig("out_ready")

        block = ctx.enter_context(nc.Block())

        def by_batch(ap):
            return ap.rearrange("p (b l) -> p b l", b=NB)

        def over_e(ap):
            return ap.rearrange("p (k a) -> p k a", a=1).to_broadcast((128, ap.shape[1], E))

        def col0(name, k=0):
            return vec0[:, V0[name] + k:V0[name] + k + 1]

        def col1(name, k=0):
            return vec1[:, V1[name] + k:V1[name] + k + 1]

        CONSTS_FIRST = ("ident", "vec0", "w_in0", "w_r0", "br0", "iota", "w_dt0", "w_b0", "w_c0", "vec1")
        LATE = ("sel", "big", "b2", "b_out0", "w_out0", "w_in1", "w_r1", "w_b1", "w_cd1", "w_dt1", "w_out1")

        @block.sync
        def _(sp):
            for s in signals:
                sp.sem_inc(s.sem, s.start)
            rows = lambda ap, i: ap[i * T:i * T + T, :].rearrange("(k p) d -> p k d", p=128)

            def load_const(name, done):
                dst = {"ident": ident, "vec0": vec0, "w_in0": w_in0, "w_r0": w_r0, "br0": brb, "iota": iota, "w_dt0": w_dt0,
                       "w_b0": w_b0, "w_c0": w_c0, "vec1": vec1, "sel": sel, "big": big, "b2": b2, "b_out0": bout,
                       "w_out0": w_out0, "w_in1": w_in1, "w_r1": w_r1, "w_b1": w_b1, "w_cd1": w_cd1, "w_dt1": w_dt1,
                       "w_out1": w_out1}[name]
                src = w[name]
                if name in ("br0", "b_out0"):
                    src = src.to_broadcast((128, src.shape[1]))
                if name == "w_out1":
                    src = src.rearrange("(j p) d -> p j d", p=128)
                to = dst[:, :, :] if name in ("iota", "w_out1") else dst[:, :]
                sp.dma_start(to, src).then_inc(done.sem, 16)

            def load_gate(e):
                if e >= 2:
                    sp.wait_ge(wl_ready.sem, wl_ready.at0(0, E + e - 1))
                sp.dma_start(stage[:, e % 2, :], w["Wg"][e]).then_inc(stage_in.sem, 16)
                sp.wait_ge(stage_in.sem, stage_in.at0(0, 16 * (E + e + 1)))

            def load_wd(e, src):
                sp.dma_start(wd[:, FT * e:FT * e + FT, :], src.rearrange("(f p) d -> p f d", p=128)).then_inc(wd_in[e].sem, 16)

            def load_x(j, layer):
                at = (xn_ready.at0 if layer == 0 else xn_ready.at1)(j, 0)
                sp.wait_ge(xn_ready.sem, at)
                if layer == 1 and j == 0:
                    sp.wait_ge(x_out.sem, x_out.at0(0, 16))
                elif layer == 1:
                    sp.wait_ge(x_out.sem, x_out.at0(PAIRS, 0))
                sp.dma_start(xt[:, :, :], rows(x if layer == 0 else x1, j)).then_inc(x_in.sem, 16)

            def load_piece0(j, p):
                if j > 0 or p >= PIECES:
                    sp.wait_ge(state_used.sem, state_used.at0(j, PC * (p - PIECES + 1)))
                src = crow[j % 2, 0, PC * p:PC * p + PC, :].rearrange("(a r) t -> a r t", a=1)
                sp.dma_start(Cb[:, p % PIECES, :, :], src.to_broadcast((128, PC, T))).then_inc(piece_in[p % PIECES].sem, 16)

            def load_piece1(j, p):
                sp.wait_ge(state_used.sem, state_used.at1(j, PC * (p - PIECES + 1)))
                m, q = p // (N // PC), p % (N // PC)
                for h in range(2):
                    src = crow[j % 2, m, N * h + PC * q:N * h + PC * q + PC, :].rearrange("(a r) t -> a r t", a=1)
                    sp.dma_start(Cb[64 * h:64 * h + 64, p % PIECES, :, :], src.to_broadcast((64, PC, T))).then_inc(piece_in[p % PIECES].sem, 16)

            def send_rows(j, layer, m):
                sp.wait_ge(head_read.sem, head_read.at0(j, 9) if layer == 0 else head_read.at1(j, 9 + 3 * m))
                count = N if layer == 0 else 2 * N
                sp.dma_start(crow[j % 2, m, 0:count, :], cd[0:count, m, :]).then_inc(rows_out.sem, 16)
                out_at = rows_out.at0 if layer == 0 else rows_out.at1
                sp.wait_ge(rows_out.sem, out_at(j, 16 * (m + 1)))

            def load_cw(j, e):
                if j > 0 or e >= CWR:
                    sp.wait_ge(xw_ready.sem, xw_ready.at1(j, e - CWR + 1))
                src = cwrow[j % 2, e:e + 1, :].to_broadcast((128, T))
                sp.dma_start(cwb[:, e % CWR, :], src).then_inc(cw_in[e % CWR].sem, 16)

            def send_cw(j):
                sp.wait_ge(head_read.sem, head_read.at1(j, 7))
                sp.dma_start(cwrow[j % 2, :, :], cwT[:, :]).then_inc(cw_out.sem, 16)
                sp.wait_ge(cw_out.sem, cw_out.at1(j, 16))

            def send_out(i, layer):
                at = out_ready.at0 if layer == 0 else out_ready.at1
                sp.wait_ge(out_ready.sem, at(i, 1))
                sp.dma_start(rows(x1 if layer == 0 else out, i), so[:, :, :]).then_inc(x_out.sem, 16)

            def load_residual(i, layer):
                at = out_ready.at0 if layer == 0 else out_ready.at1
                sp.wait_ge(out_ready.sem, at(i, 0))
                sp.dma_start(xr[:, :, :], rows(x if layer == 0 else x1, i)).then_inc(r_in.sem, 16)

            load_x(0, 0)
            for name in CONSTS_FIRST:
                load_const(name, consts_in)
            for e in range(E):
                sp.dma_start(wu[:, e, :], w["W1"][e]).then_inc(stage_in.sem, 16)
            for name in LATE:
                load_const(name, late_in)
            for e in range(E):
                load_wd(e, w["W2"][e])
            send_rows(0, 0, 0)
            for p in range(PIECES):
                load_piece0(0, p)
            sp.wait_ge(wl_ready.sem, wl_ready.at0(0, E))
            for e in range(E):
                sp.dma_start(wu[:, e, :], w["Wu"][e]).then_inc(wu_in.sem, 16)
            for i in range(PAIRS):
                last = i == PAIRS - 1
                load_residual(i, 0)
                for u in range(UNITS):
                    for step in now(HEAD1 if last else HEAD0, u):
                        if step == "norm":
                            load_x(0 if last else i + 1, int(last))
                        if step == "c":
                            send_rows(i + 1, 0, 0)
                        if step == "cwT":
                            send_cw(0)
                            for e in range(CWR):
                                load_cw(0, e)
                        if step in ("cd0", "cd1"):
                            send_rows(0, 1, int(step[2]))
                    for c in now(CHUNKS0, u):
                        p = c // PC + PIECES - 1
                        if c % PC == 0 and PIECES <= p < N // PC:
                            load_piece0(i, p)
                    if last and u % FT == FT - 1:
                        e = u // FT
                        sp.wait_ge(hid_ps.sem, hid_ps.at0(i, u + 1))
                        load_gate(e)
                        if e >= 1:
                            sp.wait_ge(down_done.sem, down_done.at0(i, FT * e))
                            load_wd(e - 1, w["Wd"][e - 1])
                for p in range(PIECES):
                    if last:
                        load_piece1(0, p)
                    else:
                        load_piece0(i + 1, p)
                send_out(i, 0)
            sp.wait_ge(down_done.sem, down_done.at0(PAIRS, 0))
            load_wd(E - 1, w["Wd"][E - 1])
            for i in range(PAIRS):
                last = i == PAIRS - 1
                sp.wait_ge(x_out.sem, x_out.at0(PAIRS, 0))
                load_residual(i, 1)
                for u in range(UNITS):
                    for step in ([] if last else now(HEAD1, u)):
                        if step == "norm":
                            load_x(i + 1, 1)
                        if step == "cwT":
                            send_cw(i + 1)
                        if step in ("cd0", "cd1"):
                            send_rows(i + 1, 1, int(step[2]))
                    for c in now(CHUNKS1, u):
                        p = c // PC + PIECES - 1
                        if c % PC == 0 and PIECES <= p < C1 // PC:
                            load_piece1(i, p)
                    if u % FT == 0 and u // FT + CWR < E:
                        load_cw(i, u // FT + CWR)
                if not last:
                    for e in range(CWR):
                        load_cw(i + 1, e)
                    for p in range(PIECES):
                        load_piece1(i + 1, p)
                send_out(i, 1)
            sp.wait_ge(x_out.sem, x_out.at1(PAIRS, 0))

        @block.vector
        def _(dve):
            v = nc.vector
            step = Chain(dve, dve_step)

            def split_low(k):
                e = k % E
                src = wu[:, e, :] if k < E else stage[:, e % 2, :]
                dve.wait_ge(wh_ready.sem, wh_ready.at0(0, k + 1))
                v.tensor_tensor(wl[:, e, :], src, wh[:, e, :].bitcast(F32), ALU.subtract).then_inc(wl_ready.sem, 1)

            def normalise(dst, src, var, var_sig, root, root_wait, ready):
                for k in range(TT):
                    last = v.bn_stats(stats[:, k, :], src[:, k, :])
                step(last)
                v.memset(idle[:, :], 0.0)
                for k in range(TT):
                    last = v.bn_aggr(mv[:, k, :], stats[:, k, :])
                step(last)
                v.tensor_scalar(var[:, :], mv[:, :, 1], EPS, None, ALU.add).then_inc(var_sig.sem, 1)
                dve.wait_ge(*root_wait)
                for k in range(TT):
                    last = v.tensor_scalar(dst[:, k, :], src[:, k, :], mv[:, k, 0:1], root[:, k:k + 1], ALU.subtract, ALU.mult)
                last.then_inc(ready.sem, 1)

            def convolve(m, col, taps, ready):
                cv = by_batch(conv[:, m, :])
                for k in taps:
                    ins = v.scalar_tensor_tensor(out=cv, in0=xpad[:, m, :, k:k + L], scalar=col("conv", KC * m + k),
                                                 in1=cv, op0=ALU.mult, op1=ALU.add)
                    if k < KC - 1:
                        step(ins)
                    else:
                        ins.then_inc(ready.sem, 1)

            def split_b(m):
                b = bank[HEAD_BANK][0:96, :]
                step(v.tensor_copy(Bnew[:, m, :], b))
                step(v.tensor_tensor(Bres[:, :], b, Bnew[:, m, :], ALU.subtract))
                v.tensor_copy(Bnew[32:64, m, :], Bres[32:64, :]).then_inc(head_read.sem, 1)
                step(v.tensor_copy(Bmid[64:96, :], Bres[64:96, :]))
                v.tensor_tensor(Bnew[64:96, m, :], Bres[64:96, :], Bmid[64:96, :], ALU.subtract).then_inc(bnew_ready.sem, 1)

            def log_rest(m, at_e, at_u, at_l):
                dve.wait_ge(sp_l_ready.sem, at_l)
                dve.wait_ge(sp_e_ready.sem, at_e)
                v.tensor_scalar(sp_u[:, m, :], sp_e[:, m, :], 1.0, None, ALU.add).then_inc(sp_u_ready.sem, 1)
                dve.wait_ge(sp_u_ready.sem, at_u)
                v.scalar_tensor_tensor(out=sp_e[:, m, :], in0=sp_u[:, m, :], scalar=1.0, in1=sp_e[:, m, :],
                                       op0=ALU.subtract, op1=ALU.subtract).then_inc(sp_c_ready.sem, 1)

            def head0(name, j):
                if name == "norm":
                    dve.wait_ge(x_in.sem, x_in.at0(j, 16))
                    dve.wait_ge(head_ps.sem, head_ps.at0(j, 0))
                    normalise(xn, xt, veps, var_ready, rstd, (rstd_ready.sem, rstd_ready.at0(j, 1)), xn_ready)
                    dve.wait_ge(xn_ready.sem, xn_ready.at0(j, 1))
                    normalise(xf, xn, veps, var_ready, rstd, (rstd_ready.sem, rstd_ready.at0(j, 2)), xf_ready)
                if name == "xin":
                    dve.wait_ge(tap_ready.sem, tap_ready.at0(j, 1))
                    convolve(0, col0, range(1, KC), conv_ready)
                if name == "logits":
                    dve.wait_ge(head_ps.sem, head_ps.at0(j, 4))
                    br_all = brb[:, :].rearrange("p (a e) -> p a e", a=1).to_broadcast((128, TT, E))
                    step(v.tensor_tensor(lg[:, 0:TT, :], bank[HEAD_BANK][:, 0:TT * E].rearrange("p (k e) -> p k e", k=TT), br_all, ALU.add))
                    step(v.tensor_reduce(lmax[:, 0:TT], lg[:, 0:TT, :], AXX, ALU.max))
                    v.tensor_tensor(lg[:, 0:TT, :], lg[:, 0:TT, :], over_e(lmax[:, 0:TT]), ALU.subtract).then_inc(lmax_sub.sem, 1)
                    dve.wait_ge(lmax_sub.sem, lmax_sub.at0(j, 1))
                    step(v.tensor_scalar(eq[:, :, :], lg[:, 0:TT, :], 0.0, -float(E), ALU.is_equal, ALU.mult))
                    step(v.tensor_tensor(eq[:, :, :], eq[:, :, :], iota[:, :, :], ALU.add))
                    step(v.tensor_reduce(lmax[:, 0:TT], eq[:, :, :], AXX, ALU.min))
                    v.tensor_tensor(onehot[:, :, :], eq[:, :, :], over_e(lmax[:, 0:TT]), ALU.is_equal).then_inc(choice_ready.sem, 1)
                    dve.wait_ge(head_read.sem, head_read.at0(j, 4))
                    step(v.tensor_reduce(lsum[:, 0:TT], lexp[:, 0:TT, :], AXX, ALU.add))
                    step(v.reciprocal(linv[:, 0:TT], lsum[:, 0:TT]))
                    dve.wait_ge(th_ready.sem, th_ready.at0(j, 1))
                    v.scalar_tensor_tensor(out=xs[:, 0, :], in0=th[:, :], scalar=1.0, in1=conv[:, 0, :],
                                           op0=ALU.add, op1=ALU.mult).then_inc(xs_ready.sem, 1)
                if name == "z":
                    dve.wait_ge(head_ps.sem, head_ps.at0(j, 5))
                    dve.wait_ge(xs_ready.sem, xs_ready.at0(j, 1))
                    v.tensor_tensor(xs[:, 1, :], xs[:, 0, :], bank[HEAD_BANK][:, :], ALU.mult).then_inc(head_read.sem, 1)
                if name == "onehot":
                    dve.wait_ge(head_ps.sem, head_ps.at0(j, 6))
                    v.tensor_copy(ohT[:, :], bank[HEAD_BANK][0:E, :]).then_inc(head_read.sem, 1)
                if name == "dt":
                    log_rest(0, sp_e_ready.at0(j, 1), sp_u_ready.at0(j, 1), sp_l_ready.at0(j, 0))
                if name == "b":
                    dve.wait_ge(head_ps.sem, head_ps.at0(j, 8))
                    split_b(0)

            def low0(i):
                dve.wait_ge(xh_ready.sem, xh_ready.at0(i, 1))
                v.tensor_tensor(XL[:, :], XFT[:, :], XH[:, :].bitcast(F32), ALU.subtract).then_inc(xl_ready.sem, 1)
                dve.wait_ge(head_read.sem, head_read.at0(i, 6))
                v.tensor_scalar(ohm[:, :], ohT[:, :], 1.0, None, ALU.subtract).then_inc(ohm_ready.sem, 1)

            def hand_over0(i):
                dve.wait_ge(sp_l_ready.sem, sp_l_ready.at0(i, 1))
                dve.wait_ge(sp_x_ready.sem, sp_x_ready.at0(i, 1))
                dve.wait_ge(decay_ready.sem, decay_ready.at0(i, 0))
                v.tensor_tensor(delta[:, 0, :], sp_x[:, 0, :], sp_l[:, 0, :], ALU.add).then_inc(delta_ready.sem, 1)
                dve.wait_ge(delta_ready.sem, delta_ready.at0(i, 1))
                dve.wait_ge(drive_ready.sem, drive_ready.at0(i, 0))
                v.tensor_tensor(dx[:, 0, :], delta[:, 0, :], xs[:, 1, :], ALU.mult).then_inc(dx_ready.sem, 1)
                dve.wait_ge(mix_ps.sem, mix_ps.at0(i, 0))
                v.tensor_copy(ohF[:, :], ohT[:, :]).then_inc(ohF_ready.sem, 1)

            def form_drive(at, c, m):
                dve.wait_ge(b_ps.sem, at(b_ps)(c + 1))
                dve.wait_ge(state_ready.sem, at(state_ready)(max(c - 1, 0)))
                v.tensor_tensor(drive[:, c % 2, :], dx[:, m, :], bank[B_BANK][:, :], ALU.mult).then_inc(drive_ready.sem, 1)

            def scan(at, c):
                dve.wait_ge(decay_ready.sem, at(decay_ready)(c + 1))
                dve.wait_ge(drive_ready.sem, at(drive_ready)(c + 1))
                dve.wait_ge(state_used.sem, at(state_used)(max(c - RING + 1, 0)))
                v.tensor_tensor_scan(state[:, c % RING, :], decay[:, c % RING, :], drive[:, c % 2, :], 0.0,
                                     ALU.mult, ALU.add).then_inc(state_ready.sem, 1)

            def main0(i, head, j):
                at = lambda s: (lambda n: s.at0(i, n))
                dve.wait_ge(dx_ready.sem, dx_ready.at0(i, 1))
                v.tensor_scalar(hp[:, :], linv[:, 0:TT], 0.5, None, ALU.mult).then_inc(hp_ready.sem, 1)
                for u in range(UNITS):
                    if j is not None and head is head1 and u % FT == FT - 1 and u // FT >= 1:
                        split_low(E + u // FT - 1)
                    for c in now(CHUNKS0, u):
                        if c < N:
                            form_drive(at, c, 0)
                        if 1 <= c <= N:
                            scan(at, c - 1)
                    for name in now(TAIL0, u):
                        if name == "y":
                            dve.wait_ge(summed.sem, summed.at0(i, N // GROUP))
                            v.tensor_tensor(yT[:, 0, :], XR[:, :], bank[Y_BANK][:, :], ALU.add).then_inc(yT_ready.sem, 1)
                        if name == "norm":
                            dve.wait_ge(y_ps.sem, y_ps.at0(i, 1))
                            dve.wait_ge(x_out.sem, x_out.at0(i, 0))
                            normalise(yn, tiles(bank[Y_BANK][:, :]), veps_t, tvar_ready, rstd_t,
                                      (trstd_ready.sem, trstd_ready.at0(i, 1)), yn_ready)
                        if name == "ynT":
                            dve.wait_ge(ynT_ps.sem, ynT_ps.at0(i, 1))
                            v.tensor_scalar(ynT, bank[UP_BANK][:, :], col0("gam"), col0("bet"), ALU.mult, ALU.add).then_inc(ynT_ready.sem, 1)
                        if name == "s":
                            dve.wait_ge(s_ps.sem, s_ps.at0(i, 1))
                            bo = bout[:, :].rearrange("p (a d) -> p a d", a=1).to_broadcast((128, TT, D))
                            v.tensor_tensor(so[:, :, :], tiles(bank[Y_BANK][:, :]), bo, ALU.add).then_inc(s_read.sem, 1)
                    if j is not None:
                        for name in now(HEAD0 if head is head0 else HEAD1, u):
                            head(name, j)

            def tail0(i):
                dve.wait_ge(tg_ready.sem, tg_ready.at0(i, 1))
                v.scalar_tensor_tensor(out=g[:, :, :], in0=tg[:, :, :], scalar=1.0, in1=tiles(bank[OUT_BANK][:, :]),
                                       op0=ALU.add, op1=ALU.mult).then_inc(g_ready.sem, 1)
                dve.wait_ge(g_ready.sem, g_ready.at0(i, 1))
                dve.wait_ge(s_read.sem, s_read.at0(i, 1))
                for k in range(TT):
                    last = v.scalar_tensor_tensor(out=so[:, k, :], in0=g[:, k, :], scalar=hp[:, k:k + 1], in1=so[:, k, :],
                                                  op0=ALU.mult, op1=ALU.mult)
                step(last)
                dve.wait_ge(r_in.sem, r_in.at0(i, 16))
                v.tensor_tensor(so[:, :, :], so[:, :, :], xr[:, :, :], ALU.add).then_inc(out_ready.sem, 1)

            def head1(name, j):
                if name == "norm":
                    dve.wait_ge(x_in.sem, x_in.at1(j, 16))
                    dve.wait_ge(head_ps.sem, head_ps.at1(j, 0))
                    normalise(xn, xt, veps, var_ready, rstd, (rstd_ready.sem, rstd_ready.at1(j, 1)), xn_ready)
                if name in ("x0", "x1"):
                    m = int(name[1])
                    dve.wait_ge(tap_ready.sem, tap_ready.at1(j, m + 1))
                    convolve(m, col1, range(1, KC), conv_ready)
                if name == "logits":
                    for m in range(J1):
                        dve.wait_ge(th_ready.sem, th_ready.at1(j, m + 1))
                        dve.wait_ge(kept_ready.sem, kept_ready.at1(j, 0))
                        v.scalar_tensor_tensor(out=xs[:, m, :], in0=th[:, :], scalar=1.0, in1=conv[:, m, :],
                                               op0=ALU.add, op1=ALU.mult).then_inc(xs_ready.sem, 1)
                    dve.wait_ge(head_ps.sem, head_ps.at1(j, 4))
                    lps = bank[HEAD_BANK][:, 0:2 * TT * E].rearrange("p (k e) -> p k e", e=E)
                    step(v.tensor_reduce(lmax[:, :], lps, AXX, ALU.max))
                    v.tensor_tensor(lg[:, :, :], lps, over_e(lmax[:, :]), ALU.subtract).then_inc(lmax_sub.sem, 1)
                if name in ("z0", "z1"):
                    m = int(name[1])
                    dve.wait_ge(tz_ready.sem, tz_ready.at1(j, m + 1))
                    v.scalar_tensor_tensor(out=sz[:, m, :], in0=sz[:, m, :], scalar=1.0, in1=bank[HEAD_BANK][:, :],
                                           op0=ALU.add, op1=ALU.mult).then_inc(head_read.sem, 1)
                if name == "z1":
                    dve.wait_ge(head_read.sem, head_read.at1(j, 4))
                    step(v.tensor_reduce(lsum[:, :], lexp[:, :, :], AXX, ALU.add))
                    step(v.reciprocal(linv[:, :], lsum[:, :]))
                    step(v.tensor_tensor(lexp[:, :, :], lexp[:, :, :], over_e(linv[:, :]), ALU.mult))
                    step(v.tensor_tensor(cw[:, :, :], lexp[:, 0:TT, :], lexp[:, TT:, :], ALU.mult))
                    step(v.tensor_reduce(lsum[:, 0:TT], cw[:, :, :], AXX, ALU.add))
                    step(v.tensor_scalar(lsum[:, 0:TT], lsum[:, 0:TT], 1e-9, 2.0, ALU.add, ALU.mult))
                    step(v.reciprocal(linv[:, 0:TT], lsum[:, 0:TT]))
                    v.tensor_tensor(cw[:, :, :], cw[:, :, :], over_e(linv[:, 0:TT]), ALU.mult).then_inc(choice_ready.sem, 1)
                if name == "cwT":
                    dve.wait_ge(head_ps.sem, head_ps.at1(j, 7))
                    dve.wait_ge(cw_out.sem, cw_out.at1(j, 0))
                    v.tensor_copy(cwT[:, :], bank[HEAD_BANK][0:E, :]).then_inc(head_read.sem, 1)
                if name in ("b0", "b1"):
                    m = int(name[1])
                    dve.wait_ge(head_ps.sem, head_ps.at1(j, 8 + 3 * m))
                    split_b(m)
                if name in ("dt0", "dt1"):
                    m = int(name[2])
                    log_rest(m, sp_e_ready.at1(j, m + 1), sp_u_ready.at1(j, m + 1), sp_l_ready.at1(j, 0))

            def low1(i):
                dve.wait_ge(xh_ready.sem, xh_ready.at1(i, 1))
                v.tensor_tensor(XL[:, :], XNT[:, :], XH[:, :].bitcast(F32), ALU.subtract).then_inc(xl_ready.sem, 1)

            def hand_over1(i):
                dve.wait_ge(sp_l_ready.sem, sp_l_ready.at1(i, 1))
                dve.wait_ge(sp_x_ready.sem, sp_x_ready.at1(i, J1))
                dve.wait_ge(decay_ready.sem, decay_ready.at1(i, 0))
                v.tensor_tensor(delta[:, :, :], sp_x[:, :, :], sp_l[:, :, :], ALU.add).then_inc(delta_ready.sem, 1)
                dve.wait_ge(delta_ready.sem, delta_ready.at1(i, 1))
                dve.wait_ge(drive_ready.sem, drive_ready.at1(i, 0))
                v.tensor_tensor(dx[:, :, :], delta[:, :, :], xs[:, :, :], ALU.mult).then_inc(dx_ready.sem, 1)

            def main1(i, head, j, low):
                at = lambda s: (lambda n: s.at1(i, n))
                dve.wait_ge(dx_ready.sem, dx_ready.at1(i, 1))

                def hidden(u):
                    dve.wait_ge(up_ps.sem, up_ps.at1(i, u + 1))
                    dve.wait_ge(gg_ready.sem, gg_ready.at1(i, u + 1))
                    dve.wait_ge(down_done.sem, down_done.at1(i, max(u - 1, 0)))
                    v.tensor_tensor(hid[:, u % 2, :], gg[:, u % 2, :], bank[UP_BANK + u % 2][:, :], ALU.mult).then_inc(hid_ready.sem, 1)

                for u in range(END1):
                    for c in now(CHUNKS1, u)[:1]:
                        if c < C1:
                            form_drive(at, c, c // N)
                    if u < UNITS:
                        dve.wait_ge(tanh_ready.sem, tanh_ready.at1(i, u + 1))
                        dve.wait_ge(hid_ready.sem, hid_ready.at1(i, max(u - 1, 0)))
                        v.scalar_tensor_tensor(out=gg[:, u % 2, :], in0=sg[:, u % 2, :], scalar=1.0, in1=bank[HID_BANK + u % 2][:, :],
                                               op0=ALU.add, op1=ALU.mult).then_inc(gg_ready.sem, 1)
                    for k, c in enumerate(now(CHUNKS1, u)):
                        if k > 0 and c < C1:
                            form_drive(at, c, c // N)
                        if 1 <= c <= C1:
                            scan(at, c - 1)
                    if low and u == UNITS:
                        low()
                    if 1 <= u <= UNITS:
                        hidden(u - 1)
                    for c in now(CHUNKS1, u):
                        if c in (N + LAG - 1, C1 + LAG - 1):
                            m = c // N - 1
                            dve.wait_ge(summed.sem, summed.at1(i, (m + 1) * N // GROUP))
                            dve.wait_ge(kept_ready.sem, kept_ready.at1(i, 1))
                            v.tensor_tensor(yT[:, m, :], xd[:, m, :], bank[Y_BANK][:, :], ALU.add).then_inc(yT_ready.sem, 1)
                            dve.wait_ge(yT_ready.sem, yT_ready.at1(i, m + 1))
                            v.tensor_tensor(yT[:, m, :], yT[:, m, :], szm[:, m, :], ALU.mult).then_inc(yz_ready.sem, 1)
                    if j is not None and u < UNITS:
                        for name in now(HEAD1, u):
                            head(name, j)

            def tail1(i):
                dve.wait_ge(tg_ready.sem, tg_ready.at1(i, 1))
                v.scalar_tensor_tensor(out=g[:, :, :], in0=tg[:, :, :], scalar=1.0, in1=tiles(bank[OUT_BANK][:, :]),
                                       op0=ALU.add, op1=ALU.mult).then_inc(g_ready.sem, 1)
                dve.wait_ge(g_ready.sem, g_ready.at1(i, 1))
                dve.wait_ge(s_ps.sem, s_ps.at1(i, 1))
                dve.wait_ge(x_out.sem, x_out.at1(i, 0))
                v.tensor_tensor(so[:, :, :], g[:, :, :], tiles(bank[Y_BANK][:, :]), ALU.mult).then_inc(s_read.sem, 1)
                dve.wait_ge(s_read.sem, s_read.at1(i, 1))
                dve.wait_ge(r_in.sem, r_in.at1(i, 16))
                v.scalar_tensor_tensor(out=so[:, :, :], in0=so[:, :, :], scalar=0.5, in1=xr[:, :, :],
                                       op0=ALU.mult, op1=ALU.add).then_inc(out_ready.sem, 1)

            v.memset(xpad[:, :, :, 0:KC - 1].rearrange("p j b l -> p (j b) l"), 0.0).then_inc(setup_dve.sem, 1)
            for k in range(RING):
                v.memset(by_batch(decay[:, k, :])[:, :, 0:1], 0.0).then_inc(setup_dve.sem, 1)
            v.memset(half[:, :], -0.5).then_inc(setup_dve.sem, 1)
            v.memset(ones[:, :], 1.0).then_inc(setup_dve.sem, 1)
            v.memset(halves[:, :], 0.5).then_inc(setup_dve.sem, 1)
            dve.wait_ge(setup_act.sem, setup_act.at0(0, 1))
            v.tensor_scalar(negA0[:, :], negA0[:, :], -1.0, None, ALU.mult).then_inc(setup_dve.sem, 1)
            v.tensor_scalar(negA1[:, :], negA1[:, :], -1.0, None, ALU.mult).then_inc(setup_dve.sem, 1)
            v.tensor_scalar(vec0[:, 0:KC + 1], vec0[:, 0:KC + 1], 0.5, None, ALU.mult).then_inc(setup_dve.sem, 1)
            v.tensor_scalar(vec1[:, 0:J1 * (KC + 1)], vec1[:, 0:J1 * (KC + 1)], 0.5, None, ALU.mult).then_inc(setup_dve.sem, 1)
            dve.wait_ge(setup_dve.sem, setup_dve.at0(0, SETUP_DVE))
            for name in HEAD0:
                head0(name, 0)
            for e in range(E):
                split_low(e)
            low0(0)
            hand_over0(0)
            with dve.Fori(0, PAIRS - 1) as i:
                step.turn(i, DVE0)
                main0(i, head0, i + 1)
                low0(i + 1)
                hand_over0(i + 1)
                tail0(i)
            step.turned(PAIRS - 1)
            main0(PAIRS - 1, head1, 0)
            low1(0)
            hand_over1(0)
            tail0(PAIRS - 1)
            split_low(2 * E - 1)
            with dve.Fori(0, PAIRS - 1) as i:
                step.turn(i, DVE1)
                main1(i, head1, i + 1, lambda: low1(i + 1))
                hand_over1(i + 1)
                tail1(i)
            step.turned(PAIRS - 1)
            main1(PAIRS - 1, None, None, None)
            tail1(PAIRS - 1)

        @block.gpsimd
        def _(pool):
            p = nc.gpsimd
            step = Chain(pool, pool_step)
            wide = lambda col: col.to_broadcast((128, T))

            def root(var, out_, var_at, sig_var, done):
                pool.wait_ge(sig_var.sem, var_at)
                p.tensor_tensor(out_[:, :], var[:, :], half[:, :], ALU.pow).then_inc(done.sem, 1)

            def log_less(m, at_c):
                pool.wait_ge(sp_c_ready.sem, at_c)
                p.tensor_tensor(sp_x[:, m, :], sp_x[:, m, :], sp_e[:, m, :], ALU.subtract).then_inc(sp_x_ready.sem, 1)

            def head0(name, j):
                if name == "norm":
                    root(veps, rstd, var_ready.at0(j, 1), var_ready, rstd_ready)
                    root(veps, rstd, var_ready.at0(j, 2), var_ready, rstd_ready)
                if name == "dt":
                    log_less(0, sp_c_ready.at0(j, 1))

            def head1(name, j):
                if name == "norm":
                    root(veps, rstd, var_ready.at1(j, 1), var_ready, rstd_ready)
                if name in ("dt0", "dt1"):
                    m = int(name[2])
                    log_less(m, sp_c_ready.at1(j, m + 1))

            def multiply(at, c, per_piece, pieces):
                pool.wait_ge(state_ready.sem, at(state_ready)(c + 1))
                if c % PC == 0:
                    k = c // PC
                    pool.wait_ge(piece_in[k % PIECES].sem, at(piece_in[k % PIECES])(per_piece * (k // PIECES + 1)))
                q = c // GROUP
                cs = Cb[:, c // PC % PIECES, c % PC, :]
                if c % GROUP == 0:
                    pool.wait_ge(summed.sem, at(summed)(max(q - 1, 0)))
                    ins = p.tensor_tensor(product[:, q % 2, :], state[:, c % RING, :], cs, ALU.mult)
                else:
                    pool.wait_ge(group_ready.sem, at(group_ready)(q))
                    ins = p.tensor_tensor(addend[:, :], state[:, c % RING, :], cs, ALU.mult)
                ins.then_inc(state_used.sem, 1)
                if c % GROUP:
                    pool.wait_ge(state_used.sem, at(state_used)(c + 1))
                    ins = p.tensor_tensor(product[:, q % 2, :], product[:, q % 2, :], addend[:, :], ALU.add)
                    if c % GROUP == GROUP - 1:
                        ins.then_inc(group_ready.sem, 1)
                    else:
                        step(ins)

            def main0(i, head, j):
                at = lambda s: (lambda n: s.at0(i, n))
                for u in range(UNITS):
                    for c in now(CHUNKS0, u):
                        if 1 <= c <= N:
                            multiply(at, c - 1, 16, N // PC)
                    if u == TAIL0["norm"]:
                        root(veps_t, rstd_t, tvar_ready.at0(i, 1), tvar_ready, trstd_ready)
                    if j is not None:
                        for name in now(HEAD0 if head is head0 else HEAD1, u):
                            head(name, j)

            def weigh_tokens(i, e):
                pool.wait_ge(cw_in[e % CWR].sem, cw_in[e % CWR].at1(i, 16 * (e // CWR + 1)))
                pool.wait_ge(up_ps.sem, up_ps.at1(i, max(FT * (e - 1), 0)))
                p.tensor_tensor(xw[:, e % 2, :], XR[:, :], cwb[:, e % CWR, :], ALU.mult).then_inc(xw_ready.sem, 1)

            def main1(i, head, j):
                at = lambda s: (lambda n: s.at1(i, n))
                pool.wait_ge(xr_ready.sem, xr_ready.at1(i, 1))
                pool.wait_ge(wl_ready.sem, wl_ready.at0(0, 2 * E))
                weigh_tokens(i, 0)
                weigh_tokens(i, 1)
                for u in range(END1):
                    for c in now(CHUNKS1, u):
                        if 1 <= c <= C1:
                            multiply(at, c - 1, 32, C1 // PC)
                    if u % FT == 1 and 1 <= u // FT < E - 1:
                        weigh_tokens(i, u // FT + 1)
                    if j is not None and u < UNITS:
                        for name in now(HEAD1, u):
                            head(name, j)

            pool.wait_ge(setup_dve.sem, setup_dve.at0(0, SETUP_DVE))
            for name in HEAD0:
                head0(name, 0)
            with pool.Fori(0, PAIRS - 1) as i:
                step.turn(i, POOL0)
                main0(i, head0, i + 1)
            step.turned(PAIRS - 1)
            main0(PAIRS - 1, head1, 0)
            with pool.Fori(0, PAIRS - 1) as i:
                step.turn(i, POOL1)
                main1(i, head1, i + 1)
            step.turned(PAIRS - 1)
            main1(PAIRS - 1, None, None)

        @block.scalar
        def _(act):
            a = nc.scalar
            step = Chain(act, act_step)
            hb = bank[HEAD_BANK]

            def split_high(k):
                e = k % E
                act.wait_ge(stage_in.sem, stage_in.at0(0, 16 * max(k + 1, E)))
                a.activation(wh[:, e, :], wu[:, e, :] if k < E else stage[:, e % 2, :], ACT.Copy).then_inc(wh_ready.sem, 1)

            def first_tap(m, col, at_pad, at_delta):
                act.wait_ge(head_read.sem, at_pad)
                act.wait_ge(delta_ready.sem, at_delta)
                a.activation(by_batch(conv[:, m, :]), xpad[:, m, :, 0:L], ACT.Identity, bias=col("bconv", m),
                             scale=col("conv", KC * m)).then_inc(tap_ready.sem, 1)

            def softplus(m, bdt, at_x, at_delta):
                act.wait_ge(sp_x_ready.sem, at_x)
                act.wait_ge(delta_ready.sem, at_delta)
                step(a.activation(sp_e[:, m, :], hb[:, :], ACT.Abs, bias=bdt))
                a.activation(sp_x[:, m, :], hb[:, :], ACT.Relu, bias=bdt).then_inc(head_read.sem, 1)
                a.activation(sp_e[:, m, :], sp_e[:, m, :], ACT.Exp, scale=-1.0).then_inc(sp_e_ready.sem, 1)

            def head0(name, j):
                if name == "xnT":
                    act.wait_ge(head_ps.sem, head_ps.at0(j, 1))
                    act.wait_ge(xr_ready.sem, xr_ready.at0(j, 0))
                    a.activation(XNT[:, :], hb[:, :], ACT.Copy).then_inc(head_read.sem, 1)
                if name == "xfT":
                    act.wait_ge(head_ps.sem, head_ps.at0(j, 2))
                    act.wait_ge(xl_ready.sem, xl_ready.at0(j, 0))
                    a.activation(XFT[:, :], hb[:, :], ACT.Identity, bias=col0("lnb"), scale=col0("lng")).then_inc(head_read.sem, 1)
                if name == "xin":
                    act.wait_ge(head_ps.sem, head_ps.at0(j, 3))
                    a.activation(xpad[:, 0, :, KC - 1:], by_batch(hb[:, :]), ACT.Copy).then_inc(head_read.sem, 1)
                    first_tap(0, col0, head_read.at0(j, 3), delta_ready.at0(j, 0))
                if name == "logits":
                    act.wait_ge(conv_ready.sem, conv_ready.at0(j, 1))
                    act.wait_ge(sp_l_ready.sem, sp_l_ready.at0(j, 0))
                    a.activation(th[:, :], conv[:, 0, :], ACT.Tanh).then_inc(th_ready.sem, 1)
                    act.wait_ge(lmax_sub.sem, lmax_sub.at0(j, 1))
                    a.activation(lexp[:, 0:TT, :], lg[:, 0:TT, :], ACT.Exp).then_inc(head_read.sem, 1)
                if name == "dt":
                    act.wait_ge(head_ps.sem, head_ps.at0(j, 7))
                    softplus(0, col0("bdt"), sp_x_ready.at0(j, 0), delta_ready.at0(j, 0))
                if name == "ln":
                    act.wait_ge(sp_u_ready.sem, sp_u_ready.at0(j, 1))
                    a.activation(sp_l[:, 0, :], sp_u[:, 0, :], ACT.Ln).then_inc(sp_l_ready.sem, 1)
                if name == "c":
                    act.wait_ge(head_ps.sem, head_ps.at0(j, 9))
                    act.wait_ge(rows_out.sem, rows_out.at0(j, 0))
                    a.activation(cd[0:N, 0, :], hb[0:N, :], ACT.Copy).then_inc(head_read.sem, 1)

            def head1(name, j):
                if name == "xnT":
                    act.wait_ge(head_ps.sem, head_ps.at1(j, 1))
                    act.wait_ge(xr_ready.sem, xr_ready.at1(j, 0))
                    act.wait_ge(xl_ready.sem, xl_ready.at1(j, 0))
                    a.activation(XNT[:, :], hb[:, :], ACT.Copy).then_inc(head_read.sem, 1)
                if name in ("x0", "x1"):
                    m = int(name[1])
                    act.wait_ge(head_ps.sem, head_ps.at1(j, 2 + m))
                    a.activation(xpad[:, m, :, KC - 1:], by_batch(hb[:, :]), ACT.Copy).then_inc(head_read.sem, 1)
                    first_tap(m, col1, head_read.at1(j, 2 + m), delta_ready.at1(j, 0))
                if name == "logits":
                    for m in range(J1):
                        act.wait_ge(conv_ready.sem, conv_ready.at1(j, m + 1))
                        act.wait_ge(xs_ready.sem, xs_ready.at1(j, m))
                        act.wait_ge(sp_l_ready.sem, sp_l_ready.at1(j, 0))
                        a.activation(th[:, :], conv[:, m, :], ACT.Tanh).then_inc(th_ready.sem, 1)
                    act.wait_ge(lmax_sub.sem, lmax_sub.at1(j, 1))
                    a.activation(lexp[:, 0:TT, :], lg[:, 0:TT, :], ACT.Exp)
                    a.activation(lexp[:, TT:, :], lg[:, TT:, :], ACT.Exp, scale=1.0 / GATE_TEMP).then_inc(head_read.sem, 1)
                if name in ("z0", "z1"):
                    m = int(name[1])
                    act.wait_ge(head_ps.sem, head_ps.at1(j, 5 + m))
                    act.wait_ge(kept_ready.sem, kept_ready.at1(j, 0))
                    a.activation(sz[:, m, :], hb[:, :], ACT.Tanh, scale=0.5).then_inc(tz_ready.sem, 1)
                if name in ("cd0", "cd1"):
                    m = int(name[2])
                    act.wait_ge(head_ps.sem, head_ps.at1(j, 9 + 3 * m))
                    act.wait_ge(rows_out.sem, rows_out.at1(j, 0))
                    a.activation(cd[:, m, :], hb[0:64, :], ACT.Copy).then_inc(head_read.sem, 1)
                if name == "ln":
                    act.wait_ge(sp_u_ready.sem, sp_u_ready.at1(j, J1))
                    a.activation(sp_l[:, :, :], sp_u[:, :, :], ACT.Ln).then_inc(sp_l_ready.sem, 1)
                if name in ("dt0", "dt1"):
                    m = int(name[2])
                    act.wait_ge(head_ps.sem, head_ps.at1(j, 10 + 3 * m))
                    softplus(m, col1("bdt", m), sp_x_ready.at1(j, 0), delta_ready.at1(j, 0))

            def hand_over0(i):
                act.wait_ge(head_read.sem, head_read.at0(i, 2))
                act.wait_ge(hid_ps.sem, hid_ps.at0(i, 0))
                a.activation(XH[:, :], XFT[:, :], ACT.Copy).then_inc(xh_ready.sem, 1)
                act.wait_ge(yT_ready.sem, yT_ready.at0(i, 0))
                a.activation(XR[:, :], XNT[:, :], ACT.Copy).then_inc(xr_ready.sem, 1)
                act.wait_ge(b_ps.sem, b_ps.at0(i, 0))
                act.wait_ge(bnew_ready.sem, bnew_ready.at0(i, 1))
                a.activation(Bst[:, 0, :], Bnew[:, 0, :], ACT.Copy).then_inc(bst_ready.sem, 1)

            def hand_over1(i):
                act.wait_ge(head_read.sem, head_read.at1(i, 1))
                act.wait_ge(hid_ps.sem, hid_ps.at1(i, 0))
                a.activation(XH[:, :], XNT[:, :], ACT.Copy).then_inc(xh_ready.sem, 1)
                act.wait_ge(yT_ready.sem, yT_ready.at1(i, 0))
                act.wait_ge(xw_ready.sem, xw_ready.at1(i, 0))
                a.activation(XR[:, :], XNT[:, :], ACT.Copy).then_inc(xr_ready.sem, 1)
                act.wait_ge(b_ps.sem, b_ps.at1(i, 0))
                act.wait_ge(bnew_ready.sem, bnew_ready.at1(i, J1))
                a.activation(Bst[:, :, :], Bnew[:, :, :], ACT.Copy).then_inc(bst_ready.sem, 1)

            def keep(i):
                act.wait_ge(xs_ready.sem, xs_ready.at1(i, J1))
                act.wait_ge(s_ps.sem, s_ps.at1(i, 0))
                for m in range(J1):
                    a.activation(xd[:, m, :], xs[:, m, :], ACT.Identity, scale=col1("dskip", m))
                act.wait_ge(head_read.sem, head_read.at1(i, 6))
                act.wait_ge(yz_ready.sem, yz_ready.at1(i, 0))
                a.activation(szm[:, :, :], sz[:, :, :], ACT.Copy, scale=0.5).then_inc(kept_ready.sem, 1)

            def form_decay(at, c, dl, scale):
                act.wait_ge(state_ready.sem, at(state_ready)(max(c - RING + 1, 0)))
                a.activation(by_batch(decay[:, c % RING, :])[:, :, 1:], by_batch(dl)[:, :, 1:], ACT.Exp,
                             scale=scale).then_inc(decay_ready.sem, 1)

            def rectify(i, u):
                act.wait_ge(hid_ps.sem, hid_ps.at0(i, u + 1))
                act.wait_ge(down_done.sem, down_done.at0(i, u - 1))
                a.activation(hid[:, u % 2, :], bank[HID_BANK + u % 2][:, :], ACT.Relu, bias=col0("b1", u)).then_inc(hid_ready.sem, 1)

            def main0(i, head, j):
                at = lambda s: (lambda n: s.at0(i, n))
                act.wait_ge(delta_ready.sem, delta_ready.at0(i, 1))
                for c in range(RING - 1):
                    form_decay(at, c, delta[:, 0, :], negA0[:, c:c + 1])
                for u in range(UNITS):
                    if head is head1 and u % FT == FT - 1 and u // FT >= 1:
                        split_high(E + u // FT - 1)
                    if u >= AHEAD:
                        rectify(i, u)
                    for c in now(CHUNKS0, u):
                        if c + RING - 1 < N:
                            form_decay(at, c + RING - 1, delta[:, 0, :], negA0[:, c + RING - 1:c + RING])
                    if j is not None:
                        for name in now(HEAD0 if head is head0 else HEAD1, u):
                            head(name, j)

            def tail0(i, ahead):
                ahead(0)
                act.wait_ge(mix_ps.sem, mix_ps.at0(i, 1))
                a.activation(yfT[:, :], bank[OUT_BANK][:, :], ACT.Copy).then_inc(yfT_ready.sem, 1)
                ahead(1)
                act.wait_ge(yf_ps.sem, yf_ps.at0(i, 1))
                act.wait_ge(hp_ready.sem, hp_ready.at0(i, 1))
                for k in range(TT):
                    last = a.activation(tg[:, k, :], bank[OUT_BANK][:, 128 * k:128 * k + 128], ACT.Tanh, scale=hp[:, k:k + 1])
                last.then_inc(tg_ready.sem, 1)

            def half_gate(i, u):
                act.wait_ge(hid_ps.sem, hid_ps.at1(i, u + 1))
                act.wait_ge(gg_ready.sem, gg_ready.at1(i, u - 1))
                a.activation(sg[:, u % 2, :], bank[HID_BANK + u % 2][:, :], ACT.Tanh, scale=0.5).then_inc(tanh_ready.sem, 1)

            def main1(i, head, j):
                at = lambda s: (lambda n: s.at1(i, n))
                act.wait_ge(delta_ready.sem, delta_ready.at1(i, 1))
                for c in range(RING - 1):
                    form_decay(at, c, delta[:, c // N, :], negA1[:, c:c + 1])
                for u in range(UNITS):
                    if u >= AHEAD:
                        half_gate(i, u)
                    if u == AHEAD:
                        keep(i)
                    for c in now(CHUNKS1, u):
                        c += RING - 1
                        if c < C1:
                            form_decay(at, c, delta[:, c // N, :], negA1[:, c:c + 1])
                    if j is not None:
                        for name in now(HEAD1, u):
                            head(name, j)

            def tail1(i, ahead):
                if ahead:
                    ahead(0)
                act.wait_ge(down_done.sem, down_done.at1(i, UNITS))
                a.activation(yfT[:, :], bank[OUT_BANK][:, :], ACT.Copy).then_inc(yfT_ready.sem, 1)
                if ahead:
                    ahead(1)
                act.wait_ge(yf_ps.sem, yf_ps.at1(i, 1))
                a.activation(tg[:, :, :], tiles(bank[OUT_BANK][:, :]), ACT.Tanh, scale=0.5).then_inc(tg_ready.sem, 1)

            act.wait_ge(consts_in.sem, consts_in.at0(0, 16 * len(CONSTS_FIRST)))
            a.activation(negA0[:, :], vec0[:, V0["alog"]:V0["alog"] + N], ACT.Exp)
            a.activation(negA1[:, :], vec1[:, V1["alog"]:V1["alog"] + J1 * N], ACT.Exp).then_inc(setup_act.sem, 1)
            act.wait_ge(setup_dve.sem, setup_dve.at0(0, SETUP_DVE))
            for name in HEAD0:
                head0(name, 0)
            for e in range(E):
                split_high(e)
            hand_over0(0)
            for u in range(AHEAD):
                rectify(0, u)
            with act.Fori(0, PAIRS - 1) as i:
                step.turn(i, ACT0)
                main0(i, head0, i + 1)
                hand_over0(i + 1)
                tail0(i, lambda u: rectify(i + 1, u))
            step.turned(PAIRS - 1)
            main0(PAIRS - 1, head1, 0)
            hand_over1(0)
            tail0(PAIRS - 1, lambda u: half_gate(0, u))
            split_high(2 * E - 1)
            with act.Fori(0, PAIRS - 1) as i:
                step.turn(i, ACT1)
                main1(i, head1, i + 1)
                hand_over1(i + 1)
                tail1(i, lambda u: half_gate(i + 1, u))
            step.turned(PAIRS - 1)
            main1(PAIRS - 1, None, None)
            tail1(PAIRS - 1, None)

        @block.tensor
        def _(pe):
            t = nc.tensor
            hb = bank[HEAD_BANK]

            def transposes(dst, src, done):
                for k in range(TT):
                    last = t.transpose(dst[:, 128 * k:128 * k + 128], src(k), ident[:, :])
                last.then_inc(done.sem, 1)

            def head_product(rows, weights, rhs):
                t.matmul(hb[0:rows, :], weights, rhs, start=True, stop=True).then_inc(head_ps.sem, 1)

            HEAD0_USE = dict(xnT=0, xfT=1, xin=2, logits=3, z=4, onehot=5, dt=6, b=7, c=8)
            HEAD1_USE = dict(xnT=0, x0=1, x1=2, logits=3, z0=4, z1=5, cwT=6, b0=7, cd0=8, dt0=9, b1=10, cd1=11, dt1=12)

            def head0(name, j):
                if name not in HEAD0_USE:
                    return
                pe.wait_ge(head_read.sem, head_read.at0(j, HEAD0_USE[name]))
                if name == "xnT":
                    pe.wait_ge(xn_ready.sem, xn_ready.at0(j, 1))
                    transposes(hb, lambda k: xn[:, k, :], head_ps)
                if name == "xfT":
                    pe.wait_ge(xf_ready.sem, xf_ready.at0(j, 1))
                    transposes(hb, lambda k: xf[:, k, :], head_ps)
                if name == "xin":
                    head_product(128, w_in0[:, 0:D], XNT[:, :])
                if name == "logits":
                    for k in range(TT):
                        last = t.matmul(hb[:, E * k:E * k + E], XNT[:, 128 * k:128 * k + 128], w_r0[:, :], start=True, stop=True)
                    last.then_inc(head_ps.sem, 1)
                if name == "z":
                    head_product(128, w_in0[:, D:2 * D], XNT[:, :])
                if name == "onehot":
                    pe.wait_ge(choice_ready.sem, choice_ready.at0(j, 1))
                    for k in range(TT):
                        last = t.transpose(hb[0:E, 128 * k:128 * k + 128], onehot[:, k, :], ident[:, :])
                    last.then_inc(head_ps.sem, 1)
                if name == "dt":
                    head_product(128, w_dt0[:, :], xs[:, 1, :])
                if name == "b":
                    head_product(96, w_b0[:, :], xs[:, 1, :])
                if name == "c":
                    head_product(N, w_c0[:, :], xs[:, 1, :])

            def head1(name, j):
                if name not in HEAD1_USE:
                    return
                pe.wait_ge(head_read.sem, head_read.at1(j, HEAD1_USE[name]))
                if name == "xnT":
                    pe.wait_ge(xn_ready.sem, xn_ready.at1(j, 1))
                    transposes(hb, lambda k: xn[:, k, :], head_ps)
                if name in ("x0", "x1", "z0", "z1"):
                    m = J1 * "xz".index(name[0]) + int(name[1])
                    head_product(128, w_in1[:, 128 * m:128 * m + 128], XNT[:, :])
                if name == "logits":
                    for k in range(2 * TT):
                        kind, tile = k // TT, k % TT
                        last = t.matmul(hb[:, E * k:E * k + E], XNT[:, 128 * tile:128 * tile + 128],
                                        w_r1[:, E * kind:E * kind + E], start=True, stop=True)
                    last.then_inc(head_ps.sem, 1)
                if name == "cwT":
                    pe.wait_ge(choice_ready.sem, choice_ready.at1(j, 1))
                    for k in range(TT):
                        last = t.transpose(hb[0:E, 128 * k:128 * k + 128], cw[:, k, :], ident[:, :])
                    last.then_inc(head_ps.sem, 1)
                m = int(name[-1]) if name[-1] in "01" else 0
                if name in ("b0", "b1"):
                    pe.wait_ge(xs_ready.sem, xs_ready.at1(j, m + 1))
                    head_product(96, w_b1[:, 96 * m:96 * m + 96], xs[:, m, :])
                if name in ("cd0", "cd1"):
                    head_product(64, w_cd1[:, 64 * m:64 * m + 64], xs[:, m, :])
                if name in ("dt0", "dt1"):
                    head_product(128, w_dt1[32:64, 128 * m:128 * m + 128], cd[32:64, m, :])

            def three_passes(dst, e, f, stop):
                ws = slice(128 * f, 128 * f + 128)
                t.matmul(dst, wh[:, e, ws], XH[:, :], start=True, stop=False)
                t.matmul(dst, wh[:, e, ws], XL[:, :], start=False, stop=False)
                return t.matmul(dst, wl[:, e, ws], XH[:, :], start=False, stop=stop)

            def spread_b(at, c, m):
                if c == 0:
                    pe.wait_ge(bst_ready.sem, at(bst_ready)(1))
                pe.wait_ge(drive_ready.sem, at(drive_ready)(c))
                n = c % N
                t.matmul(bank[B_BANK][:, :], sel[:, 128 * n:128 * n + 128], Bst[:, m, :], start=True, stop=True).then_inc(b_ps.sem, 1)

            def sum_group(at, q):
                pe.wait_ge(group_ready.sem, at(group_ready)(q + 1))
                k = q % (N // GROUP)
                t.matmul(bank[Y_BANK][:, :], ident[:, :], product[:, q % 2, :], start=(k == 0), stop=(k == N // GROUP - 1)).then_inc(summed.sem, 1)

            def hidden0(i, u):
                e, f = u // FT, u % FT
                dst = bank[HID_BANK + u % 2][:, :]
                if u == 0:
                    pe.wait_ge(xl_ready.sem, xl_ready.at0(i, 1))
                if f == 0:
                    pe.wait_ge(wl_ready.sem, wl_ready.at0(0, e + 1))
                pe.wait_ge(hid_ready.sem, hid_ready.at0(i, u - 1))
                three_passes(dst, e, f, False)
                if u == 0:
                    pe.wait_ge(ohm_ready.sem, ohm_ready.at0(i, 1))
                t.matmul(dst, big[:, e:e + 1].to_broadcast((E, 128)), ohm[:, :], start=False, stop=True).then_inc(hid_ps.sem, 1)

            def gate1(i, u):
                e, f = u // FT, u % FT
                if u == 0:
                    pe.wait_ge(xl_ready.sem, xl_ready.at1(i, 1))
                if f == 0:
                    pe.wait_ge(wl_ready.sem, wl_ready.at0(0, E + e + 1))
                pe.wait_ge(gg_ready.sem, gg_ready.at1(i, u - 1))
                three_passes(bank[HID_BANK + u % 2][:, :], e, f, True).then_inc(hid_ps.sem, 1)

            def main0(i, head, j, ahead):
                at = lambda s: (lambda n: s.at0(i, n))

                def down(u):
                    if u == 0:
                        pe.wait_ge(g_ready.sem, g_ready.at0(i, 0))
                    if u % FT == 0:
                        pe.wait_ge(wd_in[u // FT].sem, wd_in[u // FT].at0(0, 16))
                    pe.wait_ge(hid_ready.sem, hid_ready.at0(i, u + 1))
                    t.matmul(bank[OUT_BANK][:, :], wd[:, u, :], hid[:, u % 2, :], start=(u == 0), stop=False).then_inc(down_done.sem, 1)

                for u in range(UNITS):
                    if u >= AHEAD:
                        hidden0(i, u)
                    if u >= DOWN_LAG:
                        down(u - DOWN_LAG)
                    for c in now(CHUNKS0, u):
                        if c < N:
                            spread_b(at, c, 0)
                        if c >= LAG and (c - LAG) % GROUP == GROUP - 1:
                            if c - LAG == GROUP - 1:
                                pe.wait_ge(s_read.sem, s_read.at0(i, 0))
                            sum_group(at, (c - LAG) // GROUP)
                    for name in now(TAIL0, u):
                        if name == "y":
                            pe.wait_ge(yT_ready.sem, yT_ready.at0(i, 1))
                            transposes(bank[Y_BANK], lambda k: yT[:, 0, 128 * k:128 * k + 128], y_ps)
                        if name == "ynT":
                            pe.wait_ge(yn_ready.sem, yn_ready.at0(i, 1))
                            transposes(bank[UP_BANK], lambda k: yn[:, k, :], ynT_ps)
                        if name == "s":
                            pe.wait_ge(ynT_ready.sem, ynT_ready.at0(i, 1))
                            for k in range(TT):
                                last = t.matmul(bank[Y_BANK][:, 128 * k:128 * k + 128], ynT[:, 128 * k:128 * k + 128], w_out0[:, :],
                                                start=True, stop=True)
                            last.then_inc(s_ps.sem, 1)
                    if j is not None:
                        for name in now(HEAD0 if head is head0 else HEAD1, u):
                            head(name, j)
                for k in range(DOWN_LAG):
                    ahead(k)
                    down(UNITS - DOWN_LAG + k)
                pe.wait_ge(ohF_ready.sem, ohF_ready.at0(i, 1))
                t.matmul(bank[OUT_BANK][:, :], b2[:, :], ohF[:, :], start=False, stop=True).then_inc(mix_ps.sem, 1)
                pe.wait_ge(yfT_ready.sem, yfT_ready.at0(i, 1))
                transposes(bank[OUT_BANK], lambda k: yfT[:, 128 * k:128 * k + 128], yf_ps)

            def main1(i, head, j, ahead):
                at = lambda s: (lambda n: s.at1(i, n))

                def up(u):
                    e, f = u // FT, u % FT
                    if f == 0:
                        pe.wait_ge(xw_ready.sem, xw_ready.at1(i, e + 1))
                    pe.wait_ge(hid_ready.sem, hid_ready.at1(i, max(u - 1, 0)))
                    t.matmul(bank[UP_BANK + u % 2][:, :], wu[:, e, 128 * f:128 * f + 128], xw[:, e % 2, :], start=True, stop=True).then_inc(up_ps.sem, 1)

                def down(u):
                    if u == 0:
                        pe.wait_ge(g_ready.sem, g_ready.at1(i, 0))
                    if u % FT == 0:
                        pe.wait_ge(wd_in[u // FT].sem, wd_in[u // FT].at0(0, 32))
                    pe.wait_ge(hid_ready.sem, hid_ready.at1(i, u + 1))
                    ins = t.matmul(bank[OUT_BANK][:, :], wd[:, u, :], hid[:, u % 2, :], start=(u == 0), stop=(u == UNITS - 1))
                    ins.then_inc(down_done.sem, 1)

                for u in range(END1):
                    for c in now(CHUNKS1, u)[:1]:
                        if c < C1:
                            spread_b(at, c, c // N)
                    if AHEAD <= u < UNITS:
                        gate1(i, u)
                    if 1 <= u <= UNITS:
                        up(u - 1)
                    if ahead and UNITS <= u < UNITS + AHEAD:
                        ahead(u - UNITS)
                    if DOWN_LAG <= u < UNITS + DOWN_LAG:
                        down(u - DOWN_LAG)
                    for k, c in enumerate(now(CHUNKS1, u)):
                        if k > 0 and c < C1:
                            spread_b(at, c, c // N)
                        if c >= LAG and (c - LAG) % GROUP == GROUP - 1:
                            if c - LAG == GROUP - 1:
                                pe.wait_ge(s_read.sem, s_read.at1(i, 0))
                            if c - LAG == N + GROUP - 1:
                                pe.wait_ge(yT_ready.sem, yT_ready.at1(i, 1))
                            sum_group(at, (c - LAG) // GROUP)
                    if j is not None and u < UNITS:
                        for name in now(HEAD1, u):
                            head(name, j)
                pe.wait_ge(yz_ready.sem, yz_ready.at1(i, J1))
                for k in range(TT):
                    for m in range(J1):
                        last = t.matmul(bank[Y_BANK][:, 128 * k:128 * k + 128], yT[:, m, 128 * k:128 * k + 128], w_out1[:, m, :],
                                        start=(m == 0), stop=(m == J1 - 1))
                last.then_inc(s_ps.sem, 1)
                pe.wait_ge(yfT_ready.sem, yfT_ready.at1(i, 1))
                transposes(bank[OUT_BANK], lambda k: yfT[:, 128 * k:128 * k + 128], yf_ps)

            pe.wait_ge(consts_in.sem, consts_in.at0(0, 16 * len(CONSTS_FIRST)))
            for name in HEAD0:
                head0(name, 0)
            pe.wait_ge(late_in.sem, late_in.at0(0, 16 * len(LATE)))
            for u in range(AHEAD):
                hidden0(0, u)
            with pe.Fori(0, PAIRS - 1) as i:
                main0(i, head0, i + 1, lambda u: hidden0(i + 1, u))
            main0(PAIRS - 1, head1, 0, lambda u: gate1(0, u))
            pe.wait_ge(wu_in.sem, wu_in.at0(0, 16 * E))
            with pe.Fori(0, PAIRS - 1) as i:
                main1(i, head1, i + 1, lambda u: gate1(i + 1, u))
            main1(PAIRS - 1, None, None, None)


CONSTS = {
    "ident": ((128, 128), F32), "vec0": ((128, V0_COLS), F32), "w_in0": ((128, 2 * D), F32),
    "w_r0": ((128, E), F32), "br0": ((1, E), F32), "iota": ((128, TT, E), F32), "w_dt0": ((128, D), F32),
    "w_b0": ((128, 96), F32), "w_c0": ((128, N), F32), "big": ((E, E), BF16),
    "w_out0": ((128, D), F32), "b2": ((E, D), F32), "b_out0": ((1, D), F32),
    "W1": ((E, D, FT * 128), F32), "W2": ((E, FT * 128, D), F32),
    "vec1": ((128, V1_COLS), F32), "w_in1": ((128, 2 * J1 * 128), F32), "w_r1": ((128, 2 * E), F32),
    "w_b1": ((128, J1 * 96), F32), "w_cd1": ((128, J1 * 64), F32), "w_dt1": ((64, J1 * 128), F32),
    "sel": ((96, N * 128), BF16), "w_out1": ((J1 * 128, D), F32),
    "Wg": ((E, D, FT * 128), F32), "Wu": ((E, D, FT * 128), F32), "Wd": ((E, FT * 128, D), F32),
}


def program(nc, x, out, w):
    x1 = nc.dram_tensor("x1", (B * L, D), F32, kind="Internal").ap()
    crow = nc.dram_tensor("crow", (2, J1, 2 * N, T), F32, kind="Internal").ap()
    cwrow = nc.dram_tensor("cwrow", (2, E, T), F32, kind="Internal").ap()
    build(nc, x, out, x1, crow, cwrow, w)


def kernel(**inputs):
    import numpy as np
    import ml_dtypes
    import concourse.bacc as bacc
    from concourse.bass_utils import run_bass_kernel_spmd

    a = {k: np.asarray(v) for k, v in inputs.items()}
    col = lambda v: v.reshape(1, -1).T if v.ndim == 1 else v
    c = {}
    c["ident"] = np.eye(128, dtype=np.float32)
    c["vec0"] = np.concatenate([a["L0_attn_W_conv"][:, 0, :], col(a["L0_attn_b_conv"]), col(a["L0_attn_b_dt"]),
                                a["L0_attn_A_log"], col(a["L0_attn_ln_gamma"]), col(a["L0_attn_ln_beta"]),
                                col(a["L0_ffn_ln_g"]), col(a["L0_ffn_ln_b"]), a["L0_ffn_b1"].reshape(UNITS, 128).T], axis=1)
    c["w_in0"] = a["L0_attn_W_in"].T
    c["w_r0"] = a["L0_ffn_Wr"]
    c["br0"] = a["L0_ffn_br"].reshape(1, E)
    c["iota"] = np.tile(np.arange(E, dtype=np.float32), (128, TT, 1))
    c["w_dt0"] = a["L0_attn_W_dt"].T
    bt = a["L0_attn_W_xproj"][:N].T
    c["w_b0"] = np.concatenate([bt] * 6, axis=1)
    c["w_c0"] = a["L0_attn_W_xproj"][N:].T
    c["big"] = (BIG * np.eye(E)).astype(ml_dtypes.bfloat16)
    c["w_out0"] = a["L0_attn_W_out"].T
    c["b2"] = a["L0_ffn_b2"]
    c["b_out0"] = a["L0_attn_b_out"].reshape(1, D)
    c["W1"], c["W2"] = a["L0_ffn_W1"], a["L0_ffn_W2"]

    per_tile = lambda v: v.reshape(J1, 128, -1).transpose(1, 0, 2).reshape(128, -1)
    c["vec1"] = np.concatenate([per_tile(v) for v in (
        a["L1_attn_conv_w"][:, 0, :], a["L1_attn_conv_b"], a["L1_attn_dt_proj_b"], a["L1_attn_A_log"], a["L1_attn_Dskip"])], axis=1)
    c["w_in1"] = a["L1_attn_in_proj_w"].T
    c["w_r1"] = np.concatenate([a["L1_ffn_w_router"], a["L1_ffn_w_gating"]], axis=1)
    xp = a["L1_attn_x_proj_w"].reshape(2 * J1, 3 * N, 64)
    dp = a["L1_attn_dt_proj_w"].reshape(2 * J1, 64, N)
    w_b, w_cd, w_dt = np.zeros((128, J1, 3, 32), np.float32), np.zeros((128, J1, 64), np.float32), np.zeros((64, J1, 128), np.float32)
    sel = np.zeros((3, 32, N, 128), np.float32)
    for h in range(2):
        ch, row = slice(64 * h, 64 * h + 64), slice(N * h, N * h + N)
        for j in range(J1):
            w_b[ch, j, :, row] = xp[2 * j + h, N:2 * N].T[:, None, :]
            w_cd[ch, j, row] = xp[2 * j + h, 2 * N:].T
            w_cd[ch, j, 32 + N * h:32 + N * h + N] = xp[2 * j + h, :N].T
            w_dt[32 + N * h:32 + N * h + N, j, ch] = dp[2 * j + h].T
        for n in range(N):
            sel[:, N * h + n, n, ch] = 1.0
    c["w_b1"], c["w_cd1"], c["w_dt1"] = w_b.reshape(128, -1), w_cd.reshape(128, -1), w_dt.reshape(64, -1)
    c["sel"] = sel.reshape(96, N * 128).astype(ml_dtypes.bfloat16)
    c["w_out1"] = a["L1_attn_out_proj_w"].T
    c["Wg"], c["Wu"], c["Wd"] = a["L1_ffn_w_gate"], a["L1_ffn_w_up"], a["L1_ffn_w_down"]

    nc = bacc.Bacc("TRN2", target_bir_lowering=False, num_devices=1)
    arrays = {"x_dram": np.ascontiguousarray(a["L0_attn_x"].reshape(B * L, D))}
    x = nc.dram_tensor("x_dram", (B * L, D), F32, kind="ExternalInput").ap()
    w = {}
    for name, (shape, dt) in CONSTS.items():
        arrays[name + "_dram"] = np.ascontiguousarray(c[name])
        assert arrays[name + "_dram"].shape == shape, name
        w[name] = nc.dram_tensor(name + "_dram", shape, dt, kind="ExternalInput").ap()
    out = nc.dram_tensor("out_dram", (B * L, D), F32, kind="ExternalOutput").ap()
    program(nc, x, out, w)
    r = run_bass_kernel_spmd(nc, [arrays], core_ids=[0])
    return r.results[0]["out_dram"].reshape(B, L, D)
```

```python
import concourse.bass as bass
from concourse import mybir
from contextlib import ExitStack

F32 = mybir.dt.float32
F32R = mybir.dt.float32r
BF16 = mybir.dt.bfloat16
ALU = mybir.AluOpType
ACT = mybir.ActivationFunctionType
AXX = mybir.AxisListType.X

B, L, D = 8, 256, 128
NB = 2
T = NB * L
PAIRS = B // NB
TT = T // 128
E, FT = 8, 4
UNITS = E * FT
N = 16
KC = 4
J1 = 2
C1 = J1 * N
RING = 4
HIDS = 3
ROWS = 4
CWR = 2
LATE = 6
LAG0, LAG1 = 2, 3
GROUP = 4
GATE_TEMP = 0.1
EPS = 1e-5
BIG = 2.0 ** 100

V0 = dict(conv=0, bconv=4, bdt=5, alog=6, gam=22, bet=23, lng=24, lnb=25, b1=26)
V0_COLS = 26 + UNITS
V1 = dict(conv=0, bconv=8, bdt=10, alog=12, dskip=44)
V1_COLS = 46

HEAD0 = {6: "stat1", 7: "var1", 9: "xn", 10: "stat2", 11: "xnT var2", 12: "xin", 13: "logits xf tap1", 14: "lmax tap2",
         15: "lexp xfT tap3", 16: "th pick", 17: "xs prob", 18: "onehot", 19: "z", 20: "zx", 22: "dt", 23: "row", 24: "rest",
         25: "less ln"}
HEAD1 = {6: "stat1", 7: "var1", 9: "xn", 11: "xnT", 12: "xi0", 13: "tap01 logits", 14: "lmax", 15: "tap02 lexp xi1",
         16: "tap03 z0 tz0", 17: "th0 sz0", 18: "xs0", 19: "tap11", 20: "row0 tap12", 21: "z1 tz1 tap13 soft1", 22: "sz1 th1",
         23: "xs1", 24: "dt0 soft2", 25: "row1 rest0 soft3", 26: "dt1 less0", 27: "cwT rest1", 28: "less1 ln", 29: "xr"}
XW_SLOT = 30
CHUNKS0 = [int(1.4 * c) for c in range(N)]
CHUNKS1 = [c if c < 8 else c - 1 for c in range(C1)]
SUM_LAG0, SUM_LAG1 = 5, 4
TAIL0 = {27: "y", 28: "yn1", 29: "yn2", 30: "yn", 31: "ynT s"}

EARLY = dict(ident=128, vec0=V0_COLS, w_in0=2 * D, w_r0=E, w_dt0=D, w_row0=96, iota=TT * E, vec1=V1_COLS)
LATER = dict(w_out0=D, w_in1=2 * J1 * 128, w_r1=2 * E, w_row1=J1 * 96, w_out1=J1 * D)

SETUP_DVE = 11
DVE0, DVE1, POOL0, POOL1, ACT0, ACT1 = 15, 14, 8, 16, 2, 4


def now(slots, u):
    if isinstance(slots, dict):
        return slots.get(u, "").split()
    return [c for c, at in enumerate(slots) if at == u]


def steps(slots):
    return " ".join(slots.values()).split()


def tile_of(step):
    digits = [c for c in step if c.isdigit()]
    return int(digits[0]) if digits else 0


def sums(chunks, lag, u):
    return [q for q in range(len(chunks) // GROUP) if chunks[GROUP * q + GROUP - 1] + lag == u]


FIRST = steps(HEAD0)[:steps(HEAD0).index("onehot") + 1]
BETWEEN = {0: "z zx", 1: "dt", 2: "row rest", 3: "less ln"}
SPLIT_AFTER = ["xfT", "prob"]
SPLIT_SLOTS = [0, 1, 5, 7, 8, 9]
BEHIND = 4
assert FIRST + steps(BETWEEN) == steps(HEAD0)

BANK0 = [s for s in steps(HEAD0) if s in "xnT xfT xin logits z onehot dt row".split()]
BANK1 = [s for s in steps(HEAD1) if s in "xnT xi0 xi1 logits z0 z1 cwT row0 dt0 row1 dt1".split()]


class Signal:

    def __init__(self, sem, per0, per1, start):
        self.sem, self.per0, self.per1, self.start = sem, per0, per1, start

    def at0(self, i, n):
        return i * self.per0 + n + self.start

    def at1(self, i, n):
        return i * self.per1 + n + self.start + PAIRS * self.per0


class Chain:

    def __init__(self, eng, sem):
        self.eng, self.sem, self.base, self.i, self.per, self.n = eng, sem, 0, 0, 0, 0

    def turn(self, i, per):
        self.base, self.i, self.per, self.n = self.base + self.n, i, per, 0

    def turned(self, turns):
        assert self.n == self.per, (self.n, self.per)
        self.base, self.i, self.n = self.base + turns * self.per, 0, 0
        self.per = 0

    def __call__(self, ins):
        self.n += 1
        ins.then_inc(self.sem, 1)
        self.eng.wait_ge(self.sem, self.i * self.per + self.base + self.n)


def build(nc, x, out, x1, crow, cwrow, w):
    ctx = ExitStack()
    with ctx:
        sb = lambda name, shape, dt=F32: ctx.enter_context(nc.sbuf_tensor(name, shape, dt))
        def tiles(ap):
            return ap.rearrange("p (k d) -> p k d", k=TT)

        signals = []

        def sig(name, per0=1, per1=1, start=1):
            signals.append(Signal(ctx.enter_context(nc.semaphore(name)), per0, per1, start))
            return signals[-1]

        bank = [ctx.enter_context(nc.psum_tensor(f"bank{k}", [128, 512], F32)) for k in range(8)]
        Y_BANK, OUT_BANK, HID_BANK, UP_BANK, HEAD_BANK = 0, 1, 2, 5, 7

        big = sb("big", [E, E], BF16)
        brb, bout, b2 = sb("brb", [128, E]), sb("bout", [128, D]), sb("b2", [E, D])
        w_dt1 = sb("w_dt1", [64, J1 * 128])

        def parts(name, columns):
            whole = sb(name, [128, sum(columns.values())])
            ends = [sum(list(columns.values())[:k + 1]) for k in range(len(columns))]
            return whole, {part: whole[:, end - columns[part]:end] for part, end in zip(columns, ends)}

        early, part = parts("early", EARLY)
        ident, vec0, vec1, w_in0, w_r0, w_dt0, w_row0 = (part[n] for n in ("ident", "vec0", "vec1", "w_in0", "w_r0", "w_dt0", "w_row0"))
        iota = part["iota"].rearrange("p (k e) -> p k e", k=TT)
        later, part = parts("later", LATER)
        w_out0, w_in1, w_r1, w_row1 = (part[n] for n in ("w_out0", "w_in1", "w_r1", "w_row1"))
        w_out1 = part["w_out1"].rearrange("p (j d) -> p j d", j=J1)
        wh = sb("wh", [128, E, FT * 128], F32R)
        wl = sb("wl", [128, E, FT * 128], F32R)
        wd = sb("wd", [128, UNITS, D])
        wu = sb("wu", [128, E, FT * 128])
        xw = sb("xw", [128, 2, T])
        stage = xw
        negA0, negA1 = sb("negA0", [128, N]), sb("negA1", [128, J1 * N])
        half, ones = sb("half", [128, TT]), sb("ones", [128, 1])
        warm = sb("warm", [128, 1])
        idle = sb("idle", [128, 1])

        xt, xn = sb("xt", [128, TT, D]), sb("xn", [128, TT, D])
        XNT = sb("XNT", [128, T])
        stats, mv = sb("stats", [128, TT, 6]), sb("mv", [128, TT, 2])
        veps, rstd = sb("veps", [128, TT]), sb("rstd", [128, TT])
        veps_t, rstd_t = sb("veps_t", [128, TT]), sb("rstd_t", [128, TT])
        xpad = sb("xpad", [128, J1, NB, KC - 1 + L])
        xs = sb("xs", [128, J1, T])
        sz = sb("sz", [128, J1, T])
        lg, lexp = sb("lg", [128, 2 * TT, E]), sb("lexp", [128, 2 * TT, E])
        lmax, lsum, linv = sb("lmax", [128, 2 * TT]), sb("lsum", [128, 2 * TT]), sb("linv", [128, 2 * TT])
        eq, onehot, cw = sb("eq", [128, TT, E]), sb("onehot", [128, TT, E]), sb("cw", [128, TT, E])
        ohT = sb("ohT", [E, T])
        cwT = ohT
        sp_e, sp_u = sb("sp_e", [128, J1, T]), sb("sp_u", [128, J1, T])
        sp_l, sp_x = sb("sp_l", [128, J1, T]), sb("sp_x", [128, J1, T])
        conv, th = sp_l, sp_u[:, J1 - 1, :]
        rows = sb("rows", [96, J1, T])

        XH, XL, XR = sb("XH", [128, T], F32R), sb("XL", [128, T], F32R), sb("XR", [128, T])
        ohm = sb("ohm", [E, T], BF16)
        hp = sb("hp", [128, TT])
        delta, dx = sb("delta", [128, J1, T]), sb("dx", [128, J1, T])
        CB = sb("CB", [128, ROWS, 2, T])
        decay, state = sb("decay", [128, RING, T]), sb("state", [128, RING, T])
        drive, product, addend = sb("drive", [128, 2, T]), sb("product", [128, 2, T]), sb("addend", [128, T])
        xd, szm = sb("xd", [128, J1, T]), sb("szm", [128, J1, T])
        cwb = sb("cwb", [128, CWR, T])
        sg, gg, hid = sb("sg", [128, 2, T]), sb("gg", [128, 2, T]), sb("hid", [128, 2, T])
        xf, XFT, ohF = tiles(sg[:, 0, :]), sg[:, 1, :], szm[0:E, 0, :]

        yT, ynT = xd, xd[:, 1, :]
        xr, so = sb("xr", [128, TT, D]), sb("so", [128, TT, D])
        yn = so
        yfT = sb("yfT", [128, T])
        g = tg = tiles(yfT[:, :])

        early_in, br_in, late_in = sig("early_in"), sig("br_in"), sig("late_in")
        stage_in = [sig(f"stage_in{e}") for e in range(E)]
        wh_ready, wl_ready = sig("wh_ready"), sig("wl_ready")
        wd_in = [sig(f"wd_in{e}") for e in range(E)]
        wu_in = sig("wu_in")
        setup_act, setup_dve = sig("setup_act"), sig("setup_dve")
        dve_step, pool_step, act_step = (ctx.enter_context(nc.semaphore(n)) for n in ("dve_step", "pool_step", "act_step"))
        x_in, r_in, x_out = sig("x_in", 16, 16), sig("r_in", 16, 16), sig("x_out", 16, 16)
        rows_out = sig("rows_out", 32, 32 * J1)
        cb_in = [sig(f"cb_in{k}", 16 * (N // ROWS), 32 * (C1 // ROWS)) for k in range(ROWS)]
        cw_out = sig("cw_out", 0, 16)
        cw_in = [sig(f"cw_in{k}", 0, 16 * (E // CWR)) for k in range(CWR)]
        var_ready, rstd_ready = sig("var_ready", 2, 1), sig("rstd_ready", 2, 1)
        xn_ready, xf_ready = sig("xn_ready"), sig("xf_ready", 1, 0)
        head_ps = sig("head_ps", len(BANK0), len(BANK1))
        head_read = sig("head_read", len(BANK0), len(BANK1))
        conv_ready, th_ready, xs_ready = sig("conv_ready", 1, J1), sig("th_ready", 1, J1), sig("xs_ready", 1, J1)
        tz_ready, sz_ready = sig("tz_ready", 0, J1), sig("sz_ready", 0, J1)
        tap_ready = sig("tap_ready", 1, J1)
        lexp_ready, choice_ready = sig("lexp_ready"), sig("choice_ready")
        sp_u_ready, sp_c_ready, sp_x_ready = (sig(n, 1, J1) for n in ("sp_u_ready", "sp_c_ready", "sp_x_ready"))
        sp_l_ready, ohF_ready = sig("sp_l_ready"), sig("ohF_ready", 1, 0)
        xh_ready, xl_ready, xr_ready, ohm_ready = sig("xh_ready"), sig("xl_ready"), sig("xr_ready"), sig("ohm_ready", 1, 0)
        delta_ready, dx_ready = sig("delta_ready", 1, J1), sig("dx_ready", 1, J1)
        kept_ready, hp_ready = sig("kept_ready", 0, 1), sig("hp_ready", 1, 0)
        drive_ready, decay_ready = sig("drive_ready", N, C1), sig("decay_ready", N, C1)
        state_ready, state_used = sig("state_ready", N, C1), sig("state_used", N, C1)
        group_ready, summed = sig("group_ready", N // GROUP, C1 // GROUP), sig("summed", N // GROUP, C1 // GROUP)
        hid_ps, hid_ready, down_done = sig("hid_ps", UNITS, UNITS), sig("hid_ready", UNITS, UNITS, 2), sig("down_done", UNITS, UNITS, 2)
        xw_ready, tanh_ready, gg_ready, up_ps = sig("xw_ready", 0, E), sig("tanh_ready", 0, UNITS), sig("gg_ready", 0, UNITS, 2), sig("up_ps", 0, UNITS, FT + 1)
        mix_ps, yfT_ready, yf_ps, tg_ready, g_ready = sig("mix_ps", 1, 0), sig("yfT_ready"), sig("yf_ps"), sig("tg_ready"), sig("g_ready", 1, 1, 2)
        yT_ready, y_ps, yn_ready, ynT_ps, ynT_ready = sig("yT_ready", 1, J1), sig("y_ps", 1, 0), sig("yn_ready", 1, 0), sig("ynT_ps", 1, 0), sig("ynT_ready", 1, 0)
        tvar_ready, trstd_ready = sig("tvar_ready", 1, 0), sig("trstd_ready", 1, 0)
        yz_ready = sig("yz_ready", 0, J1)
        s_ps, s_read, gated, out_ready = sig("s_ps"), sig("s_read", 1, 0), sig("gated"), sig("out_ready")

        block = ctx.enter_context(nc.Block())

        def by_batch(ap):
            return ap.rearrange("p (b l) -> p b l", b=NB)

        def use0(signal, j, step):
            return signal.sem, signal.at0(j, BANK0.index(step) + 1)

        def use1(signal, j, step):
            return signal.sem, signal.at1(j, BANK1.index(step) + 1)

        def in0(i):
            return lambda signal, n: signal.at0(i, n)

        def in1(i):
            return lambda signal, n: signal.at1(i, n)

        def over_e(ap):
            return ap.rearrange("p (k a) -> p k a", a=1).to_broadcast((128, ap.shape[1], E))

        def col0(name, k=0):
            return vec0[:, V0[name] + k:V0[name] + k + 1]

        def col1(name, k=0):
            return vec1[:, V1[name] + k:V1[name] + k + 1]

        @block.sync
        def _(sp):
            tokens = lambda ap, i: ap[i * T:i * T + T, :].rearrange("(k p) d -> p k d", p=128)

            def load_gate(e):
                if e >= 2:
                    sp.wait_ge(wl_ready.sem, wl_ready.at0(0, E + e - 1))
                sp.dma_start(stage[:, e % 2, :], w["Wg"][e]).then_inc(stage_in[e].sem, 16)

            def load_wd(e, src):
                sp.dma_start(wd[:, FT * e:FT * e + FT, :], src.rearrange("(f p) d -> p f d", p=128)).then_inc(wd_in[e].sem, 16)

            def load_x(j, layer):
                at = (xn_ready.at0 if layer == 0 else xn_ready.at1)(j, 0)
                if j > 0 or layer == 1:
                    sp.wait_ge(xn_ready.sem, at)
                if layer == 1:
                    sp.wait_ge(x_out.sem, x_out.at0(j + 1, 0))
                sp.dma_start(xt[:, :, :], tokens(x if layer == 0 else x1, j)).then_inc(x_in.sem, 16)

            def load_cb0(j, c):
                if j > 0 or c >= ROWS:
                    sp.wait_ge(state_used.sem, state_used.at0(j, c - ROWS + 1))
                src = crow[j % 2, 0:1, :, c, :]
                sp.dma_start(CB[:, c % ROWS, :, :], src.to_broadcast((128, 2, T))).then_inc(cb_in[c % ROWS].sem, 16)

            def load_cb1(j, c):
                sp.wait_ge(state_used.sem, state_used.at1(j, c - ROWS + 1))
                m, n = c // N, c % N
                for h in range(2):
                    src = crow[j % 2, m:m + 1, :, N * h + n, :]
                    sp.dma_start(CB[64 * h:64 * h + 64, c % ROWS, :, :], src.to_broadcast((64, 2, T))).then_inc(cb_in[c % ROWS].sem, 16)

            def send_rows(j, layer, m):
                sp.wait_ge(*(use0(head_read, j, "row") if layer == 0 else use1(head_read, j, f"row{m}")))
                count = N if layer == 0 else 2 * N
                for k, at in enumerate((0, 64)):
                    sp.dma_start(crow[j % 2, m, k, 0:count, :], rows[at:at + count, m, :]).then_inc(rows_out.sem, 16)
                out_at = rows_out.at0 if layer == 0 else rows_out.at1
                sp.wait_ge(rows_out.sem, out_at(j, 32 * (m + 1)))

            def load_cw(j, e):
                if j > 0 or e >= CWR:
                    sp.wait_ge(xw_ready.sem, xw_ready.at1(j, e - CWR + 1))
                src = cwrow[j % 2, e:e + 1, :].to_broadcast((128, T))
                sp.dma_start(cwb[:, e % CWR, :], src).then_inc(cw_in[e % CWR].sem, 16)

            def send_cw(j):
                sp.wait_ge(*use1(head_read, j, "cwT"))
                sp.dma_start(cwrow[j % 2, :, :], cwT[:, :]).then_inc(cw_out.sem, 16)
                sp.wait_ge(cw_out.sem, cw_out.at1(j, 16))

            def send_out(i, layer):
                at = out_ready.at0 if layer == 0 else out_ready.at1
                sp.wait_ge(out_ready.sem, at(i, 1))
                sp.dma_start(tokens(x1 if layer == 0 else out, i), so[:, :, :]).then_inc(x_out.sem, 16)

            def load_residual(i, layer):
                at = out_ready.at0 if layer == 0 else out_ready.at1
                sp.wait_ge(out_ready.sem, at(i, 0))
                sp.dma_start(xr[:, :, :], tokens(x if layer == 0 else x1, i)).then_inc(r_in.sem, 16)

            load_x(0, 0)
            sp.dma_start(early[:, :], w["early"]).then_inc(early_in.sem, 16)
            sp.dma_start(brb[:, :], w["br0"].to_broadcast((128, E))).then_inc(br_in.sem, 16)
            for e in range(E):
                sp.dma_start(wu[:, e, :], w["W1"][e]).then_inc(stage_in[e].sem, 16)
            sp.dma_start(big[:, :], w["big"]).then_inc(late_in.sem, 16)
            sp.dma_start(b2[:, :], w["b2"]).then_inc(late_in.sem, 16)
            sp.dma_start(bout[:, :], w["b_out0"].to_broadcast((128, D))).then_inc(late_in.sem, 16)
            sp.dma_start(w_dt1[:, :], w["w_dt1"]).then_inc(late_in.sem, 16)
            sp.dma_start(later[:, :], w["later"]).then_inc(late_in.sem, 16)
            for e in range(E):
                load_wd(e, w["W2"][e])
            send_rows(0, 0, 0)
            for i in range(PAIRS):
                last = i == PAIRS - 1
                load_x(0 if last else i + 1, int(last))
                for c in range(ROWS):
                    load_cb0(i, c)
                for u in range(UNITS):
                    if i == 0 and u >= UNITS - E:
                        sp.wait_ge(wl_ready.sem, wl_ready.at0(0, E))
                        sp.dma_start(wu[:, u - (UNITS - E), :], w["Wu"][u - (UNITS - E)]).then_inc(wu_in.sem, 16)
                    if u == LATE:
                        if i > 0:
                            send_out(i - 1, 0)
                        load_residual(i, 0)
                    for step in now(HEAD1 if last else HEAD0, u):
                        if step == "row":
                            send_rows(i + 1, 0, 0)
                        if step == "cwT":
                            send_cw(0)
                        if step in ("row0", "row1"):
                            send_rows(0, 1, int(step[3]))
                    for c in now(CHUNKS0, u - 1):
                        if c + ROWS < N:
                            load_cb0(i, c + ROWS)
                    if last and u % FT == FT - 1:
                        e = u // FT
                        sp.wait_ge(hid_ps.sem, hid_ps.at0(i, u + 1))
                        load_gate(e)
                        if e >= 1:
                            sp.wait_ge(down_done.sem, down_done.at0(i, FT * e))
                            load_wd(e - 1, w["Wd"][e - 1])
            for i in range(PAIRS):
                last = i == PAIRS - 1
                if not last:
                    load_x(i + 1, 1)
                if i == 0:
                    load_cw(0, 0)
                load_cw(i, 1)
                for c in range(ROWS):
                    load_cb1(i, c)
                if i == 0:
                    sp.wait_ge(down_done.sem, down_done.at0(PAIRS, 0))
                    load_wd(E - 1, w["Wd"][E - 1])
                for u in range(UNITS):
                    if u == LATE:
                        send_out(i - 1 if i else PAIRS - 1, int(i > 0))
                        if i == PAIRS - 1:
                            sp.wait_ge(x_out.sem, x_out.at0(PAIRS, 0))
                        load_residual(i, 1)
                    for step in ([] if last else now(HEAD1, u)):
                        if step == "cwT":
                            send_cw(i + 1)
                        if step in ("row0", "row1"):
                            send_rows(i + 1, 1, int(step[3]))
                    for c in now(CHUNKS1, u - 1):
                        if c + ROWS < C1:
                            load_cb1(i, c + ROWS)
                    if u % FT == 0 and u // FT + CWR < E:
                        load_cw(i, u // FT + CWR)
                    if u == XW_SLOT - 1 and not last:
                        load_cw(i + 1, 0)
            send_out(PAIRS - 1, 1)
            sp.wait_ge(x_out.sem, x_out.at1(PAIRS, 0))

        @block.vector
        def _(dve):
            v = nc.vector
            step = Chain(dve, dve_step)

            def split_low(k):
                e = k % E
                src = wu[:, e, :] if k < E else stage[:, e % 2, :]
                dve.wait_ge(wh_ready.sem, wh_ready.at0(0, k + 1))
                v.tensor_tensor(wl[:, e, :], src, wh[:, e, :].bitcast(F32), ALU.subtract).then_inc(wl_ready.sem, 1)

            def row_sums(src):
                for k in range(TT):
                    last = v.bn_stats(stats[:, k, :], src[:, k, :])
                step(last)

            def variance(var, var_sig):
                v.memset(idle[:, :], 0.0)
                for k in range(TT):
                    last = v.bn_aggr(mv[:, k, :], stats[:, k, :])
                step(last)
                v.tensor_scalar(var[:, :], mv[:, :, 1], EPS, None, ALU.add).then_inc(var_sig.sem, 1)

            def normalise(dst, src, root, ready):
                for k in range(TT):
                    last = v.tensor_scalar(dst[:, k, :], src[:, k, :], mv[:, k, 0:1], root[:, k:k + 1], ALU.subtract, ALU.mult)
                last.then_inc(ready.sem, 1)

            def tap(m, k, col, ready):
                cv = by_batch(conv[:, m, :])
                ins = v.scalar_tensor_tensor(out=cv, in0=xpad[:, m, :, k:k + L], scalar=col("conv", KC * m + k),
                                             in1=cv, op0=ALU.mult, op1=ALU.add)
                if k < KC - 1:
                    step(ins)
                else:
                    ins.then_inc(ready.sem, 1)

            def rounding(m, at_u):
                dve.wait_ge(sp_u_ready.sem, at_u)
                v.scalar_tensor_tensor(out=sp_e[:, m, :], in0=sp_u[:, m, :], scalar=1.0, in1=sp_e[:, m, :],
                                       op0=ALU.subtract, op1=ALU.subtract).then_inc(sp_c_ready.sem, 1)

            def head0(name, j):
                if name == "stat1":
                    dve.wait_ge(x_in.sem, x_in.at0(j, 16))
                    row_sums(xt)
                if name in ("var1", "var2"):
                    variance(veps, var_ready)
                if name == "xn":
                    dve.wait_ge(head_ps.sem, head_ps.at0(j, 0))
                    dve.wait_ge(rstd_ready.sem, rstd_ready.at0(j, 1))
                    normalise(xn, xt, rstd, xn_ready)
                if name == "stat2":
                    dve.wait_ge(xn_ready.sem, xn_ready.at0(j, 1))
                    row_sums(xn)
                if name == "xf":
                    dve.wait_ge(rstd_ready.sem, rstd_ready.at0(j, 2))
                    normalise(xf, xn, rstd, xf_ready)
                if name == "tap1":
                    dve.wait_ge(tap_ready.sem, tap_ready.at0(j, 1))
                if name in ("tap1", "tap2", "tap3"):
                    tap(0, int(name[3]), col0, conv_ready)
                if name == "lmax":
                    dve.wait_ge(*use0(head_ps, j, "logits"))
                    br_all = brb[:, :].rearrange("p (a e) -> p a e", a=1).to_broadcast((128, TT, E))
                    step(v.tensor_tensor(lg[:, 0:TT, :], bank[HEAD_BANK][:, 0:TT * E].rearrange("p (k e) -> p k e", k=TT), br_all, ALU.add))
                    step(v.tensor_reduce(lmax[:, 0:TT], lg[:, 0:TT, :], AXX, ALU.max))
                    v.tensor_tensor(lg[:, 0:TT, :], lg[:, 0:TT, :], over_e(lmax[:, 0:TT]), ALU.subtract).then_inc(head_read.sem, 1)
                if name == "pick":
                    dve.wait_ge(*use0(head_read, j, "logits"))
                    step(v.tensor_scalar(eq[:, :, :], lg[:, 0:TT, :], 0.0, -float(E), ALU.is_equal, ALU.mult))
                    step(v.tensor_tensor(eq[:, :, :], eq[:, :, :], iota[:, :, :], ALU.add))
                    step(v.tensor_reduce(lmax[:, 0:TT], eq[:, :, :], AXX, ALU.min))
                    v.tensor_tensor(onehot[:, :, :], eq[:, :, :], over_e(lmax[:, 0:TT]), ALU.is_equal).then_inc(choice_ready.sem, 1)
                if name == "prob":
                    dve.wait_ge(lexp_ready.sem, lexp_ready.at0(j, 1))
                    step(v.tensor_reduce(lsum[:, 0:TT], lexp[:, 0:TT, :], AXX, ALU.add))
                    step(v.reciprocal(linv[:, 0:TT], lsum[:, 0:TT]))
                if name == "xs":
                    dve.wait_ge(th_ready.sem, th_ready.at0(j, 1))
                    dve.wait_ge(dx_ready.sem, dx_ready.at0(j, 0))
                    v.scalar_tensor_tensor(out=xs[:, 0, :], in0=th[:, :], scalar=1.0, in1=conv[:, 0, :],
                                           op0=ALU.add, op1=ALU.mult).then_inc(xs_ready.sem, 1)
                if name == "zx":
                    dve.wait_ge(*use0(head_ps, j, "z"))
                    dve.wait_ge(xs_ready.sem, xs_ready.at0(j, 1))
                    v.tensor_tensor(xs[:, 1, :], xs[:, 0, :], bank[HEAD_BANK][:, :], ALU.mult).then_inc(head_read.sem, 1)
                if name == "rest":
                    rounding(0, sp_u_ready.at0(j, 1))

            def low0(i):
                dve.wait_ge(xh_ready.sem, xh_ready.at0(i, 1))
                v.tensor_tensor(XL[:, :], XFT[:, :], XH[:, :].bitcast(F32), ALU.subtract).then_inc(xl_ready.sem, 1)
                dve.wait_ge(*use0(head_read, i, "onehot"))
                v.tensor_scalar(ohm[:, :], ohT[:, :], 1.0, None, ALU.subtract).then_inc(ohm_ready.sem, 1)

            def form_delta(i, at, m, u, tiles_):
                dve.wait_ge(sp_l_ready.sem, at(sp_l_ready, 1))
                dve.wait_ge(sp_x_ready.sem, at(sp_x_ready, tiles_))
                dve.wait_ge(decay_ready.sem, at(decay_ready, 0))
                v.tensor_tensor(delta[:, m, :], sp_x[:, m, :], sp_l[:, m, :], ALU.add).then_inc(delta_ready.sem, 1)
                dve.wait_ge(delta_ready.sem, at(delta_ready, m + 1))
                dve.wait_ge(drive_ready.sem, at(drive_ready, 0))
                v.tensor_tensor(dx[:, m, :], delta[:, m, :], xs[:, u, :], ALU.mult).then_inc(dx_ready.sem, 1)

            def form_drive(at, c, m, tiles_):
                dve.wait_ge(dx_ready.sem, at(dx_ready, m + 1))
                dve.wait_ge(cb_in[c % ROWS].sem, at(cb_in[c % ROWS], (16 if tiles_ == 1 else 32) * (c // ROWS + 1)))
                dve.wait_ge(state_ready.sem, at(state_ready, max(c - 1, 0)))
                v.tensor_tensor(drive[:, c % 2, :], dx[:, m, :], CB[:, c % ROWS, 1, :], ALU.mult).then_inc(drive_ready.sem, 1)

            def scan(at, c):
                dve.wait_ge(decay_ready.sem, at(decay_ready, c + 1))
                dve.wait_ge(drive_ready.sem, at(drive_ready, c + 1))
                dve.wait_ge(state_used.sem, at(state_used, max(c - RING + 1, 0)))
                v.tensor_tensor_scan(state[:, c % RING, :], decay[:, c % RING, :], drive[:, c % 2, :], 0.0,
                                     ALU.mult, ALU.add).then_inc(state_ready.sem, 1)

            def slot0(i, u, head=None, j=None, late=None, units=True, chunks=True):
                at = in0(i)
                if u == 0 and units:
                    low0(i)
                if chunks:
                    for c in now(CHUNKS0, u - 1):
                        scan(at, c)
                if late:
                    late(u)
                if u == 0 and chunks:
                    form_delta(i, at, 0, 1, 1)
                if chunks:
                    for c in now(CHUNKS0, u):
                        form_drive(at, c, 0, 1)
                if u == LATE:
                    dve.wait_ge(mix_ps.sem, mix_ps.at0(i, 0))
                    v.tensor_copy(ohF[:, :], ohT[:, :]).then_inc(ohF_ready.sem, 1)
                    v.tensor_scalar(hp[:, :], linv[:, 0:TT], 0.5, None, ALU.mult).then_inc(hp_ready.sem, 1)
                if head is head1 and u % FT == FT - 1 and u // FT >= 1:
                    split_low(E + u // FT - 1)
                for name in now(TAIL0, u):
                    if name == "y":
                        dve.wait_ge(summed.sem, summed.at0(i, N // GROUP))
                        v.tensor_tensor(yT[:, 0, :], XR[:, :], bank[Y_BANK][:, :], ALU.add).then_inc(yT_ready.sem, 1)
                    if name == "yn1":
                        dve.wait_ge(y_ps.sem, y_ps.at0(i, 1))
                        row_sums(tiles(bank[Y_BANK][:, :]))
                    if name == "yn2":
                        variance(veps_t, tvar_ready)
                    if name == "yn":
                        dve.wait_ge(x_out.sem, x_out.at0(i, 0))
                        dve.wait_ge(trstd_ready.sem, trstd_ready.at0(i, 1))
                        normalise(yn, tiles(bank[Y_BANK][:, :]), rstd_t, yn_ready)
                    if name == "ynT":
                        dve.wait_ge(ynT_ps.sem, ynT_ps.at0(i, 1))
                        v.tensor_scalar(ynT, bank[UP_BANK][:, :], col0("gam"), col0("bet"), ALU.mult, ALU.add).then_inc(ynT_ready.sem, 1)
                    if name == "s":
                        dve.wait_ge(s_ps.sem, s_ps.at0(i, 1))
                        bo = bout[:, :].rearrange("p (a d) -> p a d", a=1).to_broadcast((128, TT, D))
                        v.tensor_tensor(so[:, :, :], tiles(bank[Y_BANK][:, :]), bo, ALU.add).then_inc(s_read.sem, 1)
                if head:
                    for name in now(HEAD0 if head is head0 else HEAD1, u):
                        head(name, j)

            def late0(i, u):
                if u == 4:
                    dve.wait_ge(tg_ready.sem, tg_ready.at0(i, 1))
                    v.scalar_tensor_tensor(out=g[:, :, :], in0=tg[:, :, :], scalar=1.0, in1=tiles(bank[HEAD_BANK][:, :]),
                                           op0=ALU.add, op1=ALU.mult).then_inc(g_ready.sem, 1)
                if u == 5:
                    dve.wait_ge(g_ready.sem, g_ready.at0(i, 1))
                    dve.wait_ge(s_read.sem, s_read.at0(i, 1))
                    for k in range(TT):
                        last = v.scalar_tensor_tensor(out=so[:, k, :], in0=g[:, k, :], scalar=hp[:, k:k + 1], in1=so[:, k, :],
                                                      op0=ALU.mult, op1=ALU.mult)
                    last.then_inc(gated.sem, 1)

            def head1(name, j):
                m = tile_of(name)
                if name == "stat1":
                    dve.wait_ge(x_in.sem, x_in.at1(j, 16))
                    row_sums(xt)
                if name == "var1":
                    variance(veps, var_ready)
                if name == "xn":
                    dve.wait_ge(head_ps.sem, head_ps.at1(j, 0))
                    dve.wait_ge(rstd_ready.sem, rstd_ready.at1(j, 1))
                    normalise(xn, xt, rstd, xn_ready)
                if name in ("tap01", "tap11"):
                    dve.wait_ge(tap_ready.sem, tap_ready.at1(j, m + 1))
                if name[:3] == "tap":
                    tap(m, int(name[-1]), col1, conv_ready)
                if name in ("xs0", "xs1"):
                    dve.wait_ge(th_ready.sem, th_ready.at1(j, m + 1))
                    dve.wait_ge(kept_ready.sem, kept_ready.at1(j, 0))
                    dve.wait_ge(dx_ready.sem, dx_ready.at1(j, 0))
                    v.scalar_tensor_tensor(out=xs[:, m, :], in0=th[:, :], scalar=1.0, in1=conv[:, m, :],
                                           op0=ALU.add, op1=ALU.mult).then_inc(xs_ready.sem, 1)
                if name == "lmax":
                    dve.wait_ge(*use1(head_ps, j, "logits"))
                    lps = bank[HEAD_BANK][:, 0:2 * TT * E].rearrange("p (k e) -> p k e", e=E)
                    step(v.tensor_reduce(lmax[:, :], lps, AXX, ALU.max))
                    v.tensor_tensor(lg[:, :, :], lps, over_e(lmax[:, :]), ALU.subtract).then_inc(head_read.sem, 1)
                if name in ("sz0", "sz1"):
                    dve.wait_ge(tz_ready.sem, tz_ready.at1(j, m + 1))
                    v.scalar_tensor_tensor(out=sz[:, m, :], in0=sz[:, m, :], scalar=1.0, in1=bank[HEAD_BANK][:, :],
                                           op0=ALU.add, op1=ALU.mult).then_inc(head_read.sem, 1)
                if name == "soft1":
                    dve.wait_ge(lexp_ready.sem, lexp_ready.at1(j, 1))
                    step(v.tensor_reduce(lsum[:, :], lexp[:, :, :], AXX, ALU.add))
                    step(v.reciprocal(linv[:, :], lsum[:, :]))
                    step(v.tensor_tensor(lexp[:, :, :], lexp[:, :, :], over_e(linv[:, :]), ALU.mult))
                if name == "soft2":
                    step(v.tensor_tensor(cw[:, :, :], lexp[:, 0:TT, :], lexp[:, TT:, :], ALU.mult))
                    step(v.tensor_reduce(lsum[:, 0:TT], cw[:, :, :], AXX, ALU.add))
                    step(v.tensor_scalar(lsum[:, 0:TT], lsum[:, 0:TT], 1e-9, 2.0, ALU.add, ALU.mult))
                if name == "soft3":
                    step(v.reciprocal(linv[:, 0:TT], lsum[:, 0:TT]))
                    v.tensor_tensor(cw[:, :, :], cw[:, :, :], over_e(linv[:, 0:TT]), ALU.mult).then_inc(choice_ready.sem, 1)
                if name in ("rest0", "rest1"):
                    rounding(m, sp_u_ready.at1(j, m + 1))

            def low1(i):
                dve.wait_ge(xh_ready.sem, xh_ready.at1(i, 1))
                v.tensor_tensor(XL[:, :], XNT[:, :], XH[:, :].bitcast(F32), ALU.subtract).then_inc(xl_ready.sem, 1)

            def finish_gate(i, u):
                dve.wait_ge(tanh_ready.sem, tanh_ready.at1(i, u + 1))
                dve.wait_ge(hid_ready.sem, hid_ready.at1(i, u - 1))
                v.scalar_tensor_tensor(out=gg[:, u % 2, :], in0=sg[:, u % 2, :], scalar=1.0, in1=bank[HID_BANK + u % HIDS][:, :],
                                       op0=ALU.add, op1=ALU.mult).then_inc(gg_ready.sem, 1)

            def finish_hidden(i, u):
                dve.wait_ge(up_ps.sem, up_ps.at1(i, u + 1))
                dve.wait_ge(gg_ready.sem, gg_ready.at1(i, u + 1))
                dve.wait_ge(down_done.sem, down_done.at1(i, u - 1))
                v.tensor_tensor(hid[:, u % 2, :], gg[:, u % 2, :], bank[UP_BANK + u % 2][:, :], ALU.mult).then_inc(hid_ready.sem, 1)

            def finish_y(i, m):
                dve.wait_ge(summed.sem, summed.at1(i, (m + 1) * N // GROUP))
                dve.wait_ge(kept_ready.sem, kept_ready.at1(i, 1))
                v.tensor_tensor(yT[:, m, :], xd[:, m, :], bank[Y_BANK][:, :], ALU.add).then_inc(yT_ready.sem, 1)
                if m == 1:
                    dve.wait_ge(yT_ready.sem, yT_ready.at1(i, 2))
                    dve.wait_ge(yz_ready.sem, yz_ready.at1(i, 1))
                    v.tensor_tensor(yT[:, 1, :], yT[:, 1, :], szm[:, 1, :], ALU.mult).then_inc(yz_ready.sem, 1)

            def slot1(i, u, head=None, j=None, late=None):
                at = in1(i)
                if u == 0:
                    low1(i)
                    if late is first_late:
                        split_low(2 * E - 1)
                if late:
                    late(u)
                if u >= 2:
                    finish_hidden(i, u - 2)
                if u == 0:
                    form_delta(i, at, 0, 0, J1)
                    for c in now(CHUNKS1, u):
                        form_drive(at, c, 0, J1)
                for c in now(CHUNKS1, u - 1):
                    scan(at, c)
                if u > 0:
                    for c in now(CHUNKS1, u):
                        form_drive(at, c, c // N, J1)
                finish_gate(i, u)
                if u == CHUNKS1[N - 1] + SUM_LAG1:
                    finish_y(i, 0)
                if head:
                    for name in now(HEAD1, u):
                        head(name, j)

            def late1(i, u):
                if u < 2:
                    finish_hidden(i, UNITS - 2 + u)
                if u == 2:
                    finish_y(i, 1)
                if u == 4:
                    dve.wait_ge(tg_ready.sem, tg_ready.at1(i, 1))
                    v.scalar_tensor_tensor(out=g[:, :, :], in0=tg[:, :, :], scalar=1.0, in1=tiles(bank[HEAD_BANK][:, :]),
                                           op0=ALU.add, op1=ALU.mult).then_inc(g_ready.sem, 1)
                if u == 5:
                    dve.wait_ge(g_ready.sem, g_ready.at1(i, 1))
                    dve.wait_ge(s_ps.sem, s_ps.at1(i, 1))
                    dve.wait_ge(x_out.sem, x_out.at1(i, 0))
                    v.tensor_tensor(so[:, :, :], g[:, :, :], tiles(bank[Y_BANK][:, :]), ALU.mult).then_inc(gated.sem, 1)

            first_late = lambda u: late0(PAIRS - 1, u)

            v.memset(half[:, :], -0.5).then_inc(setup_dve.sem, 1)
            v.memset(ones[:, :], 1.0).then_inc(setup_dve.sem, 1)
            v.memset(xpad[:, :, :, 0:KC - 1].rearrange("p j b l -> p (j b) l"), 0.0).then_inc(setup_dve.sem, 1)
            for k in range(RING):
                v.memset(by_batch(decay[:, k, :])[:, :, 0:1], 0.0).then_inc(setup_dve.sem, 1)
            for name in FIRST:
                if name == "xnT":
                    dve.wait_ge(setup_act.sem, setup_act.at0(0, 1))
                    v.tensor_scalar(negA0[:, :], negA0[:, :], -1.0, None, ALU.mult).then_inc(setup_dve.sem, 1)
                    v.tensor_scalar(negA1[:, :], negA1[:, :], -1.0, None, ALU.mult).then_inc(setup_dve.sem, 1)
                    v.tensor_scalar(vec0[:, 0:KC + 1], vec0[:, 0:KC + 1], 0.5, None, ALU.mult).then_inc(setup_dve.sem, 1)
                    v.tensor_scalar(vec1[:, 0:J1 * (KC + 1)], vec1[:, 0:J1 * (KC + 1)], 0.5, None, ALU.mult).then_inc(setup_dve.sem, 1)
                    dve.wait_ge(setup_dve.sem, setup_dve.at0(0, SETUP_DVE))
                if name == "lmax":
                    dve.wait_ge(br_in.sem, br_in.at0(0, 16))
                head0(name, 0)
                if name in SPLIT_AFTER:
                    split_low(SPLIT_AFTER.index(name))
            for u in range(LATE + BEHIND):
                if u < LATE:
                    slot0(0, u, chunks=False)
                for name in now(BETWEEN, u):
                    head0(name, 0)
                if u >= BEHIND:
                    slot0(0, u - BEHIND, units=False)
                if u in SPLIT_SLOTS:
                    split_low(len(SPLIT_AFTER) + SPLIT_SLOTS.index(u))
            with dve.Fori(0, PAIRS - 1) as i:
                step.turn(i, DVE0)
                for u in range(LATE, UNITS):
                    slot0(i, u, head0, i + 1)
                for u in range(LATE):
                    slot0(i + 1, u, late=lambda u: late0(i, u))
            step.turned(PAIRS - 1)
            for u in range(LATE, UNITS):
                slot0(PAIRS - 1, u, head1, 0)
            for u in range(LATE):
                slot1(0, u, late=first_late)
            with dve.Fori(0, PAIRS - 1) as i:
                step.turn(i, DVE1)
                for u in range(LATE, UNITS):
                    slot1(i, u, head1, i + 1)
                for u in range(LATE):
                    slot1(i + 1, u, late=lambda u: late1(i, u))
            step.turned(PAIRS - 1)
            for u in range(LATE, UNITS):
                slot1(PAIRS - 1, u)
            for u in range(LATE):
                late1(PAIRS - 1, u)

        @block.gpsimd
        def _(pool):
            p = nc.gpsimd
            step = Chain(pool, pool_step)
            for s in signals:
                pool.sem_inc(s.sem, s.start)
            wide = lambda col: col.to_broadcast((128, T))

            def root(var, out_, var_at, sig_var, done):
                pool.wait_ge(sig_var.sem, var_at)
                p.tensor_tensor(out_[:, :], var[:, :], half[:, :], ALU.pow).then_inc(done.sem, 1)

            def log_less(m, at_c):
                pool.wait_ge(sp_c_ready.sem, at_c)
                p.tensor_tensor(sp_x[:, m, :], sp_x[:, m, :], sp_e[:, m, :], ALU.subtract).then_inc(sp_x_ready.sem, 1)

            def head0(name, j):
                if name in ("var1", "var2"):
                    root(veps, rstd, var_ready.at0(j, int(name[3])), var_ready, rstd_ready)
                if name == "less":
                    log_less(0, sp_c_ready.at0(j, 1))

            def head1(name, j):
                if name == "var1":
                    root(veps, rstd, var_ready.at1(j, 1), var_ready, rstd_ready)
                if name in ("less0", "less1"):
                    m = int(name[4])
                    log_less(m, sp_c_ready.at1(j, m + 1))

            def multiply(at, c, per_chunk):
                pool.wait_ge(state_ready.sem, at(state_ready, c + 1))
                pool.wait_ge(cb_in[c % ROWS].sem, at(cb_in[c % ROWS], per_chunk * (c // ROWS + 1)))
                q = c // GROUP
                cs = CB[:, c % ROWS, 0, :]
                if c % GROUP == 0:
                    pool.wait_ge(summed.sem, at(summed, max(q - 1, 0)))
                    ins = p.tensor_tensor(product[:, q % 2, :], state[:, c % RING, :], cs, ALU.mult)
                else:
                    pool.wait_ge(group_ready.sem, at(group_ready, q))
                    ins = p.tensor_tensor(addend[:, :], state[:, c % RING, :], cs, ALU.mult)
                ins.then_inc(state_used.sem, 1)
                if c % GROUP:
                    pool.wait_ge(state_used.sem, at(state_used, c + 1))
                    ins = p.tensor_tensor(product[:, q % 2, :], product[:, q % 2, :], addend[:, :], ALU.add)
                    if c % GROUP == GROUP - 1:
                        ins.then_inc(group_ready.sem, 1)
                    else:
                        step(ins)

            def slot0(i, u, head=None, j=None, late=None, units=True, chunks=True):
                if chunks:
                    for c in now(CHUNKS0, u - 1):
                        multiply(in0(i), c, 16)
                if late:
                    late(u)
                if "yn2" in now(TAIL0, u):
                    root(veps_t, rstd_t, tvar_ready.at0(i, 1), tvar_ready, trstd_ready)
                if head:
                    for name in now(HEAD0 if head is head0 else HEAD1, u):
                        head(name, j)

            def add_residual(i, at):
                pool.wait_ge(gated.sem, at(gated, 1))
                pool.wait_ge(r_in.sem, at(r_in, 16))
                p.tensor_tensor(so[:, :, :], so[:, :, :], xr[:, :, :], ALU.add).then_inc(out_ready.sem, 1)

            def late0(i, u):
                if u == 5:
                    add_residual(i, in0(i))

            def weigh_tokens(i, e):
                if e == 0:
                    pool.wait_ge(xr_ready.sem, xr_ready.at1(i, 1))
                pool.wait_ge(cw_in[e % CWR].sem, cw_in[e % CWR].at1(i, 16 * (e // CWR + 1)))
                pool.wait_ge(up_ps.sem, up_ps.at1(i, FT * (e - 1)))
                p.tensor_tensor(xw[:, e % 2, :], XR[:, :], cwb[:, e % CWR, :], ALU.mult).then_inc(xw_ready.sem, 1)

            def slot1(i, u, head=None, j=None, late=None):
                if u == 0 and late is first_late:
                    pool.wait_ge(wl_ready.sem, wl_ready.at0(0, 2 * E))
                    weigh_tokens(i, 0)
                if u == 0:
                    weigh_tokens(i, 1)
                for c in now(CHUNKS1, u - 1):
                    multiply(in1(i), c, 32)
                if u > 0 and late:
                    late(u)
                at = in1(i)
                if u == LATE + 2:
                    pool.wait_ge(sp_l_ready.sem, at(sp_l_ready, 1))
                    pool.wait_ge(sp_x_ready.sem, at(sp_x_ready, J1))
                    pool.wait_ge(decay_ready.sem, at(decay_ready, 0))
                    pool.wait_ge(delta_ready.sem, at(delta_ready, 1))
                    p.tensor_tensor(delta[:, 1, :], sp_x[:, 1, :], sp_l[:, 1, :], ALU.add).then_inc(delta_ready.sem, 1)
                if u == LATE + 3:
                    pool.wait_ge(dx_ready.sem, at(dx_ready, 1))
                    pool.wait_ge(delta_ready.sem, at(delta_ready, 2))
                    pool.wait_ge(drive_ready.sem, at(drive_ready, 0))
                    p.tensor_tensor(dx[:, 1, :], delta[:, 1, :], xs[:, 1, :], ALU.mult).then_inc(dx_ready.sem, 1)
                if u == CHUNKS1[N - 1] + SUM_LAG1 + 1:
                    pool.wait_ge(yT_ready.sem, yT_ready.at1(i, 1))
                    pool.wait_ge(kept_ready.sem, kept_ready.at1(i, 1))
                    p.tensor_tensor(yT[:, 0, :], yT[:, 0, :], szm[:, 0, :], ALU.mult).then_inc(yz_ready.sem, 1)
                if u % FT == 1 and 1 <= u // FT < E - 1:
                    weigh_tokens(i, u // FT + 1)
                if head:
                    if u == XW_SLOT:
                        weigh_tokens(j, 0)
                    for name in now(HEAD1, u):
                        head(name, j)

            def late1(i, u):
                if u == 5:
                    add_residual(i, in1(i))

            first_late = lambda u: late0(PAIRS - 1, u)

            for name in FIRST:
                head0(name, 0)
            for u in range(LATE + BEHIND):
                if u < LATE:
                    slot0(0, u, chunks=False)
                for name in now(BETWEEN, u):
                    head0(name, 0)
                if u >= BEHIND:
                    slot0(0, u - BEHIND, units=False)
            with pool.Fori(0, PAIRS - 1) as i:
                step.turn(i, POOL0)
                for u in range(LATE, UNITS):
                    slot0(i, u, head0, i + 1)
                for u in range(LATE):
                    slot0(i + 1, u, late=lambda u: late0(i, u))
            step.turned(PAIRS - 1)
            for u in range(LATE, UNITS):
                slot0(PAIRS - 1, u, head1, 0)
            for u in range(LATE):
                slot1(0, u, late=first_late)
            with pool.Fori(0, PAIRS - 1) as i:
                step.turn(i, POOL1)
                for u in range(LATE, UNITS):
                    slot1(i, u, head1, i + 1)
                for u in range(LATE):
                    slot1(i + 1, u, late=lambda u: late1(i, u))
            step.turned(PAIRS - 1)
            for u in range(LATE, UNITS):
                slot1(PAIRS - 1, u)
            for u in range(LATE):
                late1(PAIRS - 1, u)

        @block.scalar
        def _(act):
            a = nc.scalar
            step = Chain(act, act_step)
            hb = bank[HEAD_BANK]

            def split_high(k):
                e = k % E
                act.wait_ge(stage_in[e].sem, stage_in[e].at0(0, 16 * (k // E + 1)))
                a.activation(wh[:, e, :], wu[:, e, :] if k < E else stage[:, e % 2, :], ACT.Copy).then_inc(wh_ready.sem, 1)

            def first_tap(m, col, at_pad, at_delta):
                act.wait_ge(*at_pad)
                act.wait_ge(delta_ready.sem, at_delta)
                a.activation(by_batch(conv[:, m, :]), xpad[:, m, :, 0:L], ACT.Identity, bias=col("bconv", m),
                             scale=col("conv", KC * m)).then_inc(tap_ready.sem, 1)

            def softplus(m, bdt, at_x, at_delta, at_l):
                act.wait_ge(sp_x_ready.sem, at_x)
                act.wait_ge(delta_ready.sem, at_delta)
                step(a.activation(sp_e[:, m, :], hb[:, :], ACT.Abs, bias=bdt))
                a.activation(sp_x[:, m, :], hb[:, :], ACT.Relu, bias=bdt).then_inc(head_read.sem, 1)
                step(a.activation(sp_e[:, m, :], sp_e[:, m, :], ACT.Exp, scale=-1.0))
                act.wait_ge(sp_l_ready.sem, at_l)
                a.activation(sp_u[:, m, :], sp_e[:, m, :], ACT.Copy, bias=1.0).then_inc(sp_u_ready.sem, 1)

            def head0(name, j):
                if name == "xnT":
                    act.wait_ge(*use0(head_ps, j, "xnT"))
                    act.wait_ge(xr_ready.sem, xr_ready.at0(j, 0))
                    a.activation(XNT[:, :], hb[:, :], ACT.Copy).then_inc(head_read.sem, 1)
                if name == "xfT":
                    act.wait_ge(*use0(head_ps, j, "xfT"))
                    act.wait_ge(xl_ready.sem, xl_ready.at0(j, 0))
                    a.activation(XFT[:, :], hb[:, :], ACT.Identity, bias=col0("lnb"), scale=col0("lng")).then_inc(head_read.sem, 1)
                if name == "xin":
                    act.wait_ge(*use0(head_ps, j, "xin"))
                    a.activation(xpad[:, 0, :, KC - 1:], by_batch(hb[:, :]), ACT.Copy).then_inc(head_read.sem, 1)
                    first_tap(0, col0, use0(head_read, j, "xin"), delta_ready.at0(j, 0))
                if name == "lexp":
                    act.wait_ge(*use0(head_read, j, "logits"))
                    a.activation(lexp[:, 0:TT, :], lg[:, 0:TT, :], ACT.Exp).then_inc(lexp_ready.sem, 1)
                if name == "th":
                    act.wait_ge(conv_ready.sem, conv_ready.at0(j, 1))
                    act.wait_ge(sp_l_ready.sem, sp_l_ready.at0(j, 0))
                    a.activation(th[:, :], conv[:, 0, :], ACT.Tanh).then_inc(th_ready.sem, 1)
                if name == "dt":
                    act.wait_ge(*use0(head_ps, j, "dt"))
                    softplus(0, col0("bdt"), sp_x_ready.at0(j, 0), delta_ready.at0(j, 0), sp_l_ready.at0(j, 0))
                if name == "ln":
                    act.wait_ge(sp_u_ready.sem, sp_u_ready.at0(j, 1))
                    a.activation(sp_l[:, 0, :], sp_u[:, 0, :], ACT.Ln).then_inc(sp_l_ready.sem, 1)
                    a.activation(warm[:, :], ones[:, :], ACT.Exp)
                if name == "row":
                    act.wait_ge(*use0(head_ps, j, "row"))
                    act.wait_ge(rows_out.sem, rows_out.at0(j, 0))
                    a.activation(rows[:, 0, :], hb[0:96, :], ACT.Copy).then_inc(head_read.sem, 1)
                if name == "onehot":
                    act.wait_ge(*use0(head_ps, j, "onehot"))
                    a.activation(ohT[:, :], hb[0:E, :], ACT.Copy).then_inc(head_read.sem, 1)

            def head1(name, j):
                m = tile_of(name)
                if name == "xnT":
                    act.wait_ge(*use1(head_ps, j, "xnT"))
                    act.wait_ge(xr_ready.sem, xr_ready.at1(j, 0))
                    act.wait_ge(xl_ready.sem, xl_ready.at1(j, 0))
                    a.activation(XNT[:, :], hb[:, :], ACT.Copy).then_inc(head_read.sem, 1)
                if name in ("xi0", "xi1"):
                    act.wait_ge(*use1(head_ps, j, name))
                    a.activation(xpad[:, m, :, KC - 1:], by_batch(hb[:, :]), ACT.Copy).then_inc(head_read.sem, 1)
                    first_tap(m, col1, use1(head_read, j, name), delta_ready.at1(j, 0))
                if name == "xr":
                    act.wait_ge(yT_ready.sem, yT_ready.at1(j, -1))
                    act.wait_ge(xw_ready.sem, xw_ready.at1(j, 0))
                    a.activation(XR[:, :], XNT[:, :], ACT.Copy).then_inc(xr_ready.sem, 1)
                if name in ("th0", "th1"):
                    act.wait_ge(conv_ready.sem, conv_ready.at1(j, m + 1))
                    act.wait_ge(xs_ready.sem, xs_ready.at1(j, m))
                    act.wait_ge(sp_l_ready.sem, sp_l_ready.at1(j, 0))
                    a.activation(th[:, :], conv[:, m, :], ACT.Tanh).then_inc(th_ready.sem, 1)
                if name == "lexp":
                    act.wait_ge(*use1(head_read, j, "logits"))
                    a.activation(lexp[:, 0:TT, :], lg[:, 0:TT, :], ACT.Exp)
                    a.activation(lexp[:, TT:, :], lg[:, TT:, :], ACT.Exp, scale=1.0 / GATE_TEMP).then_inc(lexp_ready.sem, 1)
                if name in ("tz0", "tz1"):
                    act.wait_ge(*use1(head_ps, j, f"z{m}"))
                    act.wait_ge(kept_ready.sem, kept_ready.at1(j, 0))
                    a.activation(sz[:, m, :], hb[:, :], ACT.Tanh, scale=0.5).then_inc(tz_ready.sem, 1)
                if name == "cwT":
                    act.wait_ge(*use1(head_ps, j, "cwT"))
                    act.wait_ge(cw_out.sem, cw_out.at1(j, 0))
                    a.activation(cwT[:, :], hb[0:E, :], ACT.Copy).then_inc(head_read.sem, 1)
                if name in ("row0", "row1"):
                    act.wait_ge(*use1(head_ps, j, name))
                    act.wait_ge(rows_out.sem, rows_out.at1(j, 0))
                    a.activation(rows[:, m, :], hb[0:96, :], ACT.Copy).then_inc(head_read.sem, 1)
                if name == "ln":
                    act.wait_ge(sp_u_ready.sem, sp_u_ready.at1(j, J1))
                    a.activation(sp_l[:, :, :], sp_u[:, :, :], ACT.Ln).then_inc(sp_l_ready.sem, 1)
                    a.activation(warm[:, :], ones[:, :], ACT.Exp)
                if name in ("dt0", "dt1"):
                    act.wait_ge(*use1(head_ps, j, name))
                    softplus(m, col1("bdt", m), sp_x_ready.at1(j, 0), delta_ready.at1(j, 0), sp_l_ready.at1(j, 0))

            def hand_over0(i):
                act.wait_ge(*use0(head_read, i, "xfT"))
                act.wait_ge(hid_ps.sem, hid_ps.at0(i, 0))
                a.activation(XH[:, :], XFT[:, :], ACT.Copy).then_inc(xh_ready.sem, 1)
                act.wait_ge(yT_ready.sem, yT_ready.at0(i, 0))
                a.activation(XR[:, :], XNT[:, :], ACT.Copy).then_inc(xr_ready.sem, 1)

            def hand_over1(i):
                act.wait_ge(*use1(head_read, i, "xnT"))
                act.wait_ge(hid_ps.sem, hid_ps.at1(i, 0))
                a.activation(XH[:, :], XNT[:, :], ACT.Copy).then_inc(xh_ready.sem, 1)

            def keep(i):
                act.wait_ge(xs_ready.sem, xs_ready.at1(i, J1))
                act.wait_ge(s_ps.sem, s_ps.at1(i, 0))
                for m in range(J1):
                    a.activation(xd[:, m, :], xs[:, m, :], ACT.Identity, scale=col1("dskip", m))
                act.wait_ge(*use1(head_read, i, "z1"))
                act.wait_ge(yz_ready.sem, yz_ready.at1(i, 0))
                a.activation(szm[:, :, :], sz[:, :, :], ACT.Copy, scale=0.25).then_inc(kept_ready.sem, 1)

            def form_decay(at, c, m, negA):
                act.wait_ge(delta_ready.sem, at(delta_ready, m + 1))
                act.wait_ge(state_ready.sem, at(state_ready, max(c - RING + 1, 0)))
                a.activation(by_batch(decay[:, c % RING, :])[:, :, 1:], by_batch(delta[:, m, :])[:, :, 1:], ACT.Exp,
                             scale=negA[:, c:c + 1]).then_inc(decay_ready.sem, 1)

            def rectify(i, u):
                act.wait_ge(hid_ps.sem, hid_ps.at0(i, u + 1))
                act.wait_ge(down_done.sem, down_done.at0(i, u - 1))
                a.activation(hid[:, u % 2, :], bank[HID_BANK + u % HIDS][:, :], ACT.Relu, bias=col0("b1", u)).then_inc(hid_ready.sem, 1)

            def slot0(i, u, head=None, j=None, late=None, units=True, chunks=True):
                if u == 0 and units:
                    hand_over0(i)
                    if late:
                        late(u)
                if units:
                    rectify(i, u)
                if u == 0 and chunks:
                    for c in range(RING - 2):
                        form_decay(in0(i), c, 0, negA0)
                if chunks:
                    for c in now(CHUNKS0, u):
                        if c + RING - 2 < N:
                            form_decay(in0(i), c + RING - 2, 0, negA0)
                if u > 0 and late:
                    late(u)
                if head is head1 and u % FT == FT - 1 and u // FT >= 1:
                    split_high(E + u // FT - 1)
                if head:
                    for name in now(HEAD0 if head is head0 else HEAD1, u):
                        head(name, j)

            def late0(i, u):
                if u == 1:
                    act.wait_ge(mix_ps.sem, mix_ps.at0(i, 1))
                    a.activation(yfT[:, :], bank[OUT_BANK][:, :], ACT.Copy).then_inc(yfT_ready.sem, 1)
                if u == 3:
                    act.wait_ge(yf_ps.sem, yf_ps.at0(i, 1))
                    act.wait_ge(hp_ready.sem, hp_ready.at0(i, 1))
                    for k in range(TT):
                        last = a.activation(tg[:, k, :], bank[HEAD_BANK][:, 128 * k:128 * k + 128], ACT.Tanh, scale=hp[:, k:k + 1])
                    last.then_inc(tg_ready.sem, 1)

            def half_gate(i, u):
                act.wait_ge(hid_ps.sem, hid_ps.at1(i, u + 1))
                act.wait_ge(gg_ready.sem, gg_ready.at1(i, u - 1))
                a.activation(sg[:, u % 2, :], bank[HID_BANK + u % HIDS][:, :], ACT.Tanh, scale=0.5).then_inc(tanh_ready.sem, 1)

            def slot1(i, u, head=None, j=None, late=None):
                if u == 0:
                    hand_over1(i)
                    if late is first_late:
                        split_high(2 * E - 1)
                    if late:
                        late(u)
                half_gate(i, u)
                if u == 0:
                    for c in range(RING - 2):
                        form_decay(in1(i), c, 0, negA1)
                for c in now(CHUNKS1, u):
                    c += RING - 2
                    if c < C1:
                        form_decay(in1(i), c, c // N, negA1)
                if u > 0 and late:
                    late(u)
                if u == LATE:
                    keep(i)
                if head:
                    for name in now(HEAD1, u):
                        head(name, j)

            def late1(i, u):
                if u == 2:
                    act.wait_ge(down_done.sem, down_done.at1(i, UNITS))
                    a.activation(yfT[:, :], bank[OUT_BANK][:, :], ACT.Copy).then_inc(yfT_ready.sem, 1)
                if u == 3:
                    act.wait_ge(yf_ps.sem, yf_ps.at1(i, 1))
                    a.activation(tg[:, :, :], tiles(bank[HEAD_BANK][:, :]), ACT.Tanh, scale=0.5).then_inc(tg_ready.sem, 1)

            first_late = lambda u: late0(PAIRS - 1, u)

            act.wait_ge(early_in.sem, early_in.at0(0, 16))
            a.activation(negA0[:, :], vec0[:, V0["alog"]:V0["alog"] + N], ACT.Exp)
            a.activation(negA1[:, :], vec1[:, V1["alog"]:V1["alog"] + J1 * N], ACT.Exp).then_inc(setup_act.sem, 1)
            for name in FIRST:
                if name == "xin":
                    act.wait_ge(setup_dve.sem, setup_dve.at0(0, SETUP_DVE))
                head0(name, 0)
                if name in SPLIT_AFTER:
                    split_high(SPLIT_AFTER.index(name))
            for u in range(LATE + BEHIND):
                if u < LATE:
                    slot0(0, u, chunks=False)
                for name in now(BETWEEN, u):
                    head0(name, 0)
                if u >= BEHIND:
                    slot0(0, u - BEHIND, units=False)
                if u in SPLIT_SLOTS:
                    split_high(len(SPLIT_AFTER) + SPLIT_SLOTS.index(u))
            with act.Fori(0, PAIRS - 1) as i:
                step.turn(i, ACT0)
                for u in range(LATE, UNITS):
                    slot0(i, u, head0, i + 1)
                for u in range(LATE):
                    slot0(i + 1, u, late=lambda u: late0(i, u))
            step.turned(PAIRS - 1)
            for u in range(LATE, UNITS):
                slot0(PAIRS - 1, u, head1, 0)
            for u in range(LATE):
                slot1(0, u, late=first_late)
            with act.Fori(0, PAIRS - 1) as i:
                step.turn(i, ACT1)
                for u in range(LATE, UNITS):
                    slot1(i, u, head1, i + 1)
                for u in range(LATE):
                    slot1(i + 1, u, late=lambda u: late1(i, u))
            step.turned(PAIRS - 1)
            for u in range(LATE, UNITS):
                slot1(PAIRS - 1, u)
            for u in range(LATE):
                late1(PAIRS - 1, u)

        @block.tensor
        def _(pe):
            t = nc.tensor
            hb = bank[HEAD_BANK]

            def transposes(dst, src, done):
                for k in range(TT):
                    last = t.transpose(dst[:, 128 * k:128 * k + 128], src(k), ident[:, :])
                last.then_inc(done.sem, 1)

            def head_product(rows, weights, rhs):
                t.matmul(hb[0:rows, :], weights, rhs, start=True, stop=True).then_inc(head_ps.sem, 1)

            def head0(name, j):
                if name not in BANK0:
                    return
                pe.wait_ge(head_read.sem, head_read.at0(j, BANK0.index(name)))
                if name == "xnT":
                    pe.wait_ge(g_ready.sem, g_ready.at0(j, -1))
                    pe.wait_ge(xn_ready.sem, xn_ready.at0(j, 1))
                    transposes(hb, lambda k: xn[:, k, :], head_ps)
                if name == "xfT":
                    pe.wait_ge(xf_ready.sem, xf_ready.at0(j, 1))
                    transposes(hb, lambda k: xf[:, k, :], head_ps)
                if name == "xin":
                    head_product(128, w_in0[:, 0:D], XNT[:, :])
                if name == "logits":
                    for k in range(TT):
                        last = t.matmul(hb[:, E * k:E * k + E], XNT[:, 128 * k:128 * k + 128], w_r0[:, :], start=True, stop=True)
                    last.then_inc(head_ps.sem, 1)
                if name == "z":
                    head_product(128, w_in0[:, D:2 * D], XNT[:, :])
                if name == "onehot":
                    pe.wait_ge(choice_ready.sem, choice_ready.at0(j, 1))
                    for k in range(TT):
                        last = t.transpose(hb[0:E, 128 * k:128 * k + 128], onehot[:, k, :], ident[:, :])
                    last.then_inc(head_ps.sem, 1)
                if name == "dt":
                    head_product(128, w_dt0[:, :], xs[:, 1, :])
                if name == "row":
                    head_product(96, w_row0[:, :], xs[:, 1, :])

            def head1(name, j):
                if name not in BANK1:
                    return
                pe.wait_ge(head_read.sem, head_read.at1(j, BANK1.index(name)))
                if name == "xnT":
                    pe.wait_ge(g_ready.sem, g_ready.at1(j, -1))
                    pe.wait_ge(xn_ready.sem, xn_ready.at1(j, 1))
                    transposes(hb, lambda k: xn[:, k, :], head_ps)
                if name in ("xi0", "xi1", "z0", "z1"):
                    m = J1 * "xz".index(name[0]) + int(name[-1])
                    head_product(128, w_in1[:, 128 * m:128 * m + 128], XNT[:, :])
                if name == "logits":
                    for k in range(2 * TT):
                        kind, tile = k // TT, k % TT
                        last = t.matmul(hb[:, E * k:E * k + E], XNT[:, 128 * tile:128 * tile + 128],
                                        w_r1[:, E * kind:E * kind + E], start=True, stop=True)
                    last.then_inc(head_ps.sem, 1)
                if name == "cwT":
                    pe.wait_ge(choice_ready.sem, choice_ready.at1(j, 1))
                    for k in range(TT):
                        last = t.transpose(hb[0:E, 128 * k:128 * k + 128], cw[:, k, :], ident[:, :])
                    last.then_inc(head_ps.sem, 1)
                m = int(name[-1]) if name[-1] in "01" else 0
                if name in ("row0", "row1"):
                    pe.wait_ge(xs_ready.sem, xs_ready.at1(j, m + 1))
                    head_product(96, w_row1[:, 96 * m:96 * m + 96], xs[:, m, :])
                if name in ("dt0", "dt1"):
                    head_product(128, w_dt1[32:64, 128 * m:128 * m + 128], rows[32:64, m, :])

            def three_passes(dst, e, f, stop):
                ws = slice(128 * f, 128 * f + 128)
                t.matmul(dst, wh[:, e, ws], XH[:, :], start=True, stop=False)
                t.matmul(dst, wh[:, e, ws], XL[:, :], start=False, stop=False)
                return t.matmul(dst, wl[:, e, ws], XH[:, :], start=False, stop=stop)

            def sum_group(at, q):
                if q == 0:
                    pe.wait_ge(s_read.sem, at(s_read, 0))
                    pe.wait_ge(gated.sem, at(gated, 0))
                if q == N // GROUP:
                    pe.wait_ge(yT_ready.sem, at(yT_ready, 1))
                pe.wait_ge(group_ready.sem, at(group_ready, q + 1))
                k = q % (N // GROUP)
                t.matmul(bank[Y_BANK][:, :], ident[:, :], product[:, q % 2, :], start=(k == 0), stop=(k == N // GROUP - 1)).then_inc(summed.sem, 1)

            def bank_free(u):
                if u >= HIDS:
                    return u - HIDS + 1
                return max(k for k in range(-HIDS, 0) if (UNITS + k) % HIDS == u) + 1

            def hidden0(i, u):
                e, f = u // FT, u % FT
                dst = bank[HID_BANK + u % HIDS][:, :]
                if u == 0:
                    pe.wait_ge(xl_ready.sem, xl_ready.at0(i, 1))
                if f == 0:
                    pe.wait_ge(wl_ready.sem, wl_ready.at0(0, e + 1))
                pe.wait_ge(hid_ready.sem, hid_ready.at0(i, bank_free(u)))
                three_passes(dst, e, f, False)
                if u == 0:
                    pe.wait_ge(ohm_ready.sem, ohm_ready.at0(i, 1))
                t.matmul(dst, big[:, e:e + 1].to_broadcast((E, 128)), ohm[:, :], start=False, stop=True).then_inc(hid_ps.sem, 1)

            def gate1(i, u):
                e, f = u // FT, u % FT
                if u == 0:
                    pe.wait_ge(xl_ready.sem, xl_ready.at1(i, 1))
                if f == 0:
                    pe.wait_ge(wl_ready.sem, wl_ready.at0(0, E + e + 1))
                pe.wait_ge(gg_ready.sem, gg_ready.at1(i, bank_free(u)))
                three_passes(bank[HID_BANK + u % HIDS][:, :], e, f, True).then_inc(hid_ps.sem, 1)

            def down0(i, u):
                if u == 0:
                    pe.wait_ge(yfT_ready.sem, yfT_ready.at0(i, 0))
                if u % FT == 0:
                    pe.wait_ge(wd_in[u // FT].sem, wd_in[u // FT].at0(0, 16))
                pe.wait_ge(hid_ready.sem, hid_ready.at0(i, u + 1))
                t.matmul(bank[OUT_BANK][:, :], wd[:, u, :], hid[:, u % 2, :], start=(u == 0), stop=False).then_inc(down_done.sem, 1)

            def slot0(i, u, head=None, j=None, late=None, units=True, chunks=True):
                at = in0(i)
                if u == 0 and late:
                    late(u)
                hidden0(i, u)
                if u > 0 and late:
                    late(u)
                if u >= LAG0:
                    down0(i, u - LAG0)
                for q in sums(CHUNKS0, SUM_LAG0, u):
                    sum_group(at, q)
                for name in now(TAIL0, u):
                    if name == "y":
                        pe.wait_ge(yT_ready.sem, yT_ready.at0(i, 1))
                        transposes(bank[Y_BANK], lambda k: yT[:, 0, 128 * k:128 * k + 128], y_ps)
                    if name == "yn":
                        pe.wait_ge(yn_ready.sem, yn_ready.at0(i, 1))
                        transposes(bank[UP_BANK], lambda k: yn[:, k, :], ynT_ps)
                    if name == "s":
                        pe.wait_ge(ynT_ready.sem, ynT_ready.at0(i, 1))
                        for k in range(TT):
                            last = t.matmul(bank[Y_BANK][:, 128 * k:128 * k + 128], ynT[:, 128 * k:128 * k + 128], w_out0[:, :],
                                            start=True, stop=True)
                        last.then_inc(s_ps.sem, 1)
                if head:
                    for name in now(HEAD0 if head is head0 else HEAD1, u):
                        head(name, j)

            def transpose_mixture(at, last_read):
                pe.wait_ge(yfT_ready.sem, at(yfT_ready, 1))
                pe.wait_ge(head_read.sem, last_read)
                transposes(hb, lambda k: yfT[:, 128 * k:128 * k + 128], yf_ps)

            def late0(i, u):
                if u < LAG0:
                    down0(i, UNITS - LAG0 + u)
                if u == LAG0 - 1:
                    pe.wait_ge(ohF_ready.sem, ohF_ready.at0(i, 1))
                    t.matmul(bank[OUT_BANK][:, :], b2[:, :], ohF[:, :], start=False, stop=True).then_inc(mix_ps.sem, 1)
                if u == 3:
                    transpose_mixture(in0(i), head_read.at0(PAIRS, 0) + len(BANK1) if i is PAIRS - 1 else head_read.at0(i + 2, 0))

            def up1(i, u):
                e, f = u // FT, u % FT
                if f == 0:
                    pe.wait_ge(xw_ready.sem, xw_ready.at1(i, e + 1))
                if u == 0:
                    pe.wait_ge(wu_in.sem, wu_in.at0(0, 16 * E))
                pe.wait_ge(hid_ready.sem, hid_ready.at1(i, u - 1))
                t.matmul(bank[UP_BANK + u % 2][:, :], wu[:, e, 128 * f:128 * f + 128], xw[:, e % 2, :], start=True, stop=True).then_inc(up_ps.sem, 1)

            def down1(i, u):
                if u == 0:
                    pe.wait_ge(yfT_ready.sem, yfT_ready.at1(i, 0))
                if u % FT == 0:
                    pe.wait_ge(wd_in[u // FT].sem, wd_in[u // FT].at0(0, 32))
                pe.wait_ge(hid_ready.sem, hid_ready.at1(i, u + 1))
                ins = t.matmul(bank[OUT_BANK][:, :], wd[:, u, :], hid[:, u % 2, :], start=(u == 0), stop=(u == UNITS - 1))
                ins.then_inc(down_done.sem, 1)

            def slot1(i, u, head=None, j=None, late=None):
                at = in1(i)
                if u == 0 and late:
                    late(u)
                gate1(i, u)
                if u > 0:
                    up1(i, u - 1)
                if u > 0 and late:
                    late(u)
                if u >= LAG1:
                    down1(i, u - LAG1)
                for q in sums(CHUNKS1, SUM_LAG1, u):
                    sum_group(at, q)
                if head:
                    for name in now(HEAD1, u):
                        head(name, j)

            def late1(i, u):
                if u == 0:
                    up1(i, UNITS - 1)
                if u < LAG1:
                    down1(i, UNITS - LAG1 + u)
                for q in sums(CHUNKS1, SUM_LAG1, UNITS + u):
                    sum_group(in1(i), q)
                if u == 3:
                    transpose_mixture(in1(i), head_read.at1(PAIRS, 0) if i is PAIRS - 1 else head_read.at1(i + 2, 0))
                if u == 3:
                    pe.wait_ge(yz_ready.sem, yz_ready.at1(i, J1))
                    for k in range(TT):
                        for m in range(J1):
                            last = t.matmul(bank[Y_BANK][:, 128 * k:128 * k + 128], yT[:, m, 128 * k:128 * k + 128], w_out1[:, m, :],
                                            start=(m == 0), stop=(m == J1 - 1))
                    last.then_inc(s_ps.sem, 1)

            pe.wait_ge(early_in.sem, early_in.at0(0, 16))
            for name in FIRST:
                head0(name, 0)
            pe.wait_ge(late_in.sem, late_in.at0(0, 16 * 5))
            for u in range(LATE):
                slot0(0, u, chunks=False)
                for name in now(BETWEEN, u):
                    head0(name, 0)
            with pe.Fori(0, PAIRS - 1) as i:
                for u in range(LATE, UNITS):
                    slot0(i, u, head0, i + 1)
                for u in range(LATE):
                    slot0(i + 1, u, late=lambda u: late0(i, u))
            for u in range(LATE, UNITS):
                slot0(PAIRS - 1, u, head1, 0)
            for u in range(LATE):
                slot1(0, u, late=lambda u: late0(PAIRS - 1, u))
            with pe.Fori(0, PAIRS - 1) as i:
                for u in range(LATE, UNITS):
                    slot1(i, u, head1, i + 1)
                for u in range(LATE):
                    slot1(i + 1, u, late=lambda u: late1(i, u))
            for u in range(LATE, UNITS):
                slot1(PAIRS - 1, u)
            for u in range(LATE):
                late1(PAIRS - 1, u)


CONSTS = {
    "early": ((128, sum(EARLY.values())), F32), "later": ((128, sum(LATER.values())), F32),
    "br0": ((1, E), F32), "big": ((E, E), BF16), "b2": ((E, D), F32), "b_out0": ((1, D), F32), "w_dt1": ((64, J1 * 128), F32),
    "W1": ((E, D, FT * 128), F32), "W2": ((E, FT * 128, D), F32),
    "Wg": ((E, D, FT * 128), F32), "Wu": ((E, D, FT * 128), F32), "Wd": ((E, FT * 128, D), F32),
}


def program(nc, x, out, w):
    x1 = nc.dram_tensor("x1", (B * L, D), F32, kind="Internal").ap()
    crow = nc.dram_tensor("crow", (2, J1, 2, 2 * N, T), F32, kind="Internal").ap()
    cwrow = nc.dram_tensor("cwrow", (2, E, T), F32, kind="Internal").ap()
    build(nc, x, out, x1, crow, cwrow, w)


def kernel(**inputs):
    import numpy as np
    import ml_dtypes
    import concourse.bacc as bacc
    from concourse.bass_utils import run_bass_kernel_spmd

    a = {k: np.asarray(v) for k, v in inputs.items()}
    col = lambda v: v.reshape(1, -1).T if v.ndim == 1 else v
    c = {}
    c["ident"] = np.eye(128, dtype=np.float32)
    c["vec0"] = np.concatenate([a["L0_attn_W_conv"][:, 0, :], col(a["L0_attn_b_conv"]), col(a["L0_attn_b_dt"]),
                                a["L0_attn_A_log"], col(a["L0_attn_ln_gamma"]), col(a["L0_attn_ln_beta"]),
                                col(a["L0_ffn_ln_g"]), col(a["L0_ffn_ln_b"]), a["L0_ffn_b1"].reshape(UNITS, 128).T], axis=1)
    c["w_in0"] = a["L0_attn_W_in"].T
    c["w_r0"] = a["L0_ffn_Wr"]
    c["br0"] = a["L0_ffn_br"].reshape(1, E)
    c["iota"] = np.tile(np.arange(E, dtype=np.float32), (128, TT))
    c["w_dt0"] = a["L0_attn_W_dt"].T
    w_row = np.zeros((128, 96), np.float32)
    w_row[:, 0:N], w_row[:, 64:64 + N] = a["L0_attn_W_xproj"][N:].T, a["L0_attn_W_xproj"][:N].T
    c["w_row0"] = w_row
    c["big"] = (BIG * np.eye(E)).astype(ml_dtypes.bfloat16)
    c["w_out0"] = a["L0_attn_W_out"].T
    c["b2"] = a["L0_ffn_b2"]
    c["b_out0"] = a["L0_attn_b_out"].reshape(1, D)
    c["W1"], c["W2"] = a["L0_ffn_W1"], a["L0_ffn_W2"]

    per_tile = lambda v: v.reshape(J1, 128, -1).transpose(1, 0, 2).reshape(128, -1)
    c["vec1"] = np.concatenate([per_tile(v) for v in (
        a["L1_attn_conv_w"][:, 0, :], a["L1_attn_conv_b"], a["L1_attn_dt_proj_b"], a["L1_attn_A_log"], a["L1_attn_Dskip"])], axis=1)
    c["w_in1"] = a["L1_attn_in_proj_w"].T
    c["w_r1"] = np.concatenate([a["L1_ffn_w_router"], a["L1_ffn_w_gating"]], axis=1)
    xp = a["L1_attn_x_proj_w"].reshape(2 * J1, 3 * N, 64)
    dp = a["L1_attn_dt_proj_w"].reshape(2 * J1, 64, N)
    w_row, w_dt = np.zeros((128, J1, 96), np.float32), np.zeros((64, J1, 128), np.float32)
    for h in range(2):
        ch = slice(64 * h, 64 * h + 64)
        for j in range(J1):
            for at, kind in ((0, 2), (32, 0), (64, 1)):
                w_row[ch, j, at + N * h:at + N * h + N] = xp[2 * j + h, N * kind:N * kind + N].T
            w_dt[32 + N * h:32 + N * h + N, j, ch] = dp[2 * j + h].T
    c["w_row1"], c["w_dt1"] = w_row.reshape(128, -1), w_dt.reshape(64, -1)
    c["w_out1"] = per_tile(a["L1_attn_out_proj_w"].T)
    c["Wg"], c["Wu"], c["Wd"] = a["L1_ffn_w_gate"], a["L1_ffn_w_up"], a["L1_ffn_w_down"]

    c["early"] = np.concatenate([c[n] for n in EARLY], axis=1)
    c["later"] = np.concatenate([c[n] for n in LATER], axis=1)

    nc = bacc.Bacc("TRN2", target_bir_lowering=False, num_devices=1)
    arrays = {"x_dram": np.ascontiguousarray(a["L0_attn_x"].reshape(B * L, D))}
    x = nc.dram_tensor("x_dram", (B * L, D), F32, kind="ExternalInput").ap()
    w = {}
    for name, (shape, dt) in CONSTS.items():
        arrays[name + "_dram"] = np.ascontiguousarray(c[name])
        assert arrays[name + "_dram"].shape == shape, name
        w[name] = nc.dram_tensor(name + "_dram", shape, dt, kind="ExternalInput").ap()
    out = nc.dram_tensor("out_dram", (B * L, D), F32, kind="ExternalOutput").ap()
    program(nc, x, out, w)
    r = run_bass_kernel_spmd(nc, [arrays], core_ids=[0])
    return r.results[0]["out_dram"].reshape(B, L, D)
```
